# Optimizing a Trainium2 kernel written in Bass

```python
import numpy as np
import jax
import jax.numpy as jnp

def _softmax(x, axis=-1):
    return jax.nn.softmax(x, axis=axis)

def _gelu(x):
    return jax.nn.gelu(x, approximate=True)

def _silu(x):
    return jax.nn.silu(x)

def _sigmoid(x):
    return jax.nn.sigmoid(x)

def _layernorm(x, axis=-1, eps=1e-05):
    m = jnp.mean(x, axis=axis, keepdims=True)
    v = jnp.var(x, axis=axis, keepdims=True)
    return (x - m) / jnp.sqrt(v + eps)

def _scatter_add(tgt, idx, src, axis=0):
    return tgt.at[idx].add(src)

def _segment_sum(src, seg, n):
    return jax.ops.segment_sum(src, seg, n)
kernel_name = 'mk_xattn_ffn_d1_seqx_r4_da0f9e'

def setup_inputs(seed: int=0):
    np.random.seed(seed)
    _w = jnp.asarray

    def _rec_inputs():
        import jax
        import jax.numpy as jnp
        _rk = jax.random.key(seed)
        x = 7.22e-05 + 1 * jax.random.normal(jax.random.fold_in(_rk, 1), (2, 1024, 256), jnp.float32)
        _lenS = 1024 - jax.random.randint(jax.random.fold_in(_rk, 7), (2,), 0, max(1, 1024 // 4) + 1, jnp.int32)
        _lenS2 = 77 - jax.random.randint(jax.random.fold_in(_rk, 8), (2,), 0, max(1, 77 // 4) + 1, jnp.int32)
        _ctx_1024P = jax.random.normal(jax.random.fold_in(_rk, 11), (2, 16, 256), jnp.float32)
        _ctx_1024c = jax.random.dirichlet(jax.random.fold_in(_rk, 511), 0.3 * jnp.ones((16,), jnp.float32), (2, 77))
        _ctx_1024t = jnp.einsum('bsk,bkd->bsd', _ctx_1024c, _ctx_1024P)
        _ctx_1024t = _ctx_1024t * jax.lax.rsqrt(jnp.mean(jnp.square(_ctx_1024t)) + 1e-12) * 0.953939
        ctx_1024 = 4.13588e-05 + 0.999923 * (_ctx_1024t + 0.3 * jax.random.normal(jax.random.fold_in(_rk, 611), (2, 77, 256), jnp.float32))
        _validS = jnp.arange(1024)[None, :] < _lenS[:, None]
        _validS2 = jnp.arange(77)[None, :] < _lenS2[:, None]
        _causal = jnp.tril(jnp.ones((1024, 1024), dtype=bool))
        mask_BxSxS2_ik0 = jnp.where(jnp.broadcast_to(_validS2[:, None, :], (2, 1024, 77)), 0, 1).astype(jnp.int32)
        return (x, ctx_1024, mask_BxSxS2_ik0)
    x, ctx_1024, mask_BxSxS2_ik0 = _rec_inputs()

    def _L0_xattn_setup():
        import jax, jax.numpy as jnp
        import numpy as np
        D_MODEL = 256
        H = 16
        D_K = D_MODEL // H
        B, S = (4, 512)
        NEG = -1000000000.0
        key = jax.random.key(seed)
        ks = jax.random.split(key, 12)
        scale = 1.0 / np.sqrt(D_MODEL)
        inp = {'query': jax.random.normal(ks[0], (B, S, D_MODEL), jnp.float32), 'key': jax.random.normal(ks[1], (B, S, D_MODEL), jnp.float32), 'value': jax.random.normal(ks[2], (B, S, D_MODEL), jnp.float32), 'mask': jnp.broadcast_to(jnp.tril(jnp.ones((S, S), jnp.int32)), (B, S, S)), 'Wq': jax.random.normal(ks[3], (D_MODEL, D_MODEL), jnp.float32) * scale, 'bq': jnp.zeros((D_MODEL,), jnp.float32), 'Wk': jax.random.normal(ks[4], (D_MODEL, D_MODEL), jnp.float32) * scale, 'bk': jnp.zeros((D_MODEL,), jnp.float32), 'Wv': jax.random.normal(ks[5], (D_MODEL, D_MODEL), jnp.float32) * scale, 'bv': jnp.zeros((D_MODEL,), jnp.float32), 'Wo': jax.random.normal(ks[6], (D_MODEL, D_MODEL), jnp.float32) * scale, 'bo': jnp.zeros((D_MODEL,), jnp.float32)}
        return inp
    _L0_xattn_all = _L0_xattn_setup()
    _L0_xattn_in = {k: v for k, v in _L0_xattn_all.items() if k in ('Wq', 'bq', 'Wk', 'bk', 'Wv', 'bv', 'Wo', 'bo')}
    del _L0_xattn_all

    def _L0_ffn_setup():
        import jax, jax.numpy as jnp
        import numpy as np
        HIDDEN = 256
        INTER = 1024
        NUM_EXPERTS = 8
        TOP_K = 2
        EPS = 1e-05

        def _layer_norm(x, g, b):
            m = jnp.mean(x, axis=-1, keepdims=True)
            v = jnp.mean(jnp.square(x - m), axis=-1, keepdims=True)
            return (x - m) * jax.lax.rsqrt(v + EPS) * g + b
        key = jax.random.key(seed)
        ks = jax.random.split(key, 8)
        s = 0.02
        return {'x': jax.random.normal(ks[0], (4, 512, HIDDEN), dtype=jnp.float32), 'ln1_g': jnp.ones((HIDDEN,), jnp.float32), 'ln1_b': jnp.zeros((HIDDEN,), jnp.float32), 'attn_w': jax.random.normal(ks[1], (HIDDEN, HIDDEN), jnp.float32) * s, 'ln2_g': jnp.ones((HIDDEN,), jnp.float32), 'ln2_b': jnp.zeros((HIDDEN,), jnp.float32), 'gate_w': jax.random.normal(ks[2], (NUM_EXPERTS, HIDDEN), jnp.float32) * s, 'gate_proj': jax.random.normal(ks[3], (NUM_EXPERTS, INTER, HIDDEN), jnp.float32) * s, 'up_proj': jax.random.normal(ks[4], (NUM_EXPERTS, INTER, HIDDEN), jnp.float32) * s, 'down_proj': jax.random.normal(ks[5], (NUM_EXPERTS, HIDDEN, INTER), jnp.float32) * s}
    _L0_ffn_all = _L0_ffn_setup()
    _L0_ffn_in = {k: v for k, v in _L0_ffn_all.items() if k in ('ln1_g', 'ln1_b', 'attn_w', 'ln2_g', 'ln2_b', 'gate_w', 'gate_proj', 'up_proj', 'down_proj')}
    del _L0_ffn_all
    return {'x': x, 'ctx_1024': ctx_1024, 'mask_BxSxS2_ik0': mask_BxSxS2_ik0, 'L0_xattn_Wq': _L0_xattn_in['Wq'], 'L0_xattn_bq': _L0_xattn_in['bq'], 'L0_xattn_Wk': _L0_xattn_in['Wk'], 'L0_xattn_bk': _L0_xattn_in['bk'], 'L0_xattn_Wv': _L0_xattn_in['Wv'], 'L0_xattn_bv': _L0_xattn_in['bv'], 'L0_xattn_Wo': _L0_xattn_in['Wo'], 'L0_xattn_bo': _L0_xattn_in['bo'], 'L0_ffn_ln1_g': _L0_ffn_in['ln1_g'], 'L0_ffn_ln1_b': _L0_ffn_in['ln1_b'], 'L0_ffn_attn_w': _L0_ffn_in['attn_w'], 'L0_ffn_ln2_g': _L0_ffn_in['ln2_g'], 'L0_ffn_ln2_b': _L0_ffn_in['ln2_b'], 'L0_ffn_gate_w': _L0_ffn_in['gate_w'], 'L0_ffn_gate_proj': _L0_ffn_in['gate_proj'], 'L0_ffn_up_proj': _L0_ffn_in['up_proj'], 'L0_ffn_down_proj': _L0_ffn_in['down_proj']}

def reference(x, ctx_1024, mask_BxSxS2_ik0, L0_xattn_Wq, L0_xattn_bq, L0_xattn_Wk, L0_xattn_bk, L0_xattn_Wv, L0_xattn_bv, L0_xattn_Wo, L0_xattn_bo, L0_ffn_ln1_g, L0_ffn_ln1_b, L0_ffn_attn_w, L0_ffn_ln2_g, L0_ffn_ln2_b, L0_ffn_gate_w, L0_ffn_gate_proj, L0_ffn_up_proj, L0_ffn_down_proj):
    import jax
    import jax.numpy as jnp

    def _L0_xattn_ref(query, key, value, mask, Wq, bq, Wk, bk, Wv, bv, Wo, bo):
        import jax, jax.numpy as jnp
        import numpy as np
        D_MODEL = 256
        H = 16
        D_K = D_MODEL // H
        B, S = (4, 512)
        NEG = -1000000000.0
        b, s, _ = query.shape

        def proj(x, W, bias):
            return (x @ W.T + bias).reshape(b, -1, H, D_K).transpose(0, 2, 1, 3)
        Q = proj(query, Wq, bq)
        K = proj(key, Wk, bk)
        V = proj(value, Wv, bv)
        scores = jnp.einsum('bhqd,bhkd->bhqk', Q, K) / np.sqrt(D_K)
        m = mask[:, None, :, :]
        scores = jnp.where(m == 0, NEG, scores)
        attn = jax.nn.softmax(scores, axis=-1)
        x = jnp.einsum('bhqk,bhkd->bhqd', attn, V)
        x = x.transpose(0, 2, 1, 3).reshape(b, -1, D_MODEL)
        return x @ Wo.T + bo

    def _L0_ffn_ref(x, ln1_g, ln1_b, attn_w, ln2_g, ln2_b, gate_w, gate_proj, up_proj, down_proj):
        import jax, jax.numpy as jnp
        import numpy as np
        HIDDEN = 256
        INTER = 1024
        NUM_EXPERTS = 8
        TOP_K = 2
        EPS = 1e-05

        def _layer_norm(x, g, b):
            m = jnp.mean(x, axis=-1, keepdims=True)
            v = jnp.mean(jnp.square(x - m), axis=-1, keepdims=True)
            return (x - m) * jax.lax.rsqrt(v + EPS) * g + b
        B, S, H = x.shape
        h = x + jnp.einsum('bsh,oh->bso', _layer_norm(x, ln1_g, ln1_b), attn_w)
        t = _layer_norm(h, ln2_g, ln2_b).reshape(-1, H)
        T = t.shape[0]
        logits = jnp.einsum('th,eh->te', t, gate_w)
        top_vals, top_idx = jax.lax.top_k(logits, TOP_K)
        rw = jax.nn.softmax(top_vals, axis=-1)
        comb = jnp.zeros((T, NUM_EXPERTS), dtype=t.dtype)
        comb = comb.at[jnp.arange(T)[:, None], top_idx].add(rw)
        out = jnp.zeros_like(t)
        for e in range(NUM_EXPERTS):
            g = jnp.einsum('th,ih->ti', t, gate_proj[e])
            u = jnp.einsum('th,ih->ti', t, up_proj[e])
            oe = jnp.einsum('ti,hi->th', jax.nn.silu(g) * u, down_proj[e])
            out = out + comb[:, e:e + 1] * oe
        return h + out.reshape(B, S, H)
    x = x + _L0_xattn_ref(_layernorm(x, axis=-1), ctx_1024, ctx_1024, mask_BxSxS2_ik0, L0_xattn_Wq, L0_xattn_bq, L0_xattn_Wk, L0_xattn_bk, L0_xattn_Wv, L0_xattn_bv, L0_xattn_Wo, L0_xattn_bo)
    x = x + _L0_ffn_ref(_layernorm(x, axis=-1), L0_ffn_ln1_g, L0_ffn_ln1_b, L0_ffn_attn_w, L0_ffn_ln2_g, L0_ffn_ln2_b, L0_ffn_gate_w, L0_ffn_gate_proj, L0_ffn_up_proj, L0_ffn_down_proj)
    return x

_drawn_inputs = setup_inputs


def setup_inputs(seed=0):
    import zlib

    import numpy as np

    out = dict(_drawn_inputs(seed))
    spreads = {'L0_xattn_bq': (0.0, 0.284),
     'L0_xattn_bk': (0.0, 0.8),
     'L0_xattn_bv': (0.0, 0.1),
     'L0_xattn_bo': (0.0, 0.1),
     'L0_ffn_ln1_g': (1.0, 0.54),
     'L0_ffn_ln1_b': (0.0, 0.509),
     'L0_ffn_ln2_g': (1.0, 0.6),
     'L0_ffn_ln2_b': (0.0, 0.8)}
    factors = {'L0_ffn_gate_w': 5.591,
     'L0_ffn_gate_proj': 5.0,
     'L0_ffn_up_proj': 4.936,
     'L0_ffn_down_proj': 4.936}
    for name, (base, spread) in spreads.items():
        noise = np.random.default_rng([zlib.crc32(name.encode()), seed]).standard_normal(out[name].shape)
        drawn = base * np.exp(spread * noise) if base else spread * noise
        out[name] = jnp.asarray(drawn.astype(out[name].dtype))
    for name, factor in factors.items():
        out[name] = (out[name] * factor).astype(out[name].dtype)
    return out
```

```python
from contextlib import ExitStack

import concourse.bass as bass
from concourse import mybir

F32 = mybir.dt.float32
I32 = mybir.dt.int32
U32 = mybir.dt.uint32
ALU = mybir.AluOpType
ACT = mybir.ActivationFunctionType
AX_X = mybir.AxisListType.X

P = 128
BATCH, SEQ, D, KEYS = 2, 1024, 256, 77
HEADS, HD = 16, 16
KD = D // P
TOKENS = BATCH * SEQ
TILES = TOKENS // P
GROUPS = 4
SLOTS = HEADS // GROUPS
SCORES = HEADS * KEYS
CHUNKS = -(-SCORES // P)
VW = HD + 1
EXPERTS, INTER, TOPK = 8, 1024, 2
IC = INTER // P
BLOCKS = TOKENS * TOPK // P + EXPERTS - 1
SPARE = EXPERTS - 1
LIST_ROWS = EXPERTS * TOKENS + SPARE * P
LIST_COLS = LIST_ROWS // P
WCOLS = KD * 2 * INTER + IC * D
WSLOTS = 3
EPS = 1e-5
NEG = -1e9
SCALE = 1.0 / HD ** 0.5


def chunk_heads(c):
    width = min(P, SCORES - c * P)
    first = c * P // KEYS
    return first, (c * P + width - 1) // KEYS - first + 1


PT_ROUNDS = -(-CHUNKS // 4)
SMALL, CONSTS = 3, 9
CHUNK_SLOTS = max(chunk_heads(c)[1] for c in range(CHUNKS))


def back(it, lag):
    d = it[1] - lag
    return it[0] + d // 2, d % 2


def number(tile):
    return 2 * tile[0] + tile[1]


def within(tile, count):
    t = number(tile)
    return not isinstance(t, int) or 0 <= t < count


def wait_count(eng, sem, count):
    if not isinstance(count, int) or count > 0:
        eng.wait_ge(sem, count)


def wait_apart(eng, sem, count, met):
    eng.wait_ge(sem, count)
    eng.sem_inc(met, 1)


def pipeline(eng, body, count, lag, first):
    pairs = (count - first) // 2
    for i in range(first):
        body((i // 2, i % 2))
    with eng.Fori(first // 2, first // 2 + pairs) as n:
        body((n, 0))
        body((n, 1))
    for i in range(first + 2 * pairs, count + lag):
        body((i // 2, i % 2))


def xattn_moe(nc, x, ctx, mask, wqT, wkT, wvT, woT, awT, gwT, columns, bv, bo, experts, out):
    with ExitStack() as stack:
        def sb(name, shape, dt=F32):
            return stack.enter_context(nc.sbuf_tensor(name, shape, dt))

        def sem(name):
            return stack.enter_context(nc.semaphore(name))

        z2_rows = nc.dram_tensor("z2_rows", (TOKENS + P, D), F32).ap()
        acc_rows = nc.dram_tensor("acc_rows", (TOKENS + P, D), F32).ap()
        lists = nc.dram_tensor("lists", (LIST_ROWS, 2), I32).ap()

        psum = stack.enter_context(nc.psum_tensor("psum", [P, 8, 512], F32))
        bank = [psum[:, i, :] for i in range(8)]

        ident = sb("ident", [P, P])
        below = sb("below", [P, P])
        ones = sb("ones", [P, P])
        half_neg = sb("half_neg", [P, 1])
        head_of = sb("head_of", [P, 2])
        row_i = sb("row_i", [P, 1], I32)
        wq_sb, wk_sb, wv_sb, wo_sb, aw_sb = (sb(n, [P, KD, D]) for n in ("wq", "wk", "wv", "wo", "aw"))
        gw_sb = sb("gw", [P, KD, EXPERTS])
        vecs = sb("vecs", [P, 6, KD])
        bq_c, bk_c, g1_c, b1_c, g2_c, b2_c = range(6)
        bv_sb = sb("bv", [P, D])
        bo_sb = sb("bo", [P, D])

        ctx_sb = sb("ctx_sb", [P, BATCH, D])
        ctxT = sb("ctxT", [P, KD, BATCH, KEYS])
        k_diag = sb("k_diag", [P, BATCH, 2, 2, KEYS])
        v_heads = sb("v_heads", [P, BATCH, HEADS, VW])
        v_chunks = sb("v_chunks", [P, CHUNKS, BATCH, CHUNK_SLOTS, VW])

        x_sb = sb("x_sb", [P, TILES, D])
        x1_sb = sb("x1_sb", [P, TILES, D])
        ceil_i = sb("ceil_i", [P, TILES, KEYS], I32)
        ceil_f = sb("ceil_f", [P, TILES, KEYS])
        stats = sb("stats", [P, 2, 6])
        mv = [sb(f"mv{i}", [P, 2, 2]) for i in range(4)]
        var_eps = [sb(f"var_eps{i}", [P, 2]) for i in range(4)]
        rstd = [sb(f"rstd{i}", [P, 2]) for i in range(4)]
        xn = sb("xn", [P, 2, D])
        xnT = sb("xnT", [P, 2, KD, P])
        qT = sb("qT", [P, 2, KD, P])
        s_sb = sb("s_sb", [P, 2, SCORES])
        s_max = sb("s_max", [P, 2, HEADS])
        p_sb = sb("p_sb", [P, 2, SCORES])
        pT = sb("pT", [P, 2, CHUNKS, P])
        o_rec = sb("o_rec", [P, 2, HEADS])
        o_sb = sb("o_sb", [P, 2, D])
        oT = sb("oT", [P, 2, KD, P])
        xf = sb("xf", [P, 2, D])
        z = sb("z", [P, 2, D])
        uT = sb("uT", [P, 2, KD, P])
        h = sb("h", [P, 2, D])
        z2 = sb("z2", [P, 2, D])
        tT = sb("tT", [P, 2, KD, P])

        expert_f = sb("expert_f", [P, EXPERTS])
        list_base = sb("list_base", [P, EXPERTS])
        top = sb("top", [P, 2, 8])
        top_i = sb("top_i", [P, 2, 8], U32)
        top_f = sb("top_f", [P, 2, TOPK])
        hot = sb("hot", [P, 2, TOPK, EXPERTS])
        chosen = sb("chosen", [P, 2, EXPERTS])
        before = sb("before", [P, 2, EXPERTS])
        place = sb("place", [P, 2, EXPERTS])
        picked = sb("picked", [P, 2, TOPK, EXPERTS])
        pos = sb("pos", [P, 2, TOPK], I32)
        tokens = sb("tokens", [P, TILES, TOPK], I32)
        expert_i = sb("expert_i", [P, EXPERTS], I32)
        gap = sb("gap", [P, 2, 1])
        e2 = sb("e2", [P, 2, 1])
        e_sum = sb("e_sum", [P, 2, 1])
        pair = sb("pair", [P, 2, TOPK, 2], I32)
        fill = sb("fill", [P, LIST_COLS, 2], I32)
        zeros = sb("zeros", [P, D])

        J = BLOCKS + 1
        steps_i = sb("steps_i", [1, J], I32)
        steps = sb("steps", [1, J])
        upto = sb("upto", [1, EXPERTS, EXPERTS])
        cnt = sb("cnt", [1, EXPERTS])
        over = sb("over", [1, EXPERTS, TILES])
        nblk = sb("nblk", [1, EXPERTS])
        cum_t = sb("cum_t", [1, EXPERTS, EXPERTS])
        cum = sb("cum", [1, EXPERTS])
        passed = sb("passed", [1, J, EXPERTS])
        passed_n = sb("passed_n", [1, J, EXPERTS])
        e_of = sb("e_of", [1, J])
        b_of = sb("b_of", [1, J])
        r_of = sb("r_of", [1, J])
        slot3 = sb("slot3", [1, J])
        slot6 = sb("slot6", [1, J])
        row_tab = sb("row_tab", [1, J], I32)
        wait_tab = sb("wait_tab", [1, J], I32)
        slot_tab = sb("slot_tab", [1, J], I32)
        free_tab = sb("free_tab", [1, EXPERTS], I32)

        w_sb = sb("w_sb", [P, WSLOTS * WCOLS])
        blk = sb("blk", [P, BLOCKS, 2], I32)
        zg = sb("zg", [P, 2, D])
        gather_at = sb("gather_at", [P, 2, 1], I32)
        add_at = sb("add_at", [P, 2, 1], I32)
        tbT = sb("tbT", [P, 2, KD, P])
        silu = p_sb[:, :, 0:512]
        act = s_sb[:, :, 0:INTER]
        actT = pT[:, :, 0:IC, :]
        y = sb("y", [P, 2, D])

        x_in = [sem(f"x_in{i}") for i in range(4)]
        ctx_in, mask_in, small_in, wkv_in, wqo_in, aw_in = (
            sem(n) for n in ("ctx_in", "mask_in", "small_in", "wkv_in", "wqo_in", "aw_in"))
        w_in = [sem(f"w_in{i}") for i in range(WSLOTS)]
        w_ready = sem("w_ready")
        consts = sem("consts")
        sel_step, head_step = sem("sel_step"), sem("head_step")
        ctxT_ps, ctxT_done, k_ps, v_ps, k_done, v_done, v_in = (
            sem(n) for n in ("ctxT_ps", "ctxT_done", "k_ps", "v_ps", "k_done", "v_done", "v_in"))
        ceil_step, ceil_done, xb_done = sem("ceil_step"), sem("ceil_done"), sem("xb_done")
        st = [sem(f"st{i}") for i in range(4)]
        var = [sem(f"var{i}") for i in range(4)]
        eps = [sem(f"eps{i}") for i in range(4)]
        rs = [sem(f"rs{i}") for i in range(4)]
        xn_done, xnT_ps, xnT_done, q_ps, q_done = (
            sem(n) for n in ("xn_done", "xnT_ps", "xnT_done", "q_ps", "q_done"))
        s_ps, s_done, max_done, sub_done, p_done, pT_ps, pT_done = (
            sem(n) for n in ("s_ps", "s_done", "max_done", "sub_done", "p_done", "pT_ps", "pT_done"))
        o_ps, orec_done, o_done, oT_ps, oT_done, wo_ps, x1_done = (
            sem(n) for n in ("o_ps", "orec_done", "o_done", "oT_ps", "oT_done", "wo_ps", "x1_done"))
        xf_done, z_done, uT_ps, uT_done, aw_ps, h_done, z2_done, tT_ps, tT_done, lg_ps = (
            sem(n) for n in ("xf_done", "z_done", "uT_ps", "uT_done", "aw_ps", "h_done", "z2_done",
                             "tT_ps", "tT_done", "lg_ps"))
        acc_done, acc_out = sem("acc_done"), sem("acc_out")
        z2_out = [sem(f"z2_out{i}") for i in range(2)]
        pad_out, fill_done, fill_out = sem("pad_out"), sem("fill_done"), sem("fill_out")
        top_done, topi_done, topf_done, hot_done, chosen_done, before_done, gap_done, e2_done, rank_ps = (
            sem(n) for n in ("top_done", "topi_done", "topf_done", "hot_done", "chosen_done",
                             "before_done", "gap_done", "e2_done", "rank_ps"))
        place_done, picked_done, esum_done, w1_done, pair_done = (
            sem(n) for n in ("place_done", "picked_done", "esum_done", "w1_done", "pair_done"))
        iota_done, router_const = sem("iota_done"), sem("router_const")
        listed = [sem(f"listed{i}") for i in range(2)]
        cnt_ps, tab, tab_done = sem("cnt_ps"), sem("tab"), sem("tab_done")
        blk_in = [sem(f"blk_in{i}") for i in range(2)]
        zg_in = [sem(f"zg_in{i}") for i in range(2)]
        tb_ps, tb_done, g_ps, u_ps, silu_done, act_done, aT_ps, aTa_done, aTb_done, y_ps, y_done, added = (
            sem(n) for n in ("tb_ps", "tb_done", "g_ps", "u_ps", "silu_done", "act_done", "aT_ps",
                             "aTa_done", "aTb_done", "y_ps", "y_done", "added"))
        dve_met, pool_met = sem("dve_met"), sem("pool_met")
        at_done, add_at_done, out_done = sem("at_done"), sem("add_at_done"), sem("out_done")

        x_tiles = x.rearrange("b (i p) d -> p i b d", p=P)
        out_tiles = out.rearrange("b (i p) d -> i b p d", p=P)
        z2_tiles = z2_rows[0:TOKENS, :].rearrange("(n b p) d -> n b p d", b=2, p=P)
        acc_tiles = acc_rows[0:TOKENS, :].rearrange("(n b p) d -> n b p d", b=2, p=P)
        x_sb_pairs = x_sb[:, :, :].rearrange("p (i b) d -> p i b d", b=2)
        x1_pairs = x1_sb[:, :, :].rearrange("p (i b) d -> p i b d", b=2)

        def of(tensor, tile):
            return tensor[:, number(tile)]

        block = stack.enter_context(nc.Block())

        @block.sync
        def _(sp):
            sp.dma_start(ctx_sb[0:KEYS, :, :], ctx.rearrange("b k d -> k b d")).then_inc(ctx_in, 16)
            for w, src in ((wk_sb, wkT), (wv_sb, wvT)):
                sp.dma_start(w[:, :, :], src.rearrange("(k p) n -> p k n", p=P)).then_inc(wkv_in, 16)
            for i in range(4):
                for b in range(BATCH):
                    sp.dma_start(x_sb_pairs[:, 2 * i:2 * i + 2, b, :], x_tiles[:, 2 * i:2 * i + 2, b, :]).then_inc(x_in[i], 16)
            for w, src in ((wq_sb, wqT), (wo_sb, woT)):
                sp.dma_start(w[:, :, :], src.rearrange("(k p) n -> p k n", p=P)).then_inc(wqo_in, 16)
            sp.dma_start(aw_sb[:, :, :], awT.rearrange("(k p) n -> p k n", p=P)).then_inc(aw_in, 16)
            sp.dma_start(gw_sb[:, :, :], gwT.rearrange("(k p) n -> p k n", p=P)).then_inc(aw_in, 16)
            for e in range(WSLOTS):
                sp.dma_start(w_sb[:, e * WCOLS:(e + 1) * WCOLS], experts[e]).then_inc(w_in[e], 16)

            sp.wait_ge(fill_done, 1)
            sp.dma_start(lists.rearrange("(p c) k -> p c k", p=P), fill[:, :, :]).then_inc(fill_out, 16)
            sp.dma_start(z2_rows[TOKENS:TOKENS + P, :], zeros[:, :]).then_inc(pad_out, 16)
            sp.dma_start(acc_rows[TOKENS:TOKENS + P, :], zeros[:, :]).then_inc(pad_out, 16)

            for e in range(WSLOTS):
                sp.wait_ge(w_in[e], 16)
                sp.sem_inc(w_ready, 1)

            def store(it):
                t = back(it, 0)
                sp.wait_ge(z2_done, number(t) + 1)
                sp.dma_start(z2_tiles[t[0], t[1]], z2[:, t[1], :]).then_inc(z2_out[t[1]], 16)
                sp.wait_ge(acc_done, number(t) + 1)
                sp.dma_start(acc_tiles[t[0], t[1]], of(x_sb, t)).then_inc(acc_out, 16)

            pipeline(sp, store, TILES, 0, 0)

            sp.wait_ge(tab_done, 1)
            for e in range(WSLOTS, EXPERTS):
                last = sp.value_load(free_tab[0:1, e - WSLOTS:e - WSLOTS + 1], min_val=1, max_val=BLOCKS + 1)
                sp.wait_ge(y_ps, last)
                s = e % WSLOTS
                sp.dma_start(w_sb[:, s * WCOLS:(s + 1) * WCOLS], experts[e]).then_inc(w_in[s], 16)
                sp.wait_ge(w_in[s], 16 * (e // WSLOTS + 1))
                sp.sem_inc(w_ready, 1)

            sp.wait_ge(added, 16 * BLOCKS)
            for b in range(BATCH):
                sp.dma_start(out_tiles[:, b], acc_tiles[:, b]).then_inc(out_done, 16)
            sp.wait_ge(out_done, 16 * BATCH)

        @block.gpsimd
        def _(pool):
            nc.gpsimd.memset(ident[:, :], 0.0).then_inc(sel_step, 1)
            nc.gpsimd.memset(below[:, :], 0.0).then_inc(sel_step, 1)
            nc.gpsimd.memset(upto[:, :, :], 1.0).then_inc(sel_step, 1)
            nc.gpsimd.memset(ones[:, :], 1.0).then_inc(consts, 1)
            nc.gpsimd.memset(half_neg[:, :], -0.5).then_inc(consts, 1)
            nc.gpsimd.memset(v_heads[:, :, :, HD:VW], 1.0).then_inc(consts, 1)
            nc.gpsimd.memset(v_chunks[:, :, :, :, :], 0.0).then_inc(consts, 1)
            nc.gpsimd.memset(before[:, 0, :], 0.0).then_inc(consts, 1)
            pool.wait_ge(sel_step, 3)
            nc.gpsimd.affine_select(out=ident[:, :], in_=ident[:, :], compare_op=ALU.not_equal, fill=1.0,
                                    base=0, pattern=[[-1, P]], channel_multiplier=1).then_inc(consts, 1)
            nc.gpsimd.affine_select(out=below[:, :], in_=below[:, :], compare_op=ALU.is_ge, fill=1.0,
                                    base=0, pattern=[[-1, P]], channel_multiplier=1).then_inc(consts, 1)
            nc.gpsimd.affine_select(out=upto[:, :, :], in_=upto[:, :, :], compare_op=ALU.is_ge, fill=0.0,
                                    base=0, pattern=[[1, EXPERTS], [-1, EXPERTS]], channel_multiplier=0).then_inc(consts, 1)
            nc.gpsimd.iota(row_i[:, :], pattern=[[0, 1]], base=0, channel_multiplier=1).then_inc(consts, 1)
            nc.gpsimd.iota(expert_i[:, :], pattern=[[1, EXPERTS]], base=0, channel_multiplier=0).then_inc(iota_done, 1)
            nc.gpsimd.iota(steps_i[:, :], pattern=[[1, J]], base=0, channel_multiplier=0).then_inc(iota_done, 1)
            nc.gpsimd.iota(fill[:, :, 0], pattern=[[1, LIST_COLS]], base=0, channel_multiplier=LIST_COLS).then_inc(iota_done, 1)
            nc.gpsimd.iota(tokens[:, :, :], pattern=[[P, TILES], [0, TOPK]], base=0, channel_multiplier=1).then_inc(iota_done, 1)
            nc.gpsimd.memset(fill[:, :, 1], 0).then_inc(iota_done, 1)
            nc.gpsimd.memset(zeros[:, :], 0.0).then_inc(iota_done, 1)

            pool.wait_ge(small_in, 16 * SMALL)
            for i in range(4):
                pool.wait_ge(x_in[i], 32)
                nc.gpsimd.tensor_tensor(x1_sb[:, 4 * i:4 * i + 4, :], x_sb[:, 4 * i:4 * i + 4, :],
                                        bo_sb[:, :].unsqueeze(1).to_broadcast([P, 4, D]), ALU.add).then_inc(xb_done, 1)

            def inverse_root(norm, t):
                par = t[1]
                wait_apart(pool, var[norm], number(t) + 1, pool_met)
                nc.gpsimd.tensor_scalar(var_eps[norm][:, par:par + 1], mv[norm][:, par, 1:2], EPS, None, ALU.add).then_inc(eps[norm], 1)
                pool.wait_ge(eps[norm], number(t) + 1)
                nc.gpsimd.tensor_tensor(rstd[norm][:, par:par + 1], var_eps[norm][:, par:par + 1], half_neg[:, :], ALU.pow).then_inc(rs[norm], 1)

            def attention(it):
                t = back(it, 0)
                if within(t, TILES):
                    inverse_root(0, t)
                t = back(it, 1)
                if within(t, TILES):
                    par = t[1]
                    pool.wait_ge(max_done, number(t) + 1)
                    s3 = s_sb[:, par, :].rearrange("p (h k) -> p h k", h=HEADS)
                    nc.gpsimd.tensor_tensor(s3, s3, s_max[:, par, :].unsqueeze(2).to_broadcast([P, HEADS, KEYS]),
                                            ALU.subtract).then_inc(sub_done, 1)

            pipeline(pool, attention, TILES, 3, 4)

            pool.wait_ge(fill_out, 16)

            def route(it):
                a, b, c = back(it, 0), back(it, 1), back(it, 2)
                if within(a, TILES):
                    inverse_root(1, a)
                if within(b, TILES):
                    inverse_root(3, b)
                if within(a, TILES):
                    inverse_root(2, a)
                if within(b, TILES):
                    pool.wait_ge(h_done, number(b) + 1)
                    nc.gpsimd.tensor_tensor(of(x_sb, b), of(x1_sb, b), h[:, b[1], :], ALU.add).then_inc(acc_done, 1)
                if within(c, TILES):
                    par = c[1]
                    wait_apart(pool, pair_done, number(c) + 1, pool_met)
                    for k in range(TOPK):
                        nc.gpsimd.indirect_dma_start(
                            lists, bass.IndirectOffsetOnAxis(ap=pos[:, par, k:k + 1], axis=0),
                            pair[:, par, k, :], None, bounds_check=LIST_ROWS - 1).then_inc(listed[par], 16)

            pipeline(pool, route, TILES, 2, 4)

            for par in range(2):
                pool.wait_ge(listed[par], 16 * TOPK * TILES // 2)
                pool.wait_ge(z2_out[par], 16 * TILES // 2)
            pool.wait_ge(pad_out, 32)
            pool.wait_ge(acc_out, 16 * TILES)
            pool.wait_ge(tab_done, 1)

            def serve(it):
                a, b, c = back(it, 0), back(it, 1), back(it, 4)
                if within(a, BLOCKS):
                    row = pool.value_load(row_tab[0:1, bass.ds(number(a), 1)], min_val=0, max_val=LIST_ROWS - P)
                    nc.gpsimd.dma_start(blk[:, number(a)], lists[bass.ds(row, P), :]).then_inc(blk_in[a[1]], 16)
                if within(b, BLOCKS):
                    pool.wait_ge(blk_in[b[1]], 16 * (b[0] + 1))
                    wait_count(pool, tb_ps, number(b) - 1)
                    pool.sem_inc(pool_met, 1)
                    nc.gpsimd.tensor_copy(gather_at[:, b[1], :], blk[:, number(b), 0:1]).then_inc(at_done, 1)
                    wait_apart(pool, at_done, number(b) + 1, pool_met)
                    nc.gpsimd.indirect_dma_start(
                        zg[:, b[1], :], None, z2_rows,
                        bass.IndirectOffsetOnAxis(ap=gather_at[:, b[1], :], axis=0),
                        bounds_check=TOKENS + P - 1).then_inc(zg_in[b[1]], 16)
                if within(c, BLOCKS):
                    pool.wait_ge(y_done, number(c) + 1)
                    wait_count(pool, added, 16 * number(c))
                    pool.sem_inc(pool_met, 1)
                    nc.gpsimd.tensor_copy(add_at[:, c[1], :], blk[:, number(c), 0:1]).then_inc(add_at_done, 1)
                    wait_apart(pool, add_at_done, number(c) + 1, pool_met)
                    nc.gpsimd.indirect_dma_start(
                        acc_rows, bass.IndirectOffsetOnAxis(ap=add_at[:, c[1], :], axis=0),
                        y[:, c[1], :], None, bounds_check=TOKENS + P - 1, compute_op=ALU.add).then_inc(added, 16)

            pipeline(pool, serve, BLOCKS, 4, 6)

        @block.scalar
        def _(act_e):
            act_e.dma_start(vecs[:, :, :], columns).then_inc(small_in, 16)
            act_e.dma_start(bv_sb[:, :], bv.partition_broadcast(P)).then_inc(small_in, 16)
            act_e.dma_start(bo_sb[:, :], bo.partition_broadcast(P)).then_inc(small_in, 16)
            for b in range(BATCH):
                act_e.dma_start(ceil_i[:, :, :].rearrange("p (i b) k -> p i b k", b=2)[:, :, b, :],
                                mask.rearrange("b (i p) k -> p i b k", p=P)[:, :, b, :]).then_inc(mask_in, 16)

            act_e.wait_ge(v_done, 2)
            act_e.wait_ge(consts, CONSTS)
            for c in range(CHUNKS):
                first, n = chunk_heads(c)
                for s in range(first, first + n):
                    k0 = max(0, c * P - s * KEYS)
                    k1 = min(KEYS, (c + 1) * P - s * KEYS)
                    r0 = s * KEYS + k0 - c * P
                    act_e.dma_start(v_chunks[r0:r0 + k1 - k0, c, :, s - first, :],
                                    v_heads[k0:k1, :, s, :]).then_inc(v_in, 16)
            act_e.wait_ge(small_in, 16 * SMALL)

            def attention(it):
                t = back(it, 1)
                if within(t, TILES):
                    act_e.wait_ge(xnT_ps, number(t) + 1)
                    nc.scalar.activation(xnT[:, t[1], :, :], bank[7][:, 0:D], ACT.Copy).then_inc(xnT_done, 1)
                t = back(it, 3)
                if within(t, TILES):
                    act_e.wait_ge(oT_ps, number(t) + 1)
                    nc.scalar.activation(oT[:, t[1], :, :], bank[6][:, 0:D], ACT.Copy).then_inc(oT_done, 1)
                t = back(it, 1)
                if within(t, TILES):
                    act_e.wait_ge(q_ps, number(t) + 1)
                    for m in range(KD):
                        nc.scalar.activation(qT[:, t[1], m, :], bank[7][:, m * P:(m + 1) * P], ACT.Identity,
                                             bias=vecs[:, bq_c, m:m + 1]).then_inc(q_done, 1)
                t = back(it, 2)
                if within(t, TILES):
                    for r, c0 in enumerate(range(0, CHUNKS, 4)):
                        n = min(4, CHUNKS - c0)
                        act_e.wait_ge(pT_ps, PT_ROUNDS * number(t) + r + 1)
                        nc.scalar.activation(pT[:, t[1], c0:c0 + n, :], bank[4 + r % 2][:, 0:n * P], ACT.Copy).then_inc(pT_done, 1)
                t = back(it, 1)
                if within(t, TILES):
                    act_e.wait_ge(sub_done, number(t) + 1)
                    nc.scalar.activation(p_sb[:, t[1], :], s_sb[:, t[1], :], ACT.Exp, scale=SCALE).then_inc(p_done, 1)

            pipeline(act_e, attention, TILES, 3, 4)

            def route(it):
                b, c = back(it, 1), back(it, 2)
                if within(b, TILES):
                    act_e.wait_ge(uT_ps, number(b) + 1)
                    for k in range(KD):
                        nc.scalar.activation(uT[:, b[1], k, :], bank[0 + b[1]][:, k * P:(k + 1) * P], ACT.Identity,
                                             bias=vecs[:, b1_c, k:k + 1], scale=vecs[:, g1_c, k:k + 1]).then_inc(uT_done, 1)
                if within(c, TILES):
                    act_e.wait_ge(tT_ps, number(c) + 1)
                    for k in range(KD):
                        nc.scalar.activation(tT[:, c[1], k, :], bank[4 + c[1]][:, k * P:(k + 1) * P], ACT.Identity,
                                             bias=vecs[:, b2_c, k:k + 1], scale=vecs[:, g2_c, k:k + 1]).then_inc(tT_done, 1)
                    act_e.wait_ge(gap_done, number(c) + 1)
                    nc.scalar.activation(e2[:, c[1], :], gap[:, c[1], :], ACT.Exp).then_inc(e2_done, 1)

            pipeline(act_e, route, TILES, 2, 4)

            def experts_(it):
                a, b, c = back(it, 0), back(it, 1), back(it, 2)
                if within(b, BLOCKS):
                    act_e.wait_ge(g_ps, 2 * number(b) + 1)
                    wait_count(act_e, act_done, 2 * number(b) - 1)
                    nc.scalar.activation(silu[:, 0, :], bank[0], ACT.Silu).then_inc(silu_done, 1)
                if within(c, BLOCKS):
                    act_e.wait_ge(aT_ps, 2 * number(c) + 1)
                    nc.scalar.activation(actT[:, c[1], 0:4, :], bank[4], ACT.Copy).then_inc(aTa_done, 1)
                if within(b, BLOCKS):
                    act_e.wait_ge(g_ps, 2 * number(b) + 2)
                    wait_count(act_e, act_done, 2 * number(b))
                    nc.scalar.activation(silu[:, 1, :], bank[2], ACT.Silu).then_inc(silu_done, 1)
                if within(a, BLOCKS):
                    act_e.wait_ge(tb_ps, number(a) + 1)
                    for k in range(KD):
                        nc.scalar.activation(tbT[:, a[1], k, :], bank[6][:, k * P:(k + 1) * P], ACT.Identity,
                                             bias=vecs[:, b2_c, k:k + 1], scale=vecs[:, g2_c, k:k + 1]).then_inc(tb_done, 1)

            pipeline(act_e, experts_, BLOCKS, 2, 4)

        @block.vector
        def _(dve):
            dve.wait_ge(ctxT_ps, 1)
            nc.vector.tensor_copy(ctxT[:, :, :, :], bank[0][:, 0:KD * BATCH * KEYS]).then_inc(ctxT_done, 1)
            dve.wait_ge(small_in, 16 * SMALL)
            dve.wait_ge(consts, CONSTS)
            dve.wait_ge(v_ps, 1)
            for b in range(BATCH):
                nc.vector.tensor_tensor(v_heads[0:KEYS, b, :, 0:HD],
                                        bank[2 + b][0:KEYS, 0:D].rearrange("p (h d) -> p h d", h=HEADS),
                                        bv_sb[0:KEYS, :].rearrange("p (h d) -> p h d", h=HEADS), ALU.add).then_inc(v_done, 1)
            nc.vector.tensor_scalar(row_i[:, :], row_i[:, :], HD, None, ALU.bitwise_and).then_inc(head_step, 1)
            dve.wait_ge(head_step, 1)
            nc.vector.tensor_scalar(head_of[:, 0:1], row_i[:, :], float(HD), None, ALU.is_lt).then_inc(head_step, 1)
            nc.vector.tensor_scalar(head_of[:, 1:2], row_i[:, :], float(HD), None, ALU.is_ge).then_inc(head_step, 1)
            dve.wait_ge(head_step, 3)
            dve.wait_ge(k_ps, 1)
            for m in range(2):
                for q in range(2):
                    nc.vector.tensor_scalar(k_diag[:, :, m, q, :],
                                            bank[1][:, m * BATCH * KEYS:(m + 1) * BATCH * KEYS].rearrange("p (b k) -> p b k", b=BATCH),
                                            vecs[:, bk_c, m:m + 1], head_of[:, q:q + 1], ALU.add, ALU.mult).then_inc(k_done, 1)
            dve.wait_ge(mask_in, 32)
            nc.vector.tensor_scalar(ceil_f[:, :, :], ceil_i[:, :, :], 0.0, 3e38, ALU.not_equal, ALU.mult).then_inc(ceil_step, 1)
            dve.wait_ge(ceil_step, 1)
            nc.vector.tensor_scalar(ceil_f[:, :, :], ceil_f[:, :, :], NEG / SCALE, None, ALU.add).then_inc(ceil_step, 1)
            dve.wait_ge(ceil_step, 2)
            dve.wait_ge(iota_done, 6)
            nc.vector.tensor_scalar(fill[:, :, 0], fill[:, :, 0], P - 1, TOKENS, ALU.bitwise_and, ALU.bitwise_or).then_inc(fill_done, 1)
            nc.vector.tensor_copy(expert_f[:, :], expert_i[:, :]).then_inc(router_const, 1)
            nc.vector.tensor_copy(steps[:, :], steps_i[:, :]).then_inc(router_const, 1)
            dve.wait_ge(router_const, 2)
            nc.vector.tensor_scalar(list_base[:, :], expert_f[:, :], float(TOKENS), None, ALU.mult).then_inc(router_const, 1)

            for i in range(4):
                dve.wait_ge(x_in[i], 32)

            def norm_stats(norm, src, t):
                nc.vector.bn_stats(stats[:, t[1], :], src).then_inc(st[norm], 1)
                wait_apart(dve, st[norm], number(t) + 1, dve_met)
                nc.vector.bn_aggr(mv[norm][:, t[1], :], stats[:, t[1], :]).then_inc(var[norm], 1)

            def norm_apply(norm, dst, src, t, done):
                dve.wait_ge(rs[norm], number(t) + 1)
                nc.vector.tensor_scalar(dst, src, mv[norm][:, t[1], 0:1], rstd[norm][:, t[1]:t[1] + 1],
                                        ALU.subtract, ALU.mult).then_inc(done, 1)

            def attention(it):
                a = back(it, 0)
                if within(a, TILES):
                    norm_stats(0, of(x_sb, a), a)
                t = back(it, 3)
                if within(t, TILES):
                    dve.wait_ge(wo_ps, number(t) + 1)
                    nc.vector.tensor_tensor(of(x1_sb, t), bank[6][:, 0:D], of(x1_sb, t), ALU.add).then_inc(x1_done, 1)
                t = back(it, 1)
                if within(t, TILES):
                    par = t[1]
                    dve.wait_ge(s_ps, number(t) + 1)
                    wait_count(dve, p_done, number(t) - 1)
                    nc.vector.tensor_tensor(
                        s_sb[:, par, :].rearrange("p (g s k) -> p g s k", g=GROUPS, s=SLOTS),
                        psum[:, 0:4, 0:SLOTS * KEYS].rearrange("p g (s k) -> p g s k", s=SLOTS),
                        of(ceil_f, t).unsqueeze(1).unsqueeze(1).to_broadcast([P, GROUPS, SLOTS, KEYS]),
                        ALU.min).then_inc(s_done, 1)
                    dve.wait_ge(s_done, number(t) + 1)
                    nc.vector.reduce_max(s_max[:, par, :], s_sb[:, par, :].rearrange("p (h k) -> p h k", h=HEADS), AX_X).then_inc(max_done, 1)
                if within(a, TILES):
                    wait_count(dve, xnT_ps, number(a) - 1)
                    norm_apply(0, xn[:, a[1], :], of(x_sb, a), a, xn_done)
                t = back(it, 2)
                if within(t, TILES):
                    par = t[1]
                    dve.wait_ge(o_ps, number(t) + 1)
                    o3 = bank[6][:, 0:HEADS * VW].rearrange("p (h v) -> p h v", h=HEADS)
                    nc.vector.reciprocal(o_rec[:, par, :], o3[:, :, HD]).then_inc(orec_done, 1)
                    dve.wait_ge(orec_done, number(t) + 1)
                    nc.vector.tensor_tensor(o_sb[:, par, :].rearrange("p (h d) -> p h d", h=HEADS), o3[:, :, 0:HD],
                                            o_rec[:, par, :].unsqueeze(2).to_broadcast([P, HEADS, HD]), ALU.mult).then_inc(o_done, 1)

            for i in range(4):
                dve.wait_ge(xb_done, i + 1)
            pipeline(dve, attention, TILES, 3, 4)

            def route(it):
                a, b, c = back(it, 0), back(it, 1), back(it, 2)
                if within(a, TILES):
                    dve.wait_ge(x1_done, number(a) + 1)
                    norm_stats(1, of(x1_sb, a), a)
                if within(b, TILES):
                    par = b[1]
                    dve.wait_ge(aw_ps, number(b) + 1)
                    wait_count(dve, acc_done, number(b) - 1)
                    nc.vector.tensor_tensor(h[:, par, :], bank[2 + par][:, 0:D], xf[:, par, :], ALU.add).then_inc(h_done, 1)
                    dve.wait_ge(h_done, number(b) + 1)
                    norm_stats(3, h[:, par, :], b)
                if within(a, TILES):
                    norm_apply(1, xf[:, a[1], :], of(x1_sb, a), a, xf_done)
                    dve.wait_ge(xf_done, number(a) + 1)
                    norm_stats(2, xf[:, a[1], :], a)
                if within(b, TILES):
                    wait_count(dve, z2_out[b[1]], 16 * b[0])
                    norm_apply(3, z2[:, b[1], :], h[:, b[1], :], b, z2_done)
                if within(c, TILES):
                    par, n = c[1], number(c) + 1
                    logits = bank[6 + par][:, 0:EXPERTS]
                    wait_apart(dve, lg_ps, n, dve_met)
                    nc.vector.max(top[:, par, :], logits).then_inc(top_done, 1)
                    wait_apart(dve, top_done, n, dve_met)
                    nc.vector.max_index(top_i[:, par, :], top[:, par, :], logits).then_inc(topi_done, 1)
                    dve.wait_ge(topi_done, n)
                    nc.vector.tensor_copy(top_f[:, par, :], top_i[:, par, 0:TOPK]).then_inc(topf_done, 1)
                    nc.vector.tensor_tensor(gap[:, par, :], top[:, par, 1:2], top[:, par, 0:1], ALU.subtract).then_inc(gap_done, 1)
                    dve.wait_ge(topf_done, n)
                    nc.vector.tensor_tensor(hot[:, par, :, :], expert_f[:, :].unsqueeze(1).to_broadcast([P, TOPK, EXPERTS]),
                                            top_f[:, par, :].unsqueeze(2).to_broadcast([P, TOPK, EXPERTS]), ALU.is_equal).then_inc(hot_done, 1)
                    dve.wait_ge(hot_done, n)
                    nc.vector.tensor_tensor(chosen[:, par, :], hot[:, par, 0, :], hot[:, par, 1, :], ALU.add).then_inc(chosen_done, 1)
                    dve.wait_ge(chosen_done, n)
                    nc.vector.tensor_tensor(before[:, 1 - par, :], before[:, par, :], chosen[:, par, :], ALU.add).then_inc(before_done, 1)
                if within(a, TILES):
                    norm_apply(2, z[:, a[1], :], xf[:, a[1], :], a, z_done)
                if within(c, TILES):
                    dve.wait_ge(rank_ps, n)
                    nc.vector.tensor_tensor(place[:, par, :], bank[6 + par][:, EXPERTS:2 * EXPERTS], list_base[:, :], ALU.add).then_inc(place_done, 1)
                    dve.wait_ge(e2_done, n)
                    nc.vector.tensor_scalar(e_sum[:, par, :], e2[:, par, :], 1.0, None, ALU.add).then_inc(esum_done, 1)
                    dve.wait_ge(place_done, n)
                    nc.vector.tensor_tensor(picked[:, par, :, :], hot[:, par, :, :],
                                            place[:, par, :].unsqueeze(1).to_broadcast([P, TOPK, EXPERTS]), ALU.mult).then_inc(picked_done, 1)
                    wait_count(dve, listed[par], 16 * TOPK * c[0])
                    weight = pair[:, par, :, :].bitcast(F32)
                    dve.wait_ge(esum_done, n)
                    nc.vector.reciprocal(weight[:, 0, 1:2], e_sum[:, par, :]).then_inc(w1_done, 1)
                    dve.wait_ge(picked_done, n)
                    with nc.allow_low_precision(reason="one of eight is not 0: a whole number under 2^24"):
                        nc.vector.tensor_reduce(pos[:, par, :], picked[:, par, :, :], AX_X, ALU.add)
                    nc.vector.tensor_copy(pair[:, par, :, 0], of(tokens, c))
                    dve.wait_ge(w1_done, n)
                    nc.vector.tensor_tensor(weight[:, 1, 1:2], weight[:, 0, 1:2], e2[:, par, :], ALU.mult).then_inc(pair_done, 1)

            pipeline(dve, route, TILES, 2, 4)

            steps_done = [0]

            def step(instruction):
                steps_done[0] += 1
                instruction.then_inc(tab, 1)
                dve.wait_ge(tab, steps_done[0])

            dve.wait_ge(cnt_ps, 1)
            step(nc.vector.tensor_copy(cnt[:, :], bank[0][0:1, 0:EXPERTS]))
            step(nc.vector.tensor_scalar(over[0:1, 0, :], steps[0:1, 0:TILES], float(P), None, ALU.mult))
            step(nc.vector.tensor_tensor(passed_n[0:1, 0:TILES, :], cnt[:, :].unsqueeze(1).to_broadcast([1, TILES, EXPERTS]),
                                         over[0:1, 0, :].unsqueeze(2).to_broadcast([1, TILES, EXPERTS]), ALU.is_gt))
            step(nc.vector.tensor_reduce(nblk[:, :], passed_n[0:1, 0:TILES, :].rearrange("o t e -> o e t"), AX_X, ALU.add))
            step(nc.vector.tensor_tensor(cum_t[:, :, :], upto[:, :, :], nblk[:, :].unsqueeze(1).to_broadcast([1, EXPERTS, EXPERTS]), ALU.mult))
            step(nc.vector.tensor_reduce(cum[:, :], cum_t[:, :, :], AX_X, ALU.add))
            step(nc.vector.tensor_scalar(free_tab[:, :], cum[:, :], 1.0, None, ALU.add))
            step(nc.vector.tensor_tensor(passed[:, :, :], steps[:, :].unsqueeze(2).to_broadcast([1, J, EXPERTS]),
                                         cum[:, :].unsqueeze(1).to_broadcast([1, J, EXPERTS]), ALU.is_ge))
            step(nc.vector.tensor_tensor(passed_n[:, :, :], passed[:, :, :], nblk[:, :].unsqueeze(1).to_broadcast([1, J, EXPERTS]), ALU.mult))
            step(nc.vector.tensor_reduce(e_of[:, :], passed[:, :, :], AX_X, ALU.add))
            step(nc.vector.tensor_reduce(b_of[:, :], passed_n[:, :, :], AX_X, ALU.add))
            step(nc.vector.scalar_tensor_tensor(r_of[:, :], e_of[:, :], float(TOKENS // P), steps[:, :], ALU.mult, ALU.add))
            step(nc.vector.tensor_tensor(r_of[:, :], r_of[:, :], b_of[:, :], ALU.subtract))
            step(nc.vector.tensor_scalar(row_tab[:, :], r_of[:, :], float(P), None, ALU.mult))
            step(nc.vector.tensor_scalar(e_of[:, :], e_of[:, :], float(EXPERTS - 1), None, ALU.min))
            step(nc.vector.tensor_scalar(wait_tab[:, :], e_of[:, :], 1.0, None, ALU.add))
            step(nc.vector.tensor_scalar(slot3[:, :], e_of[:, :], float(WSLOTS), float(WSLOTS), ALU.is_ge, ALU.mult))
            step(nc.vector.tensor_scalar(slot6[:, :], e_of[:, :], float(2 * WSLOTS), float(WSLOTS), ALU.is_ge, ALU.mult))
            step(nc.vector.tensor_tensor(slot3[:, :], slot3[:, :], slot6[:, :], ALU.add))
            step(nc.vector.tensor_tensor(slot3[:, :], e_of[:, :], slot3[:, :], ALU.subtract))
            nc.vector.tensor_scalar(slot_tab[:, :], slot3[:, :], float(WCOLS), None, ALU.mult).then_inc(tab_done, 1)

            def experts_(it):
                b, c = back(it, 1), back(it, 2)
                if within(b, BLOCKS):
                    dve.wait_ge(silu_done, 2 * number(b) + 1)
                    dve.wait_ge(u_ps, 2 * number(b) + 1)
                    nc.vector.tensor_tensor(act[:, b[1], 0:512], bank[1], silu[:, 0, :], ALU.mult).then_inc(act_done, 1)
                if within(c, BLOCKS):
                    dve.wait_ge(aT_ps, 2 * number(c) + 2)
                    nc.vector.tensor_copy(actT[:, c[1], 4:8, :], bank[5]).then_inc(aTb_done, 1)
                if within(b, BLOCKS):
                    dve.wait_ge(silu_done, 2 * number(b) + 2)
                    dve.wait_ge(u_ps, 2 * number(b) + 2)
                    nc.vector.tensor_tensor(act[:, b[1], 512:1024], bank[3], silu[:, 1, :], ALU.mult).then_inc(act_done, 1)
                if within(c, BLOCKS):
                    dve.wait_ge(y_ps, number(c) + 2)
                    wait_count(dve, added, 16 * (number(c) - 1))
                    nc.vector.tensor_scalar(y[:, c[1], :], bank[7][:, 0:D], blk[:, number(c), 1:2].bitcast(F32), None, ALU.mult).then_inc(y_done, 1)

            pipeline(dve, experts_, BLOCKS, 2, 4)

        @block.tensor
        def _(pe):
            pe.wait_ge(consts, CONSTS)
            pe.wait_ge(ctx_in, 16)
            for k in range(KD):
                for b in range(BATCH):
                    at = (k * BATCH + b) * KEYS
                    last = nc.tensor.transpose(bank[0][:, at:at + KEYS], ctx_sb[0:KEYS, b, k * P:(k + 1) * P], ident[0:KEYS, 0:KEYS])
            last.then_inc(ctxT_ps, 1)
            pe.wait_ge(wkv_in, 32)
            pe.wait_ge(ctxT_done, 1)
            for b in range(BATCH):
                for k in range(KD):
                    last = nc.tensor.matmul(bank[2 + b][0:KEYS, 0:D], ctxT[:, k, b, :], wv_sb[:, k, :], start=k == 0, stop=k == KD - 1)
            last.then_inc(v_ps, 1)
            for m in range(2):
                for k in range(KD):
                    last = nc.tensor.matmul(bank[1][:, m * BATCH * KEYS:(m + 1) * BATCH * KEYS], wk_sb[:, k, m * P:(m + 1) * P],
                                            ctxT[:, k, :, :].rearrange("p b k -> p (b k)"), start=k == 0, stop=k == KD - 1)
            last.then_inc(k_ps, 1)
            pe.wait_ge(wqo_in, 32)
            pe.wait_ge(k_done, 4)
            pe.wait_ge(v_done, 2)
            pe.wait_ge(v_in, 16 * sum(chunk_heads(c)[1] for c in range(CHUNKS)))

            def attention(it):
                t1, t2, t3 = back(it, 1), back(it, 2), back(it, 3)
                if within(t1, TILES):
                    n, par = number(t1), t1[1]
                    pe.wait_ge(xn_done, n + 1)
                    wait_count(pe, q_done, 2 * n)
                    for k in range(KD):
                        last = nc.tensor.transpose(bank[7][:, k * P:(k + 1) * P], xn[:, par, k * P:(k + 1) * P], ident[:, :])
                    last.then_inc(xnT_ps, 1)
                if within(t3, TILES):
                    pe.wait_ge(o_done, number(t3) + 1)
                    for k in range(KD):
                        last = nc.tensor.transpose(bank[6][:, k * P:(k + 1) * P], o_sb[:, t3[1], k * P:(k + 1) * P], ident[:, :])
                    last.then_inc(oT_ps, 1)
                if within(t1, TILES):
                    pe.wait_ge(xnT_done, n + 1)
                    for m in range(KD):
                        for k in range(KD):
                            last = nc.tensor.matmul(bank[7][:, m * P:(m + 1) * P], wq_sb[:, k, m * P:(m + 1) * P],
                                                    xnT[:, par, k, :], start=k == 0, stop=k == KD - 1)
                    last.then_inc(q_ps, 1)
                if within(t3, TILES):
                    pe.wait_ge(oT_done, number(t3) + 1)
                    for k in range(KD):
                        last = nc.tensor.matmul(bank[6][:, 0:D], oT[:, t3[1], k, :], wo_sb[:, k, :], start=k == 0, stop=k == KD - 1)
                    last.then_inc(wo_ps, 1)
                if within(t1, TILES):
                    pe.wait_ge(q_done, 2 * n + 2)
                    wait_count(pe, s_done, n)
                    for m in range(2):
                        for g in range(GROUPS):
                            rows = slice(32 * g, 32 * g + 32)
                            last = nc.tensor.matmul(bank[g][:, m * 2 * KEYS:(m + 1) * 2 * KEYS], qT[rows, par, m, :],
                                                    k_diag[rows, par, m, :, :].rearrange("p q k -> p (q k)"), start=True, stop=True)
                    last.then_inc(s_ps, 1)
                if within(t2, TILES):
                    n, par = number(t2), t2[1]
                    pe.wait_ge(p_done, n + 1)
                    for r, c0 in enumerate(range(0, CHUNKS, 4)):
                        wait_count(pe, pT_done, PT_ROUNDS * n + (r - 1 if r > 1 else 0))
                        for c in range(c0, min(c0 + 4, CHUNKS)):
                            w = min(P, SCORES - c * P)
                            last = nc.tensor.transpose(bank[4 + r % 2][0:w, (c - c0) * P:(c - c0 + 1) * P], p_sb[:, par, c * P:c * P + w], ident[:, :])
                        last.then_inc(pT_ps, 1)
                    pe.wait_ge(pT_done, PT_ROUNDS * (n + 1))
                    wait_count(pe, x1_done, n)
                    for c in range(CHUNKS):
                        w = min(P, SCORES - c * P)
                        first, heads = chunk_heads(c)
                        last = nc.tensor.matmul(bank[6][:, first * VW:(first + heads) * VW], pT[0:w, par, c, :],
                                                v_chunks[0:w, c, par, 0:heads, :].rearrange("p s v -> p (s v)"),
                                                start=c == 0, stop=c == CHUNKS - 1, skip_group_check=True)
                    last.then_inc(o_ps, 1)

            pipeline(pe, attention, TILES, 3, 4)

            pe.wait_ge(s_done, TILES)
            pe.wait_ge(x1_done, TILES)
            pe.wait_ge(aw_in, 32)

            def route(it):
                b, c = back(it, 1), back(it, 2)
                if within(b, TILES):
                    pe.wait_ge(z_done, number(b) + 1)
                    for k in range(KD):
                        last = nc.tensor.transpose(bank[0 + b[1]][:, k * P:(k + 1) * P], z[:, b[1], k * P:(k + 1) * P], ident[:, :])
                    last.then_inc(uT_ps, 1)
                if within(c, TILES):
                    pe.wait_ge(z2_done, number(c) + 1)
                    for k in range(KD):
                        last = nc.tensor.transpose(bank[4 + c[1]][:, k * P:(k + 1) * P], z2[:, c[1], k * P:(k + 1) * P], ident[:, :])
                    last.then_inc(tT_ps, 1)
                if within(b, TILES):
                    pe.wait_ge(uT_done, 2 * number(b) + 2)
                    for k in range(KD):
                        last = nc.tensor.matmul(bank[2 + b[1]][:, 0:D], uT[:, b[1], k, :], aw_sb[:, k, :], start=k == 0, stop=k == KD - 1)
                    last.then_inc(aw_ps, 1)
                if within(c, TILES):
                    n, par = number(c), c[1]
                    pe.wait_ge(tT_done, 2 * n + 2)
                    wait_count(pe, place_done, n - 1)
                    for k in range(KD):
                        last = nc.tensor.matmul(bank[6 + par][:, 0:EXPERTS], tT[:, par, k, :], gw_sb[:, k, :], start=k == 0, stop=k == KD - 1)
                    last.then_inc(lg_ps, 1)
                    pe.wait_ge(chosen_done, n + 1)
                    nc.tensor.matmul(bank[6 + par][:, EXPERTS:2 * EXPERTS], below[:, :], chosen[:, par, :], start=True, stop=False)
                    nc.tensor.matmul(bank[6 + par][:, EXPERTS:2 * EXPERTS], ones[:, :], before[:, par, :], start=False, stop=True).then_inc(rank_ps, 1)

            pipeline(pe, route, TILES, 2, 4)

            pe.wait_ge(before_done, TILES)
            nc.tensor.matmul(bank[0][:, 0:EXPERTS], ones[:, :], before[:, 0, :], start=True, stop=True).then_inc(cnt_ps, 1)
            pe.wait_ge(place_done, TILES)
            pe.wait_ge(tab_done, 1)
            pe.sem_inc(y_ps, 1)

            def products(half, b, slot):
                par, n = b[1], number(b)
                for which, sem_ in ((0, g_ps), (1, u_ps)):
                    wait_count(pe, silu_done if which == 0 else act_done, 2 * n - 1 + half)
                    for k in range(KD):
                        at = (2 * k + which) * INTER + half * 512
                        last = nc.tensor.matmul(bank[2 * half + which], tbT[:, par, k, :], w_sb[:, bass.ds(slot + at, 512)],
                                                start=k == 0, stop=k == KD - 1)
                    last.then_inc(sem_, 1)

            slot_of = {}

            def experts_(it):
                a, b, c = back(it, 0), back(it, 1), back(it, 2)
                if within(b, BLOCKS):
                    ready = pe.value_load(wait_tab[0:1, bass.ds(number(b), 1)], min_val=1, max_val=EXPERTS)
                    slot = pe.value_load(slot_tab[0:1, bass.ds(number(b), 1)], min_val=0, max_val=(WSLOTS - 1) * WCOLS)
                    pe.wait_ge(w_ready, ready)
                    pe.wait_ge(tb_done, 2 * number(b) + 2)
                    products(0, b, slot)
                if within(c, BLOCKS):
                    par, n = c[1], number(c)
                    for half, done in ((0, aTa_done), (1, aTb_done)):
                        pe.wait_ge(act_done, 2 * n + half + 1)
                        wait_count(pe, done, n)
                        for i in range(4):
                            at = half * 512 + i * P
                            last = nc.tensor.transpose(bank[4 + half][:, i * P:(i + 1) * P], act[:, par, at:at + P], ident[:, :])
                        last.then_inc(aT_ps, 1)
                if within(b, BLOCKS):
                    products(1, b, slot)
                if within(a, BLOCKS):
                    pe.wait_ge(zg_in[a[1]], 16 * (a[0] + 1))
                    wait_count(pe, tb_done, 2 * number(a))
                    for k in range(KD):
                        last = nc.tensor.transpose(bank[6][:, k * P:(k + 1) * P], zg[:, a[1], k * P:(k + 1) * P], ident[:, :])
                    last.then_inc(tb_ps, 1)
                if within(c, BLOCKS):
                    slot_c = pe.value_load(slot_tab[0:1, bass.ds(number(c), 1)], min_val=0, max_val=(WSLOTS - 1) * WCOLS)
                    wait_count(pe, y_done, n)
                    for i in range(IC):
                        if i % 4 == 0:
                            pe.wait_ge(aTa_done if i == 0 else aTb_done, n + 1)
                        last = nc.tensor.matmul(bank[7][:, 0:D], actT[:, par, i, :], w_sb[:, bass.ds(slot_c + KD * 2 * INTER + i * D, D)],
                                                start=i == 0, stop=i == IC - 1)
                    last.then_inc(y_ps, 1)

            pipeline(pe, experts_, BLOCKS, 2, 4)


def _heads_of_slots():
    return [m * (HEADS // 2) + 2 * g + q for g in range(GROUPS) for m in range(2) for q in range(2)]


_INS = ["x", "ctx", "mask", "wqT", "wkT", "wvT", "woT", "awT", "gwT", "columns", "bv", "bo", "experts"]


def kernel(**inputs):
    import numpy as np
    import concourse.bacc as bacc
    from concourse.bass_utils import run_bass_kernel_spmd

    a = {k: np.asarray(v) for k, v in inputs.items()}
    heads = _heads_of_slots()
    cols = np.array([h * HD + d for h in heads for d in range(HD)])
    per_column = ["L0_xattn_bq", "L0_xattn_bk", "L0_ffn_ln1_g", "L0_ffn_ln1_b", "L0_ffn_ln2_g", "L0_ffn_ln2_b"]
    gate_up = np.stack([a["L0_ffn_gate_proj"], a["L0_ffn_up_proj"]], axis=1)
    gate_up = gate_up.reshape(EXPERTS, 2, INTER, KD, P).transpose(0, 4, 3, 1, 2).reshape(EXPERTS, P, KD * 2 * INTER)
    down = a["L0_ffn_down_proj"].reshape(EXPERTS, D, IC, P).transpose(0, 3, 2, 1).reshape(EXPERTS, P, IC * D)
    laid = {
        "x": a["x"], "ctx": a["ctx_1024"], "mask": a["mask_BxSxS2_ik0"],
        "wqT": a["L0_xattn_Wq"].T, "wkT": a["L0_xattn_Wk"].T, "wvT": a["L0_xattn_Wv"].T[:, cols],
        "woT": a["L0_xattn_Wo"].T[cols, :], "awT": a["L0_ffn_attn_w"].T, "gwT": a["L0_ffn_gate_w"].T,
        "columns": np.stack([a[n].reshape(KD, P).T for n in per_column], axis=1),
        "bv": a["L0_xattn_bv"][cols], "bo": a["L0_xattn_bo"],
        "experts": np.concatenate([gate_up, down], axis=2),
    }
    nc = bacc.Bacc("TRN2", target_bir_lowering=False, num_devices=1)
    arrays, args = {}, []
    for name in _INS:
        v = np.ascontiguousarray(laid[name])
        arrays[f"in_{name}"] = v
        args.append(nc.dram_tensor(f"in_{name}", v.shape, mybir.dt.from_np(v.dtype), kind="ExternalInput").ap())
    result = nc.dram_tensor("out_x", (BATCH, SEQ, D), F32, kind="ExternalOutput").ap()
    xattn_moe(nc, *args, result)
    r = run_bass_kernel_spmd(nc, [arrays], core_ids=[0])
    return r.results[0]["out_x"]
```

```python
from contextlib import ExitStack

import concourse.bass as bass
from concourse import mybir

F32 = mybir.dt.float32
F32R = mybir.dt.float32r
I32 = mybir.dt.int32
U32 = mybir.dt.uint32
ALU = mybir.AluOpType
ACT = mybir.ActivationFunctionType
AX_X = mybir.AxisListType.X

P = 128
BATCH, SEQ, D, KEYS = 2, 1024, 256, 77
HEADS, HD = 16, 16
KD = D // P
TOKENS = BATCH * SEQ
TILES = TOKENS // P
HALF_HEADS = HEADS // KD
BANK_HEADS = 512 // KEYS
SCORES = HEADS * KEYS
FULL_BANKS = HEADS // BANK_HEADS
FULL_HEADS = FULL_BANKS * BANK_HEADS
RANKS_AT = (HEADS - FULL_HEADS) * KEYS
CHUNKS = -(-SCORES // P)
LOGITS_AT = HEADS * (HD + 1)
VW = HD + 1
EXPERTS, INTER, TOPK = 8, 1024, 2
IC = INTER // P
BLOCKS = TOKENS * TOPK // P + EXPERTS - 1
SPARE = EXPERTS - 1
LIST_ROWS = EXPERTS * TOKENS + SPARE * P
LIST_COLS = LIST_ROWS // P
WCOLS = KD * 2 * INTER + IC * D
GU_COLS = KD * 2 * INTER
SPLIT = 2 * WCOLS
GATHERS = 4
PARTS = KD + 1
EPS = 1e-5
NEG = -1e9
SCALE = 1.0 / HD ** 0.5


def chunk_heads(c):
    width = min(P, SCORES - c * P)
    first = c * P // KEYS
    return first, (c * P + width - 1) // KEYS - first + 1


PT_ROUNDS = -(-CHUNKS // 4)
SMALL, CONSTS = 3, 9
CHUNK_SLOTS = max(chunk_heads(c)[1] for c in range(CHUNKS))


class Step(tuple):
    def __new__(cls, n, r, unroll):
        step = super().__new__(cls, (n, r))
        step.unroll = unroll
        return step

    @property
    def par(self):
        return self[1] % 2


def back(it, lag):
    d = it[1] - lag
    return Step(it[0] + d // it.unroll, d % it.unroll, it.unroll)


def number(step):
    return step.unroll * step[0] + step[1]


LN1, XT, QK, PV, PROJ, LN2, MIX, LIST, SCATTER = range(9)


def within(tile, count):
    t = number(tile)
    return not isinstance(t, int) or 0 <= t < count


def wait_count(eng, sem, count):
    if not isinstance(count, int) or count > 0:
        eng.wait_ge(sem, count)


def wait_apart(eng, sem, count, met):
    eng.wait_ge(sem, count)
    eng.sem_inc(met, 1)


def pipeline(eng, body, count, lag, first, unroll=2, begin=0):
    rounds = (count - first) // unroll
    for i in range(begin, first):
        body(Step(i // unroll, i % unroll, unroll))
    with eng.Fori(first // unroll, first // unroll + rounds) as n:
        for r in range(unroll):
            body(Step(n, r, unroll))
    for i in range(first + unroll * rounds, count + lag):
        body(Step(i // unroll, i % unroll, unroll))


def xattn_moe(nc, x, ctx, mask, wqT, wkT, wvT, woT, awT, gwT, columns, bv, bo, experts, out):
    with ExitStack() as stack:
        def sb(name, shape, dt=F32):
            return stack.enter_context(nc.sbuf_tensor(name, shape, dt))

        def sem(name):
            return stack.enter_context(nc.semaphore(name))

        z2_rows = nc.dram_tensor("z2_rows", (TOKENS + P, D), F32).ap()
        acc_rows = nc.dram_tensor("acc_rows", (TOKENS + P, D), F32).ap()
        lists = nc.dram_tensor("lists", (LIST_ROWS, 2), I32).ap()

        psum = stack.enter_context(nc.psum_tensor("psum", [P, 8, 512], F32))
        bank = [psum[:, i, :] for i in range(8)]

        ident = sb("ident", [P, P])
        below = sb("below", [P, P])
        ones = sb("ones", [P, P])
        half_neg = sb("half_neg", [P, 1])
        head_of = sb("head_of", [P, HALF_HEADS])
        row_i = sb("row_i", [P, HALF_HEADS], I32)
        row_f = sb("row_f", [P, HALF_HEADS])
        gw_sb = sb("gw", [P, KD, EXPERTS])
        vecs = sb("vecs", [P, 6, KD])
        bq_c, bk_c, g1_c, b1_c, g2_c, b2_c = range(6)
        bv_sb = sb("bv", [P, D])
        bo_sb = sb("bo", [P, D])


        stats = sb("stats", [P, 2, 6])
        mv = [sb(f"mv{i}", [P, 2, 2]) for i in range(4)]
        var_eps = [sb(f"var_eps{i}", [P, 2]) for i in range(4)]
        rstd = [sb(f"rstd{i}", [P, 2]) for i in range(4)]
        shift = [sb(f"shift{i}", [P, 2]) for i in range(4)]
        rows = sb("rows", [P, GATHERS, D])
        xn = rows[:, 0:2, :]
        xnT = sb("xnT", [P, 2, KD, P])
        s_max = sb("s_max", [P, 2, HEADS])
        o_rec = sb("o_rec", [P, 2, HEADS])
        o_sb = sb("o_sb", [P, 2, D])
        z2 = rows[:, 2:4, :]
        tT = sb("tT", [P, 2, KD, P])

        expert_f = sb("expert_f", [P, EXPERTS])
        list_base = sb("list_base", [P, EXPERTS])
        top = sb("top", [P, 2, 8])
        top_i = sb("top_i", [P, 2, 8], U32)
        top_f = sb("top_f", [P, 2, TOPK])
        hot = sb("hot", [P, 2, TOPK, EXPERTS])
        chosen = sb("chosen", [P, 2, EXPERTS])
        before = sb("before", [P, 2, EXPERTS])
        place = sb("place", [P, 2, EXPERTS])
        picked = sb("picked", [P, 2, TOPK, EXPERTS])
        pos = sb("pos", [P, 2, TOPK], I32)
        tokens = sb("tokens", [P, TILES, TOPK], I32)
        expert_i = sb("expert_i", [P, EXPERTS], I32)
        gap = sb("gap", [P, 2, 1])
        e2 = sb("e2", [P, 2, 1])
        e_sum = sb("e_sum", [P, 2, 1])
        pair = sb("pair", [P, 2, TOPK, 2], I32)
        fill = sb("fill", [P, LIST_COLS, 2], I32)
        zeros = sb("zeros", [P, D])

        J = BLOCKS + 1
        steps_i = sb("steps_i", [1, J], I32)
        steps = sb("steps", [1, J])
        upto = sb("upto", [1, EXPERTS, EXPERTS])
        cnt = sb("cnt", [1, EXPERTS])
        over = sb("over", [1, EXPERTS, TILES])
        nblk = sb("nblk", [1, EXPERTS])
        cum_t = sb("cum_t", [1, EXPERTS, EXPERTS])
        cum = sb("cum", [1, EXPERTS])
        passed = sb("passed", [1, J, EXPERTS])
        passed_n = sb("passed_n", [1, J, EXPERTS])
        e_of = sb("e_of", [1, J])
        b_of = sb("b_of", [1, J])
        r_of = sb("r_of", [1, J])
        first = sb("first", [1, J])
        row_tab = sb("row_tab", [1, J], I32)
        wait_tab = sb("wait_tab", [1, J], I32)
        parity_tab = sb("parity_tab", [1, J], I32)
        next_tab = sb("next_tab", [1, J], I32)
        slot_tab = sb("slot_tab", [1, J], I32)
        first_tab = sb("first_tab", [1, J], I32)

        w_raw = sb("w_raw", [P, 2 * WCOLS])
        blk = sb("blk", [P, BLOCKS, 2], I32)
        zg = rows
        gather_at = sb("gather_at", [P, GATHERS, 1], I32)
        add_at = sb("add_at", [P, 2, 1], I32)
        tbT = xnT
        silu = sb("silu", [P, 2, 512])
        act = sb("act", [P, 2, INTER])
        y = o_sb

        tiles_only = ExitStack()

        def tile_sb(name, shape):
            return tiles_only.enter_context(nc.sbuf_tensor(name, shape, F32))

        x1_sb = tile_sb("x1_sb", [P, TILES, D])
        x_sb = tile_sb("x_sb", [P, TILES, D])
        k_diag = tile_sb("k_diag", [P, BATCH, KD, HALF_HEADS, KEYS])
        ceil_f = tile_sb("ceil_f", [P, TILES, KEYS])
        mask_i = ceil_f[:, :, :].bitcast(I32)
        s_sb = tile_sb("s_sb", [P, 2, SCORES])
        p_sb = tile_sb("p_sb", [P, 2, SCORES])
        pT = tile_sb("pT", [P, 2, CHUNKS, P])
        v_heads = tile_sb("v_heads", [P, BATCH, HEADS, VW])
        v_chunks = tile_sb("v_chunks", [P, CHUNKS, BATCH, CHUNK_SLOTS, VW])
        ctx_sb = tile_sb("ctx_sb", [P, BATCH, D])
        ctxT = tile_sb("ctxT", [P, KD, BATCH, KEYS])
        wq_sb, wk_sb, wv_sb, wo_sb, aw_sb = (tile_sb(n, [P, KD, D]) for n in ("wq", "wk", "wv", "wo", "aw"))
        xf, z, h = (tile_sb(n, [P, 2, D]) for n in ("xf", "z", "h"))
        qT, oT, uT = (tile_sb(n, [P, 2, KD, P]) for n in ("qT", "oT", "uT"))
        tiles_only.close()

        split_w = sb("split_w", [P, 2 * SPLIT], F32R)
        tb_hi = sb("tb_hi", [P, 2, KD, P], F32R)
        tb_lo = sb("tb_lo", [P, 2, KD, P], F32R)
        aT_hi = sb("aT_hi", [P, 2, IC, P], F32R)
        aT_lo = sb("aT_lo", [P, 2, IC, P], F32R)

        x_in = [sem(f"x_in{i}") for i in range(4)]
        ctx_in, mask_in, small_in, wkv_in, wqo_in, aw_in = (
            sem(n) for n in ("ctx_in", "mask_in", "small_in", "wkv_in", "wqo_in", "aw_in"))
        w_in = [sem(f"w_in{i}") for i in range(2)]
        raw_ready = sem("raw_ready")
        w_ready = sem("w_ready")
        dn_hi, gu_hi = sem("dn_hi"), [sem(f"gu_hi{k}") for k in range(KD)]
        consts = sem("consts")
        sel_step, head_step = sem("sel_step"), sem("head_step")
        ctxT_ps, ctxT_done, k_ps, v_ps, k_done, v_done, v_in = (
            sem(n) for n in ("ctxT_ps", "ctxT_done", "k_ps", "v_ps", "k_done", "v_done", "v_in"))
        ceil_step, ceil_done, xb_done = sem("ceil_step"), sem("ceil_done"), sem("xb_done")
        st = [sem(f"st{i}") for i in range(4)]
        var = [sem(f"var{i}") for i in range(4)]
        eps = [sem(f"eps{i}") for i in range(4)]
        rs = [sem(f"rs{i}") for i in range(4)]
        sh = [sem(f"sh{i}") for i in range(4)]
        xn_done, xnT_ps, xnT_done, q_ps, q_done = (
            sem(n) for n in ("xn_done", "xnT_ps", "xnT_done", "q_ps", "q_done"))
        s_ps, s_done, max_done, sub_done, p_done, pT_ps, pT_done = (
            sem(n) for n in ("s_ps", "s_done", "max_done", "sub_done", "p_done", "pT_ps", "pT_done"))
        o_ps, orec_done, o_done, oT_ps, oT_done, wo_ps, x1_done = (
            sem(n) for n in ("o_ps", "orec_done", "o_done", "oT_ps", "oT_done", "wo_ps", "x1_done"))
        xf_done, z_done, uT_ps, uT_done, aw_ps, h_done, z2_done, tT_ps, tT_done, lg_ps = (
            sem(n) for n in ("xf_done", "z_done", "uT_ps", "uT_done", "aw_ps", "h_done", "z2_done",
                             "tT_ps", "tT_done", "lg_ps"))
        acc_done, acc_out = sem("acc_done"), sem("acc_out")
        z2_out = [sem(f"z2_out{i}") for i in range(2)]
        pad_out, fill_done, fill_out = sem("pad_out"), sem("fill_done"), sem("fill_out")
        top_done, topi_done, topf_done, hot_done, chosen_done, before_done, gap_done, e2_done, rank_ps = (
            sem(n) for n in ("top_done", "topi_done", "topf_done", "hot_done", "chosen_done",
                             "before_done", "gap_done", "e2_done", "rank_ps"))
        place_done, picked_done, esum_done, w1_done, pair_done = (
            sem(n) for n in ("place_done", "picked_done", "esum_done", "w1_done", "pair_done"))
        iota_done, router_const = sem("iota_done"), sem("router_const")
        listed = [sem(f"listed{i}") for i in range(2)]
        cnt_ps, tab, tab_done = sem("cnt_ps"), sem("tab"), sem("tab_done")
        blk_in = [sem(f"blk_in{i}") for i in range(GATHERS)]
        zg_in = [sem(f"zg_in{i}") for i in range(GATHERS)]
        tb_ps, tb_done, tbh_done, tbl_done, g_ps, u_ps, silu_done, act_done, aT_ps, aTh_done, aTl_done, y_ps, y_done, added = (
            sem(n) for n in ("tb_ps", "tb_done", "tbh_done", "tbl_done", "g_ps", "u_ps", "silu_done", "act_done",
                             "aT_ps", "aTh_done", "aTl_done", "y_ps", "y_done", "added"))
        split_met = sem("split_met")
        dve_met, pool_met = sem("dve_met"), sem("pool_met")
        at_done, add_at_done, out_done = sem("at_done"), sem("add_at_done"), sem("out_done")

        x_tiles = x.rearrange("b (i p) d -> p i b d", p=P)
        out_tiles = out.rearrange("b (i p) d -> i b p d", p=P)
        z2_tiles = z2_rows[0:TOKENS, :].rearrange("(n b p) d -> n b p d", b=2, p=P)
        acc_tiles = acc_rows[0:TOKENS, :].rearrange("(n b p) d -> n b p d", b=2, p=P)
        x_sb_pairs = x_sb[:, :, :].rearrange("p (i b) d -> p i b d", b=2)
        x1_pairs = x1_sb[:, :, :].rearrange("p (i b) d -> p i b d", b=2)

        def of(tensor, tile):
            return tensor[:, number(tile)]

        def weights(buffer, slot, width, at, cols):
            return buffer[:, bass.ds(slot * width + at, cols)]

        def next_expert(eng, c, split, met=None, before=None):
            first_c = eng.value_load(first_tab[0:1, bass.ds(number(c), 1)], min_val=0, max_val=1)
            expert = eng.value_load(next_tab[0:1, bass.ds(number(c), 1)], min_val=1, max_val=EXPERTS + 1)
            slot = eng.value_load(slot_tab[0:1, bass.ds(number(c), 1)], min_val=0, max_val=1)
            if before is not None:
                before()
            with eng.If(first_c):
                wait_count(eng, y_ps, number(c))
                eng.wait_ge(raw_ready, expert)
                eng.sem_inc(split_met, 1)
                split(slot, expert)

        block = stack.enter_context(nc.Block())

        @block.sync
        def _(sp):
            sp.dma_start(ctx_sb[0:KEYS, :, :], ctx.rearrange("b k d -> k b d")).then_inc(ctx_in, 16)
            for w, src in ((wk_sb, wkT), (wv_sb, wvT)):
                sp.dma_start(w[:, :, :], src.rearrange("(k p) n -> p k n", p=P)).then_inc(wkv_in, 16)
            for i in range(4):
                for b in range(BATCH):
                    sp.dma_start(x_sb_pairs[:, 2 * i:2 * i + 2, b, :], x_tiles[:, 2 * i:2 * i + 2, b, :]).then_inc(x_in[i], 16)
            for w, src in ((wq_sb, wqT), (wo_sb, woT)):
                sp.dma_start(w[:, :, :], src.rearrange("(k p) n -> p k n", p=P)).then_inc(wqo_in, 16)
            sp.dma_start(aw_sb[:, :, :], awT.rearrange("(k p) n -> p k n", p=P)).then_inc(aw_in, 16)
            sp.dma_start(gw_sb[:, :, :], gwT.rearrange("(k p) n -> p k n", p=P)).then_inc(aw_in, 16)
            for e in range(2):
                sp.dma_start(w_raw[:, e * WCOLS:(e + 1) * WCOLS], experts[e]).then_inc(w_in[e], 16)

            sp.wait_ge(fill_done, 1)
            sp.dma_start(lists.rearrange("(p c) k -> p c k", p=P), fill[:, :, :]).then_inc(fill_out, 16)
            sp.dma_start(z2_rows[TOKENS:TOKENS + P, :], zeros[:, :]).then_inc(pad_out, 16)
            sp.dma_start(acc_rows[TOKENS:TOKENS + P, :], zeros[:, :]).then_inc(pad_out, 16)

            for e in range(2):
                sp.wait_ge(w_in[e], 16)
                sp.sem_inc(raw_ready, 1)

            def store(t):
                sp.wait_ge(z2_done, number(t) + 1)
                sp.dma_start(z2_tiles[t[0], t[1]], z2[:, t[1], :]).then_inc(z2_out[t[1]], 16)
                sp.wait_ge(acc_done, number(t) + 1)
                sp.dma_start(acc_tiles[t[0], t[1]], of(x_sb, t)).then_inc(acc_out, 16)

            pipeline(sp, store, TILES, 0, 0)

            for e in range(2, EXPERTS):
                sp.wait_ge(w_ready, PARTS * (e - 1))
                sp.dma_start(w_raw[:, e % 2 * WCOLS:(e % 2 + 1) * WCOLS], experts[e]).then_inc(w_in[e % 2], 16)
                sp.wait_ge(w_in[e % 2], 16 * (e // 2 + 1))
                sp.sem_inc(raw_ready, 1)

            sp.wait_ge(added, 16 * BLOCKS)
            for b in range(BATCH):
                sp.dma_start(out_tiles[:, b], acc_tiles[:, b]).then_inc(out_done, 16)
            sp.wait_ge(out_done, 16 * BATCH)

        @block.gpsimd
        def _(pool):
            nc.gpsimd.memset(ident[:, :], 0.0).then_inc(sel_step, 1)
            nc.gpsimd.memset(below[:, :], 0.0).then_inc(sel_step, 1)
            nc.gpsimd.memset(upto[:, :, :], 1.0).then_inc(sel_step, 1)
            nc.gpsimd.memset(ones[:, :], 1.0).then_inc(consts, 1)
            nc.gpsimd.memset(half_neg[:, :], -0.5).then_inc(consts, 1)
            nc.gpsimd.memset(v_heads[:, :, :, HD:VW], 1.0).then_inc(consts, 1)
            nc.gpsimd.memset(v_chunks[:, :, :, :, :], 0.0).then_inc(consts, 1)
            nc.gpsimd.memset(before[:, 0, :], 0.0).then_inc(consts, 1)
            pool.wait_ge(sel_step, 3)
            nc.gpsimd.affine_select(out=ident[:, :], in_=ident[:, :], compare_op=ALU.not_equal, fill=1.0,
                                    base=0, pattern=[[-1, P]], channel_multiplier=1).then_inc(consts, 1)
            nc.gpsimd.affine_select(out=below[:, :], in_=below[:, :], compare_op=ALU.is_ge, fill=1.0,
                                    base=0, pattern=[[-1, P]], channel_multiplier=1).then_inc(consts, 1)
            nc.gpsimd.affine_select(out=upto[:, :, :], in_=upto[:, :, :], compare_op=ALU.is_ge, fill=0.0,
                                    base=0, pattern=[[1, EXPERTS], [-1, EXPERTS]], channel_multiplier=0).then_inc(consts, 1)
            nc.gpsimd.iota(row_i[:, :], pattern=[[-HD, HALF_HEADS]], base=0, channel_multiplier=1).then_inc(consts, 1)
            nc.gpsimd.iota(expert_i[:, :], pattern=[[1, EXPERTS]], base=0, channel_multiplier=0).then_inc(iota_done, 1)
            nc.gpsimd.iota(steps_i[:, :], pattern=[[1, J]], base=0, channel_multiplier=0).then_inc(iota_done, 1)
            nc.gpsimd.iota(fill[:, :, 0], pattern=[[1, LIST_COLS]], base=0, channel_multiplier=LIST_COLS).then_inc(iota_done, 1)
            nc.gpsimd.iota(tokens[:, :, :], pattern=[[P, TILES], [0, TOPK]], base=0, channel_multiplier=1).then_inc(iota_done, 1)
            nc.gpsimd.memset(fill[:, :, 1], 0).then_inc(iota_done, 1)
            nc.gpsimd.memset(zeros[:, :], 0.0).then_inc(iota_done, 1)

            pool.wait_ge(small_in, 16 * SMALL)
            for i in range(4):
                pool.wait_ge(x_in[i], 32)
                nc.gpsimd.tensor_tensor(x1_sb[:, 4 * i:4 * i + 4, :], x_sb[:, 4 * i:4 * i + 4, :],
                                        bo_sb[:, :].unsqueeze(1).to_broadcast([P, 4, D]), ALU.add).then_inc(xb_done, 1)

            def inverse_root(norm, t, used=None):
                par = t[1]
                if used is not None:
                    wait_count(pool, used, number(t) - 1)
                wait_apart(pool, var[norm], number(t) + 1, pool_met)
                nc.gpsimd.tensor_scalar(var_eps[norm][:, par:par + 1], mv[norm][:, par, 1:2], EPS, None, ALU.add).then_inc(eps[norm], 1)
                pool.wait_ge(eps[norm], number(t) + 1)
                nc.gpsimd.tensor_tensor(rstd[norm][:, par:par + 1], var_eps[norm][:, par:par + 1], half_neg[:, :], ALU.pow).then_inc(rs[norm], 1)

            pool.wait_ge(fill_out, 16)

            def tiles(it):
                t0, t2, t5, t6, t8 = (back(it, lag) for lag in (LN1, QK, LN2, MIX, SCATTER))
                if within(t5, TILES):
                    inverse_root(1, t5)
                if within(t6, TILES):
                    inverse_root(3, t6)
                if within(t8, TILES):
                    par = t8[1]
                    wait_apart(pool, pair_done, number(t8) + 1, pool_met)
                    for k in range(TOPK):
                        nc.gpsimd.indirect_dma_start(
                            lists, bass.IndirectOffsetOnAxis(ap=pos[:, par, k:k + 1], axis=0),
                            pair[:, par, k, :], None, bounds_check=LIST_ROWS - 1).then_inc(listed[par], 16)
                if within(t5, TILES):
                    inverse_root(2, t5, z_done)
                if within(t6, TILES):
                    pool.wait_ge(h_done, number(t6) + 1)
                    nc.gpsimd.tensor_tensor(of(x_sb, t6), of(x1_sb, t6), h[:, t6[1], :], ALU.add).then_inc(acc_done, 1)
                if within(t0, TILES):
                    inverse_root(0, t0, xn_done)
                if within(t2, TILES):
                    par = t2[1]
                    s3 = s_sb[:, par, :].rearrange("p (h k) -> p h k", h=HEADS)
                    for part, (h0, h1) in enumerate(((0, FULL_HEADS), (FULL_HEADS, HEADS))):
                        pool.wait_ge(max_done, 2 * number(t2) + part + 1)
                        nc.gpsimd.tensor_tensor(s3[:, h0:h1, :], s3[:, h0:h1, :],
                                                s_max[:, par, h0:h1].unsqueeze(2).to_broadcast([P, h1 - h0, KEYS]),
                                                ALU.subtract).then_inc(sub_done, 1)

            pipeline(pool, tiles, TILES, SCATTER, SCATTER)

            for par in range(2):
                pool.wait_ge(listed[par], 16 * TOPK * TILES // 2)
                pool.wait_ge(z2_out[par], 16 * TILES // 2)
            pool.wait_ge(pad_out, 32)
            pool.wait_ge(acc_out, 16 * TILES)
            pool.wait_ge(tab_done, 1)

            def split(slot, expert):
                pool.wait_ge(dn_hi, expert)
                nc.gpsimd.tensor_tensor(weights(split_w, slot, SPLIT, WCOLS + GU_COLS, WCOLS - GU_COLS),
                                        weights(w_raw, slot, WCOLS, GU_COLS, WCOLS - GU_COLS),
                                        weights(split_w, slot, SPLIT, GU_COLS, WCOLS - GU_COLS).bitcast(F32), ALU.subtract).then_inc(w_ready, 1)

            def serve(it):
                a, b, s, c = back(it, 0), back(it, 1), back(it, GATHERS + 1), back(it, GATHERS + 2)
                if within(s, BLOCKS):
                    next_expert(pool, s, split)
                if within(a, BLOCKS):
                    row = pool.value_load(row_tab[0:1, bass.ds(number(a), 1)], min_val=0, max_val=LIST_ROWS - P)
                    nc.gpsimd.dma_start(blk[:, number(a)], lists[bass.ds(row, P), :]).then_inc(blk_in[a[1]], 16)
                if within(b, BLOCKS):
                    pool.wait_ge(blk_in[b[1]], 16 * (b[0] + 1))
                    wait_count(pool, tb_ps, number(b) - GATHERS + 1)
                    pool.sem_inc(pool_met, 1)
                    nc.gpsimd.tensor_copy(gather_at[:, b[1], :], blk[:, number(b), 0:1]).then_inc(at_done, 1)
                    wait_apart(pool, at_done, number(b) + 1, pool_met)
                    nc.gpsimd.indirect_dma_start(
                        zg[:, b[1], :], None, z2_rows,
                        bass.IndirectOffsetOnAxis(ap=gather_at[:, b[1], :], axis=0),
                        bounds_check=TOKENS + P - 1).then_inc(zg_in[b[1]], 16)
                if within(c, BLOCKS):
                    pool.wait_ge(y_done, number(c) + 1)
                    wait_count(pool, added, 16 * number(c))
                    pool.sem_inc(pool_met, 1)
                    nc.gpsimd.tensor_copy(add_at[:, c.par, :], blk[:, number(c), 0:1]).then_inc(add_at_done, 1)
                    wait_apart(pool, add_at_done, number(c) + 1, pool_met)
                    nc.gpsimd.indirect_dma_start(
                        acc_rows, bass.IndirectOffsetOnAxis(ap=add_at[:, c.par, :], axis=0),
                        y[:, c.par, :], None, bounds_check=TOKENS + P - 1, compute_op=ALU.add).then_inc(added, 16)

            for i in range(GATHERS):
                serve(Step(0, i, GATHERS))
            pool.wait_ge(raw_ready, 1)
            split(0, 1)
            pipeline(pool, serve, BLOCKS, GATHERS + 2, 2 * GATHERS, GATHERS, GATHERS)

        @block.scalar
        def _(act_e):
            act_e.dma_start(vecs[:, :, :], columns).then_inc(small_in, 16)
            act_e.dma_start(bv_sb[:, :], bv.partition_broadcast(P)).then_inc(small_in, 16)
            act_e.dma_start(bo_sb[:, :], bo.partition_broadcast(P)).then_inc(small_in, 16)
            for b in range(BATCH):
                act_e.dma_start(mask_i.rearrange("p (i b) k -> p i b k", b=2)[:, :, b, :],
                                mask.rearrange("b (i p) k -> p i b k", p=P)[:, :, b, :]).then_inc(mask_in, 16)

            act_e.wait_ge(v_done, 2)
            act_e.wait_ge(consts, CONSTS)
            for c in range(CHUNKS):
                first, n = chunk_heads(c)
                for s in range(first, first + n):
                    k0 = max(0, c * P - s * KEYS)
                    k1 = min(KEYS, (c + 1) * P - s * KEYS)
                    r0 = s * KEYS + k0 - c * P
                    act_e.dma_start(v_chunks[r0:r0 + k1 - k0, c, :, s - first, :],
                                    v_heads[k0:k1, :, s, :]).then_inc(v_in, 16)
            act_e.wait_ge(small_in, 16 * SMALL)

            def tiles(it):
                t0, t1, t2, t3, t4, t5, t6, t7 = (back(it, lag) for lag in (LN1, XT, QK, PV, PROJ, LN2, MIX, LIST))

                def weights_out(r):
                    c0 = 4 * r
                    n = min(4, CHUNKS - c0)
                    act_e.wait_ge(pT_ps, PT_ROUNDS * number(t3) + r + 1)
                    nc.scalar.activation(pT[:, t3[1], c0:c0 + n, :], bank[4 + r % 2][:, 0:n * P], ACT.Copy).then_inc(pT_done, 1)

                def norm_apply(norm, dst, src, t, done):
                    act_e.wait_ge(sh[norm], number(t) + 1)
                    nc.scalar.activation(dst, src, ACT.Identity, bias=shift[norm][:, t[1]:t[1] + 1],
                                         scale=rstd[norm][:, t[1]:t[1] + 1]).then_inc(done, 1)

                if within(t2, TILES):
                    act_e.wait_ge(q_ps, number(t2) + 1)
                    for m in range(KD):
                        nc.scalar.activation(qT[:, t2[1], m, :], bank[6][:, m * P:(m + 1) * P], ACT.Identity,
                                             bias=vecs[:, bq_c, m:m + 1]).then_inc(q_done, 1)
                if within(t3, TILES):
                    weights_out(0)
                    weights_out(1)
                if within(t7, TILES):
                    act_e.wait_ge(gap_done, number(t7) + 1)
                    nc.scalar.activation(e2[:, t7[1], :], gap[:, t7[1], :], ACT.Exp).then_inc(e2_done, 1)
                if within(t4, TILES):
                    act_e.wait_ge(oT_ps, number(t4) + 1)
                    nc.scalar.activation(oT[:, t4[1], :, :], bank[7][:, 0:D], ACT.Copy).then_inc(oT_done, 1)
                if within(t1, TILES):
                    act_e.wait_ge(xnT_ps, number(t1) + 1)
                    nc.scalar.activation(xnT[:, t1[1], :, :], bank[6][:, 0:D], ACT.Copy).then_inc(xnT_done, 1)
                if within(t3, TILES):
                    weights_out(2)
                if within(t6, TILES):
                    act_e.wait_ge(tT_ps, number(t6) + 1)
                    for k in range(KD):
                        nc.scalar.activation(tT[:, t6[1], k, :], bank[3][:, k * P:(k + 1) * P], ACT.Identity,
                                             bias=vecs[:, b2_c, k:k + 1], scale=vecs[:, g2_c, k:k + 1]).then_inc(tT_done, 1)
                if within(t5, TILES):
                    norm_apply(2, z[:, t5[1], :], xf[:, t5[1], :], t5, z_done)
                    act_e.wait_ge(uT_ps, number(t5) + 1)
                    for k in range(KD):
                        nc.scalar.activation(uT[:, t5[1], k, :], bank[5][:, k * P:(k + 1) * P], ACT.Identity,
                                             bias=vecs[:, b1_c, k:k + 1], scale=vecs[:, g1_c, k:k + 1]).then_inc(uT_done, 1)
                if within(t0, TILES):
                    norm_apply(0, xn[:, t0[1], :], of(x_sb, t0), t0, xn_done)
                if within(t2, TILES):
                    for part, (c0, c1) in enumerate(((0, FULL_HEADS * KEYS), (FULL_HEADS * KEYS, SCORES))):
                        act_e.wait_ge(sub_done, 2 * number(t2) + part + 1)
                        nc.scalar.activation(p_sb[:, t2[1], c0:c1], s_sb[:, t2[1], c0:c1], ACT.Exp, scale=SCALE).then_inc(p_done, 1)

            pipeline(act_e, tiles, TILES, LIST, SCATTER)

            def split(slot, expert):
                for k in range(KD):
                    at, cols = k * 2 * INTER, 2 * INTER
                    nc.scalar.activation(weights(split_w, slot, SPLIT, at, cols),
                                         weights(w_raw, slot, WCOLS, at, cols), ACT.Copy).then_inc(gu_hi[k], 1)

            act_e.wait_ge(acc_out, 16 * TILES)
            act_e.wait_ge(raw_ready, 1)
            split(0, 1)

            def experts_(it):
                a, b, c = back(it, 0), back(it, 1), back(it, 2)
                if within(c, BLOCKS):
                    next_expert(act_e, c, split)
                if within(b, BLOCKS):
                    act_e.wait_ge(g_ps, 2 * number(b) + 1)
                    wait_count(act_e, act_done, 2 * number(b) - 1)
                    nc.scalar.activation(silu[:, 0, :], bank[0], ACT.Silu).then_inc(silu_done, 1)
                if within(c, BLOCKS):
                    for half in range(2):
                        act_e.wait_ge(aT_ps, 2 * number(c) + half + 1)
                        nc.scalar.activation(aT_hi[:, c.par, 4 * half:4 * half + 4, :], bank[4 + half], ACT.Copy).then_inc(aTh_done, 1)
                if within(b, BLOCKS):
                    act_e.wait_ge(g_ps, 2 * number(b) + 2)
                    wait_count(act_e, act_done, 2 * number(b))
                    nc.scalar.activation(silu[:, 1, :], bank[2], ACT.Silu).then_inc(silu_done, 1)
                if within(a, BLOCKS):
                    act_e.wait_ge(tb_ps, number(a) + 1)
                    wait_count(act_e, tbl_done, number(a) - 1)
                    for k in range(KD):
                        nc.scalar.activation(tbT[:, a.par, k, :], bank[6][:, k * P:(k + 1) * P], ACT.Identity,
                                             bias=vecs[:, b2_c, k:k + 1], scale=vecs[:, g2_c, k:k + 1]).then_inc(tb_done, 1)

            pipeline(act_e, experts_, BLOCKS, 2, 4, GATHERS)

        @block.vector
        def _(dve):
            dve.wait_ge(ctxT_ps, 1)
            nc.vector.tensor_copy(ctxT[:, :, :, :], bank[0][:, 0:KD * BATCH * KEYS]).then_inc(ctxT_done, 1)
            dve.wait_ge(small_in, 16 * SMALL)
            dve.wait_ge(consts, CONSTS)
            dve.wait_ge(v_ps, 1)
            for b in range(BATCH):
                nc.vector.tensor_tensor(v_heads[0:KEYS, b, :, 0:HD],
                                        bank[2 + b][0:KEYS, 0:D].rearrange("p (h d) -> p h d", h=HEADS),
                                        bv_sb[0:KEYS, :].rearrange("p (h d) -> p h d", h=HEADS), ALU.add).then_inc(v_done, 1)
            nc.vector.tensor_copy(row_f[:, :], row_i[:, :]).then_inc(head_step, 1)
            dve.wait_ge(head_step, 1)
            nc.vector.tensor_scalar(head_of[:, :], row_f[:, :], float(HD), None, ALU.is_lt).then_inc(head_step, 1)
            nc.vector.tensor_scalar(row_f[:, :], row_f[:, :], 0.0, None, ALU.is_ge).then_inc(head_step, 1)
            dve.wait_ge(head_step, 3)
            nc.vector.tensor_tensor(head_of[:, :], head_of[:, :], row_f[:, :], ALU.mult).then_inc(head_step, 1)
            dve.wait_ge(head_step, 4)
            dve.wait_ge(k_ps, 1)
            for m in range(KD):
                for q in range(HALF_HEADS):
                    nc.vector.tensor_scalar(k_diag[:, :, m, q, :],
                                            bank[1][:, m * BATCH * KEYS:(m + 1) * BATCH * KEYS].rearrange("p (b k) -> p b k", b=BATCH),
                                            vecs[:, bk_c, m:m + 1], head_of[:, q:q + 1], ALU.add, ALU.mult).then_inc(k_done, 1)
            dve.wait_ge(mask_in, 32)
            nc.vector.tensor_scalar(ceil_f[:, :, :], mask_i, 0.0, 3e38, ALU.not_equal, ALU.mult).then_inc(ceil_step, 1)
            dve.wait_ge(ceil_step, 1)
            nc.vector.tensor_scalar(ceil_f[:, :, :], ceil_f[:, :, :], NEG / SCALE, None, ALU.add).then_inc(ceil_step, 1)
            dve.wait_ge(ceil_step, 2)
            dve.wait_ge(iota_done, 6)
            nc.vector.tensor_scalar(fill[:, :, 0], fill[:, :, 0], P - 1, TOKENS, ALU.bitwise_and, ALU.bitwise_or).then_inc(fill_done, 1)
            nc.vector.tensor_copy(expert_f[:, :], expert_i[:, :]).then_inc(router_const, 1)
            nc.vector.tensor_copy(steps[:, :], steps_i[:, :]).then_inc(router_const, 1)
            dve.wait_ge(router_const, 2)
            nc.vector.tensor_scalar(list_base[:, :], expert_f[:, :], float(TOKENS), None, ALU.mult).then_inc(router_const, 1)

            for i in range(4):
                dve.wait_ge(x_in[i], 32)

            def norm_stats(norm, src, t):
                nc.vector.bn_stats(stats[:, t[1], :], src).then_inc(st[norm], 1)

            def norm_moments(norm, t):
                wait_apart(dve, st[norm], number(t) + 1, dve_met)
                nc.vector.bn_aggr(mv[norm][:, t[1], :], stats[:, t[1], :]).then_inc(var[norm], 1)

            def norm_shift(norm, t):
                par = t[1]
                dve.wait_ge(rs[norm], number(t) + 1)
                nc.vector.tensor_scalar(shift[norm][:, par:par + 1], mv[norm][:, par, 0:1], rstd[norm][:, par:par + 1], -1.0,
                                        ALU.mult, ALU.mult).then_inc(sh[norm], 1)

            def norm_apply(norm, dst, src, t, done):
                dve.wait_ge(rs[norm], number(t) + 1)
                nc.vector.tensor_scalar(dst, src, mv[norm][:, t[1], 0:1], rstd[norm][:, t[1]:t[1] + 1],
                                        ALU.subtract, ALU.mult).then_inc(done, 1)

            for i in range(4):
                dve.wait_ge(xb_done, i + 1)

            def tiles(it):
                t0, t2, t4, t5, t6, t7 = (back(it, lag) for lag in (LN1, QK, PROJ, LN2, MIX, LIST))
                if within(t5, TILES):
                    dve.wait_ge(wo_ps, number(t5) + 1)
                    nc.vector.tensor_tensor(of(x1_sb, t5), bank[7][:, 0:D], of(x1_sb, t5), ALU.add).then_inc(x1_done, 1)
                if within(t6, TILES):
                    dve.wait_ge(aw_ps, number(t6) + 1)
                    wait_count(dve, acc_done, number(t6) - 1)
                    nc.vector.tensor_tensor(h[:, t6[1], :], bank[5][:, 0:D], xf[:, t6[1], :], ALU.add).then_inc(h_done, 1)
                if within(t5, TILES):
                    wait_apart(dve, x1_done, number(t5) + 1, dve_met)
                    norm_stats(1, of(x1_sb, t5), t5)
                if within(t6, TILES):
                    dve.wait_ge(h_done, number(t6) + 1)
                    norm_stats(3, h[:, t6[1], :], t6)
                if within(t5, TILES):
                    norm_moments(1, t5)
                if within(t6, TILES):
                    norm_moments(3, t6)
                if within(t7, TILES):
                    par, n = t7[1], number(t7) + 1
                    logits = bank[3][:, LOGITS_AT:LOGITS_AT + EXPERTS]
                    if within(t4, TILES):
                        dve.wait_ge(o_ps, number(t4) + 1)
                    wait_apart(dve, lg_ps, n, dve_met)
                    nc.vector.max(top[:, par, :], logits).then_inc(top_done, 1)
                    wait_apart(dve, top_done, n, dve_met)
                    nc.vector.max_index(top_i[:, par, :], top[:, par, :], logits).then_inc(topi_done, 1)
                    nc.vector.tensor_tensor(gap[:, par, :], top[:, par, 1:2], top[:, par, 0:1], ALU.subtract).then_inc(gap_done, 1)
                    dve.wait_ge(topi_done, n)
                    nc.vector.tensor_copy(top_f[:, par, :], top_i[:, par, 0:TOPK]).then_inc(topf_done, 1)
                if within(t4, TILES):
                    par = t4[1]
                    dve.wait_ge(o_ps, number(t4) + 1)
                    o3 = bank[3][:, 0:HEADS * VW].rearrange("p (h v) -> p h v", h=HEADS)
                    nc.vector.reciprocal(o_rec[:, par, :], o3[:, :, HD]).then_inc(orec_done, 1)
                if within(t7, TILES):
                    dve.wait_ge(topf_done, n)
                    nc.vector.tensor_tensor(hot[:, t7[1], :, :], expert_f[:, :].unsqueeze(1).to_broadcast([P, TOPK, EXPERTS]),
                                            top_f[:, t7[1], :].unsqueeze(2).to_broadcast([P, TOPK, EXPERTS]), ALU.is_equal).then_inc(hot_done, 1)
                if within(t4, TILES):
                    dve.wait_ge(orec_done, number(t4) + 1)
                    nc.vector.tensor_tensor(o_sb[:, t4[1], :].rearrange("p (h d) -> p h d", h=HEADS), o3[:, :, 0:HD],
                                            o_rec[:, t4[1], :].unsqueeze(2).to_broadcast([P, HEADS, HD]), ALU.mult).then_inc(o_done, 1)
                if within(t7, TILES):
                    dve.wait_ge(hot_done, n)
                    nc.vector.tensor_tensor(chosen[:, t7[1], :], hot[:, t7[1], 0, :], hot[:, t7[1], 1, :], ALU.add).then_inc(chosen_done, 1)
                if within(t5, TILES):
                    norm_apply(1, xf[:, t5[1], :], of(x1_sb, t5), t5, xf_done)
                if within(t6, TILES):
                    wait_count(dve, z2_out[t6[1]], 16 * t6[0])
                    norm_apply(3, z2[:, t6[1], :], h[:, t6[1], :], t6, z2_done)
                if within(t5, TILES):
                    dve.wait_ge(xf_done, number(t5) + 1)
                    norm_stats(2, xf[:, t5[1], :], t5)
                if within(t7, TILES):
                    dve.wait_ge(chosen_done, n)
                    nc.vector.tensor_tensor(before[:, 1 - t7[1], :], before[:, t7[1], :], chosen[:, t7[1], :], ALU.add).then_inc(before_done, 1)
                if within(t5, TILES):
                    norm_moments(2, t5)
                if within(t0, TILES):
                    norm_stats(0, of(x_sb, t0), t0)
                    norm_moments(0, t0)

                def scores_out(part):
                    s3 = s_sb[:, t2[1], :].rearrange("p (h k) -> p h k", h=HEADS)
                    if part == 0:
                        nc.vector.tensor_tensor(
                            s3[:, 0:FULL_HEADS, :].rearrange("p (g s) k -> p g s k", g=FULL_BANKS),
                            psum[:, 0:FULL_BANKS, 0:BANK_HEADS * KEYS].rearrange("p g (s k) -> p g s k", s=BANK_HEADS),
                            of(ceil_f, t2).unsqueeze(1).unsqueeze(1).to_broadcast([P, FULL_BANKS, BANK_HEADS, KEYS]), ALU.min).then_inc(s_done, 1)
                    else:
                        rest = HEADS - FULL_HEADS
                        nc.vector.tensor_tensor(
                            s3[:, FULL_HEADS:HEADS, :], psum[:, FULL_BANKS, 0:rest * KEYS].rearrange("p (s k) -> p s k", s=rest),
                            of(ceil_f, t2).unsqueeze(1).to_broadcast([P, rest, KEYS]), ALU.min).then_inc(s_done, 1)

                def maxima(part):
                    h0, h1 = ((0, FULL_HEADS), (FULL_HEADS, HEADS))[part]
                    s3 = s_sb[:, t2[1], :].rearrange("p (h k) -> p h k", h=HEADS)
                    dve.wait_ge(s_done, 2 * number(t2) + part + 1)
                    nc.vector.reduce_max(s_max[:, t2[1], h0:h1], s3[:, h0:h1, :], AX_X).then_inc(max_done, 1)

                if within(t2, TILES):
                    dve.wait_ge(s_ps, 2 * number(t2) + 1)
                    wait_count(dve, p_done, 2 * number(t2) - 2)
                    scores_out(0)
                if within(t5, TILES):
                    norm_shift(2, t5)
                if within(t2, TILES):
                    maxima(0)
                if within(t0, TILES):
                    norm_shift(0, t0)
                if within(t2, TILES):
                    dve.wait_ge(s_ps, 2 * number(t2) + 2)
                    if within(t7, TILES):
                        dve.wait_ge(rank_ps, n)
                    scores_out(1)
                if within(t7, TILES):
                    par = t7[1]
                    dve.wait_ge(rank_ps, n)
                    nc.vector.tensor_tensor(place[:, par, :], bank[FULL_BANKS][:, RANKS_AT:RANKS_AT + EXPERTS], list_base[:, :], ALU.add).then_inc(place_done, 1)
                    dve.wait_ge(e2_done, n)
                    nc.vector.tensor_scalar(e_sum[:, par, :], e2[:, par, :], 1.0, None, ALU.add).then_inc(esum_done, 1)
                if within(t2, TILES):
                    maxima(1)
                if within(t7, TILES):
                    dve.wait_ge(place_done, n)
                    nc.vector.tensor_tensor(picked[:, par, :, :], hot[:, par, :, :],
                                            place[:, par, :].unsqueeze(1).to_broadcast([P, TOPK, EXPERTS]), ALU.mult).then_inc(picked_done, 1)
                    wait_count(dve, listed[par], 16 * TOPK * t7[0])
                    weight = pair[:, par, :, :].bitcast(F32)
                    dve.wait_ge(esum_done, n)
                    nc.vector.reciprocal(weight[:, 0, 1:2], e_sum[:, par, :]).then_inc(w1_done, 1)
                    dve.wait_ge(picked_done, n)
                    with nc.allow_low_precision(reason="one of eight is not 0: a whole number under 2^24"):
                        nc.vector.tensor_reduce(pos[:, par, :], picked[:, par, :, :], AX_X, ALU.add)
                    nc.vector.tensor_copy(pair[:, par, :, 0], of(tokens, t7))
                    dve.wait_ge(w1_done, n)
                    nc.vector.tensor_tensor(weight[:, 1, 1:2], weight[:, 0, 1:2], e2[:, par, :], ALU.mult).then_inc(pair_done, 1)

            pipeline(dve, tiles, TILES, LIST, SCATTER + 2)

            steps_done = [0]

            def step(instruction):
                steps_done[0] += 1
                instruction.then_inc(tab, 1)
                dve.wait_ge(tab, steps_done[0])

            dve.wait_ge(cnt_ps, 1)
            step(nc.vector.tensor_copy(cnt[:, :], bank[0][0:1, 0:EXPERTS]))
            step(nc.vector.tensor_scalar(over[0:1, 0, :], steps[0:1, 0:TILES], float(P), None, ALU.mult))
            step(nc.vector.tensor_tensor(passed_n[0:1, 0:TILES, :], cnt[:, :].unsqueeze(1).to_broadcast([1, TILES, EXPERTS]),
                                         over[0:1, 0, :].unsqueeze(2).to_broadcast([1, TILES, EXPERTS]), ALU.is_gt))
            step(nc.vector.tensor_reduce(nblk[:, :], passed_n[0:1, 0:TILES, :].rearrange("o t e -> o e t"), AX_X, ALU.add))
            step(nc.vector.tensor_scalar(nblk[:, :], nblk[:, :], 1.0, None, ALU.max))
            step(nc.vector.tensor_tensor(cum_t[:, :, :], upto[:, :, :], nblk[:, :].unsqueeze(1).to_broadcast([1, EXPERTS, EXPERTS]), ALU.mult))
            step(nc.vector.tensor_reduce(cum[:, :], cum_t[:, :, :], AX_X, ALU.add))
            step(nc.vector.tensor_tensor(passed[:, :, :], steps[:, :].unsqueeze(2).to_broadcast([1, J, EXPERTS]),
                                         cum[:, :].unsqueeze(1).to_broadcast([1, J, EXPERTS]), ALU.is_ge))
            step(nc.vector.tensor_tensor(passed_n[:, :, :], passed[:, :, :], nblk[:, :].unsqueeze(1).to_broadcast([1, J, EXPERTS]), ALU.mult))
            step(nc.vector.tensor_reduce(e_of[:, :], passed[:, :, :], AX_X, ALU.add))
            step(nc.vector.tensor_reduce(b_of[:, :], passed_n[:, :, :], AX_X, ALU.add))
            step(nc.vector.scalar_tensor_tensor(r_of[:, :], e_of[:, :], float(TOKENS // P), steps[:, :], ALU.mult, ALU.add))
            step(nc.vector.tensor_tensor(r_of[:, :], r_of[:, :], b_of[:, :], ALU.subtract))
            step(nc.vector.tensor_scalar(row_tab[:, :], r_of[:, :], float(P), None, ALU.mult))
            step(nc.vector.tensor_scalar(e_of[:, :], e_of[:, :], float(EXPERTS - 1), None, ALU.min))
            step(nc.vector.tensor_scalar(wait_tab[:, :], e_of[:, :], 1.0, float(PARTS), ALU.add, ALU.mult))
            step(nc.vector.tensor_scalar(next_tab[:, :], e_of[:, :], 2.0, None, ALU.add))
            step(nc.vector.tensor_tensor(first[:, :], b_of[:, :], steps[:, :], ALU.is_equal))
            step(nc.vector.scalar_tensor_tensor(first_tab[:, :], e_of[:, :], float(EXPERTS - 1), first[:, :], ALU.is_lt, ALU.mult))
            step(nc.vector.tensor_copy(parity_tab[:, :], e_of[:, :]))
            step(nc.vector.tensor_scalar(slot_tab[:, :], next_tab[:, :], 1, 1, ALU.bitwise_and, ALU.bitwise_xor))
            nc.vector.tensor_scalar(parity_tab[:, :], parity_tab[:, :], 1, None, ALU.bitwise_and).then_inc(tab_done, 1)

            def split(slot, expert):
                nc.vector.tensor_copy(weights(split_w, slot, SPLIT, GU_COLS, WCOLS - GU_COLS),
                                      weights(w_raw, slot, WCOLS, GU_COLS, WCOLS - GU_COLS)).then_inc(dn_hi, 1)
                for k in range(KD):
                    at, cols = k * 2 * INTER, 2 * INTER
                    dve.wait_ge(gu_hi[k], expert)
                    nc.vector.tensor_tensor(weights(split_w, slot, SPLIT, WCOLS + at, cols),
                                            weights(w_raw, slot, WCOLS, at, cols),
                                            weights(split_w, slot, SPLIT, at, cols).bitcast(F32), ALU.subtract).then_inc(w_ready, 1)

            dve.wait_ge(acc_out, 16 * TILES)
            dve.wait_ge(raw_ready, 1)
            split(0, 1)

            def experts_(it):
                a, b, c, d = (back(it, lag) for lag in range(4))

                def weighted():
                    if within(d, BLOCKS):
                        dve.wait_ge(y_ps, number(d) + 1)
                        wait_count(dve, added, 16 * (number(d) - 1))
                        nc.vector.tensor_scalar(y[:, d.par, :], bank[7][:, 0:D], blk[:, number(d), 1:2].bitcast(F32), None, ALU.mult).then_inc(y_done, 1)

                if within(c, BLOCKS):
                    next_expert(dve, c, split, before=weighted)
                else:
                    weighted()
                if within(c, BLOCKS):
                    for half in range(2):
                        dve.wait_ge(aTh_done, 2 * number(c) + half + 1)
                        nc.vector.tensor_tensor(aT_lo[:, c.par, 4 * half:4 * half + 4, :], bank[4 + half].rearrange("p (i t) -> p i t", i=4),
                                                aT_hi[:, c.par, 4 * half:4 * half + 4, :].bitcast(F32), ALU.subtract).then_inc(aTl_done, 1)
                if within(b, BLOCKS):
                    for half in range(2):
                        dve.wait_ge(silu_done, 2 * number(b) + half + 1)
                        dve.wait_ge(u_ps, 2 * number(b) + half + 1)
                        nc.vector.tensor_tensor(act[:, b.par, half * 512:half * 512 + 512], bank[1 + 2 * half], silu[:, half, :], ALU.mult).then_inc(act_done, 1)
                if within(a, BLOCKS):
                    n = number(a)
                    dve.wait_ge(tb_done, KD * n + KD)
                    nc.vector.tensor_copy(tb_hi[:, a.par, :, :], tbT[:, a.par, :, :]).then_inc(tbh_done, 1)
                    dve.wait_ge(tbh_done, n + 1)
                    nc.vector.tensor_tensor(tb_lo[:, a.par, :, :], tbT[:, a.par, :, :], tb_hi[:, a.par, :, :].bitcast(F32), ALU.subtract).then_inc(tbl_done, 1)

            pipeline(dve, experts_, BLOCKS, 3, 4, GATHERS)

        @block.tensor
        def _(pe):
            pe.wait_ge(consts, CONSTS)
            pe.wait_ge(ctx_in, 16)
            for k in range(KD):
                for b in range(BATCH):
                    at = (k * BATCH + b) * KEYS
                    last = nc.tensor.transpose(bank[0][:, at:at + KEYS], ctx_sb[0:KEYS, b, k * P:(k + 1) * P], ident[0:KEYS, 0:KEYS])
            last.then_inc(ctxT_ps, 1)
            pe.wait_ge(wkv_in, 32)
            pe.wait_ge(ctxT_done, 1)
            for b in range(BATCH):
                for k in range(KD):
                    last = nc.tensor.matmul(bank[2 + b][0:KEYS, 0:D], ctxT[:, k, b, :], wv_sb[:, k, :], start=k == 0, stop=k == KD - 1)
            last.then_inc(v_ps, 1)
            for m in range(2):
                for k in range(KD):
                    last = nc.tensor.matmul(bank[1][:, m * BATCH * KEYS:(m + 1) * BATCH * KEYS], wk_sb[:, k, m * P:(m + 1) * P],
                                            ctxT[:, k, :, :].rearrange("p b k -> p (b k)"), start=k == 0, stop=k == KD - 1)
            last.then_inc(k_ps, 1)
            pe.wait_ge(wqo_in, 32)
            pe.wait_ge(k_done, HEADS)
            pe.wait_ge(v_done, 2)
            pe.wait_ge(aw_in, 32)

            def tiles(it):
                t1, t2, t3, t4, t5, t6, t7 = (back(it, lag) for lag in (XT, QK, PV, PROJ, LN2, MIX, LIST))

                def transposed(dst, src):
                    for k in range(KD):
                        done = nc.tensor.transpose(dst[:, k * P:(k + 1) * P], src[:, k * P:(k + 1) * P], ident[:, :])
                    return done

                def row_product(dst, rows_T, w):
                    for k in range(KD):
                        done = nc.tensor.matmul(dst, rows_T[:, k, :], w[:, k, :], start=k == 0, stop=k == KD - 1)
                    return done

                def weights_T(r):
                    for c in range(4 * r, min(4 * r + 4, CHUNKS)):
                        w = min(P, SCORES - c * P)
                        done = nc.tensor.transpose(bank[4 + r % 2][0:w, (c - 4 * r) * P:(c - 4 * r + 1) * P],
                                                   p_sb[:, t3[1], c * P:c * P + w], ident[:, :])
                    return done

                if within(t2, TILES):
                    pe.wait_ge(xnT_done, number(t2) + 1)
                    for m in range(KD):
                        for k in range(KD):
                            last = nc.tensor.matmul(bank[6][:, m * P:(m + 1) * P], wq_sb[:, k, m * P:(m + 1) * P],
                                                    xnT[:, t2[1], k, :], start=k == 0, stop=k == KD - 1)
                    last.then_inc(q_ps, 1)
                if within(t3, TILES):
                    pe.wait_ge(p_done, 2 * number(t3) + 2)
                    wait_count(pe, pT_done, PT_ROUNDS * number(t3))
                    weights_T(0).then_inc(pT_ps, 1)
                if within(t2, TILES):
                    n, par = number(t2), t2[1]
                    pe.wait_ge(q_done, KD * (n + 1))
                    wait_count(pe, s_done, 2 * n)
                    if within(t7, TILES):
                        wait_count(pe, place_done, number(t7))
                    for g in range(-(-HEADS // BANK_HEADS)):
                        for m in range(KD):
                            h0 = max(g * BANK_HEADS, m * HALF_HEADS)
                            h1 = min((g + 1) * BANK_HEADS, (m + 1) * HALF_HEADS, HEADS)
                            if h0 < h1:
                                last = nc.tensor.matmul(
                                    bank[g][:, (h0 - g * BANK_HEADS) * KEYS:(h1 - g * BANK_HEADS) * KEYS], qT[:, par, m, :],
                                    k_diag[:, par, m, h0 - m * HALF_HEADS:h1 - m * HALF_HEADS, :].rearrange("p q k -> p (q k)"),
                                    start=True, stop=True)
                        if g >= FULL_BANKS - 1:
                            last.then_inc(s_ps, 1)
                if within(t3, TILES):
                    if within(t6, TILES):
                        pe.wait_ge(h_done, number(t6) + 1)
                    weights_T(1).then_inc(pT_ps, 1)
                if within(t4, TILES):
                    pe.wait_ge(o_done, number(t4) + 1)
                    wait_count(pe, x1_done, number(t4))
                    transposed(bank[7], o_sb[:, t4[1], :]).then_inc(oT_ps, 1)
                if within(t7, TILES):
                    par = t7[1]
                    pe.wait_ge(chosen_done, number(t7) + 1)
                    ranks = bank[FULL_BANKS][:, RANKS_AT:RANKS_AT + EXPERTS]
                    if not within(t2, TILES):
                        wait_count(pe, place_done, number(t7))
                        pe.wait_ge(s_done, 2 * TILES)
                    nc.tensor.matmul(ranks, below[:, :], chosen[:, par, :], start=True, stop=False)
                    nc.tensor.matmul(ranks, ones[:, :], before[:, par, :], start=False, stop=True).then_inc(rank_ps, 1)
                if within(t1, TILES):
                    pe.wait_ge(xn_done, number(t1) + 1)
                    transposed(bank[6], xn[:, t1[1], :]).then_inc(xnT_ps, 1)
                if within(t3, TILES):
                    pe.wait_ge(pT_done, PT_ROUNDS * number(t3) + 1)
                    weights_T(2).then_inc(pT_ps, 1)
                if within(t6, TILES):
                    pe.wait_ge(z2_done, number(t6) + 1)
                    if within(t7, TILES):
                        pe.wait_ge(topi_done, number(t7) + 1)
                    transposed(bank[3], z2[:, t6[1], :]).then_inc(tT_ps, 1)
                if within(t4, TILES):
                    pe.wait_ge(oT_done, number(t4) + 1)
                    row_product(bank[7][:, 0:D], oT[:, t4[1], :, :], wo_sb).then_inc(wo_ps, 1)
                if within(t5, TILES):
                    pe.wait_ge(z_done, number(t5) + 1)
                    wait_count(pe, h_done, number(t5))
                    if within(t3, TILES):
                        pe.wait_ge(pT_done, PT_ROUNDS * number(t3) + 2)
                    transposed(bank[5], z[:, t5[1], :]).then_inc(uT_ps, 1)
                if within(t6, TILES):
                    pe.wait_ge(tT_done, KD * (number(t6) + 1))
                    row_product(bank[3][:, LOGITS_AT:LOGITS_AT + EXPERTS], tT[:, t6[1], :, :], gw_sb).then_inc(lg_ps, 1)
                if within(t3, TILES):
                    n, par = number(t3), t3[1]
                    if isinstance(n, int) and n == 0:
                        pe.wait_ge(v_in, 16 * sum(chunk_heads(c)[1] for c in range(CHUNKS)))
                    pe.wait_ge(pT_done, PT_ROUNDS * (n + 1))
                    for c in range(CHUNKS):
                        w = min(P, SCORES - c * P)
                        first, heads = chunk_heads(c)
                        last = nc.tensor.matmul(bank[3][:, first * VW:(first + heads) * VW], pT[0:w, par, c, :],
                                                v_chunks[0:w, c, par, 0:heads, :].rearrange("p s v -> p (s v)"),
                                                start=c == 0, stop=c == CHUNKS - 1, skip_group_check=True)
                    last.then_inc(o_ps, 1)
                if within(t5, TILES):
                    pe.wait_ge(uT_done, KD * (number(t5) + 1))
                    row_product(bank[5][:, 0:D], uT[:, t5[1], :, :], aw_sb).then_inc(aw_ps, 1)

            pipeline(pe, tiles, TILES, LIST, SCATTER)

            pe.wait_ge(s_done, 2 * TILES)
            pe.wait_ge(before_done, TILES)
            nc.tensor.matmul(bank[0][:, 0:EXPERTS], ones[:, :], before[:, 0, :], start=True, stop=True).then_inc(cnt_ps, 1)
            pe.wait_ge(place_done, TILES)
            pe.wait_ge(tab_done, 1)

            def three_products(dst, hi, lo, parity, at, cols, first, last):
                w_hi = weights(split_w, parity, SPLIT, at, cols)
                w_lo = weights(split_w, parity, SPLIT, WCOLS + at, cols)
                nc.tensor.matmul(dst, hi, w_hi, start=first, stop=False)
                nc.tensor.matmul(dst, hi, w_lo, start=False, stop=False)
                return nc.tensor.matmul(dst, lo, w_hi, start=False, stop=last)

            def gate_up(half, b, parity):
                par, n = b.par, number(b)
                for which, sem_ in ((0, g_ps), (1, u_ps)):
                    wait_count(pe, silu_done if which == 0 else act_done, 2 * n - 1 + half)
                    for k in range(KD):
                        last = three_products(bank[2 * half + which], tb_hi[:, par, k, :], tb_lo[:, par, k, :], parity,
                                              (2 * k + which) * INTER + half * 512, 512, k == 0, k == KD - 1)
                    last.then_inc(sem_, 1)

            def experts_(it):
                a, b, c = back(it, 0), back(it, 1), back(it, 2)
                if within(b, BLOCKS):
                    ready = pe.value_load(wait_tab[0:1, bass.ds(number(b), 1)], min_val=1, max_val=PARTS * EXPERTS)
                    parity = pe.value_load(parity_tab[0:1, bass.ds(number(b), 1)], min_val=0, max_val=1)
                    pe.wait_ge(w_ready, ready)
                    pe.wait_ge(tbl_done, number(b) + 1)
                    gate_up(0, b, parity)
                if within(c, BLOCKS):
                    par, n = c.par, number(c)
                    for half in range(2):
                        pe.wait_ge(act_done, 2 * n + half + 1)
                        wait_count(pe, aTl_done, 2 * n - 1 + half)
                        for i in range(4):
                            at = half * 512 + i * P
                            last = nc.tensor.transpose(bank[4 + half][:, i * P:(i + 1) * P], act[:, par, at:at + P], ident[:, :])
                        last.then_inc(aT_ps, 1)
                if within(b, BLOCKS):
                    gate_up(1, b, parity)
                if within(a, BLOCKS):
                    pe.wait_ge(zg_in[a[1]], 16 * (a[0] + 1))
                    wait_count(pe, tb_done, 2 * number(a))
                    for k in range(KD):
                        last = nc.tensor.transpose(bank[6][:, k * P:(k + 1) * P], zg[:, a[1], k * P:(k + 1) * P], ident[:, :])
                    last.then_inc(tb_ps, 1)
                if within(c, BLOCKS):
                    parity_c = pe.value_load(parity_tab[0:1, bass.ds(number(c), 1)], min_val=0, max_val=1)
                    wait_count(pe, y_done, n)
                    for i in range(IC):
                        if i % 4 == 0:
                            pe.wait_ge(aTl_done, 2 * n + i // 4 + 1)
                        last = three_products(bank[7][:, 0:D], aT_hi[:, par, i, :], aT_lo[:, par, i, :], parity_c,
                                              GU_COLS + i * D, D, i == 0, i == IC - 1)
                    last.then_inc(y_ps, 1)

            pipeline(pe, experts_, BLOCKS, 2, 4, GATHERS)


_INS = ["x", "ctx", "mask", "wqT", "wkT", "wvT", "woT", "awT", "gwT", "columns", "bv", "bo", "experts"]


def kernel(**inputs):
    import numpy as np
    import concourse.bacc as bacc
    from concourse.bass_utils import run_bass_kernel_spmd

    a = {k: np.asarray(v) for k, v in inputs.items()}
    per_column = ["L0_xattn_bq", "L0_xattn_bk", "L0_ffn_ln1_g", "L0_ffn_ln1_b", "L0_ffn_ln2_g", "L0_ffn_ln2_b"]
    gate_up = np.stack([a["L0_ffn_gate_proj"], a["L0_ffn_up_proj"]], axis=1)
    gate_up = gate_up.reshape(EXPERTS, 2, INTER, KD, P).transpose(0, 4, 3, 1, 2).reshape(EXPERTS, P, KD * 2 * INTER)
    down = a["L0_ffn_down_proj"].reshape(EXPERTS, D, IC, P).transpose(0, 3, 2, 1).reshape(EXPERTS, P, IC * D)
    laid = {
        "x": a["x"], "ctx": a["ctx_1024"], "mask": a["mask_BxSxS2_ik0"],
        "wqT": a["L0_xattn_Wq"].T, "wkT": a["L0_xattn_Wk"].T, "wvT": a["L0_xattn_Wv"].T,
        "woT": a["L0_xattn_Wo"].T, "awT": a["L0_ffn_attn_w"].T, "gwT": a["L0_ffn_gate_w"].T,
        "columns": np.stack([a[n].reshape(KD, P).T for n in per_column], axis=1),
        "bv": a["L0_xattn_bv"], "bo": a["L0_xattn_bo"],
        "experts": np.concatenate([gate_up, down], axis=2),
    }
    nc = bacc.Bacc("TRN2", target_bir_lowering=False, num_devices=1)
    arrays, args = {}, []
    for name in _INS:
        v = np.ascontiguousarray(laid[name])
        arrays[f"in_{name}"] = v
        args.append(nc.dram_tensor(f"in_{name}", v.shape, mybir.dt.from_np(v.dtype), kind="ExternalInput").ap())
    result = nc.dram_tensor("out_x", (BATCH, SEQ, D), F32, kind="ExternalOutput").ap()
    xattn_moe(nc, *args, result)
    r = run_bass_kernel_spmd(nc, [arrays], core_ids=[0])
    return r.results[0]["out_x"]
```

```python
from contextlib import ExitStack

import concourse.bass as bass
from concourse import mybir

F32 = mybir.dt.float32
F32R = mybir.dt.float32r
BF16 = mybir.dt.bfloat16
I32 = mybir.dt.int32
U32 = mybir.dt.uint32
ALU = mybir.AluOpType
ACT = mybir.ActivationFunctionType
AX_X = mybir.AxisListType.X

P = 128
BATCH, SEQ, D, KEYS = 2, 1024, 256, 77
HEADS, HD = 16, 16
KD = D // P
TOKENS = BATCH * SEQ
TILES = TOKENS // P
HALF_HEADS = HEADS // KD
BANK_HEADS = 512 // KEYS
SCORES = HEADS * KEYS
FULL_BANKS = HEADS // BANK_HEADS
FULL_HEADS = FULL_BANKS * BANK_HEADS
RANKS_AT = (HEADS - FULL_HEADS) * KEYS
CHUNKS = -(-SCORES // P)
LOGITS_AT = HEADS * (HD + 1)
VW = HD + 1
EXPERTS, INTER, TOPK = 8, 1024, 2
IC = INTER // P
FULL_BLOCKS = TOKENS * TOPK // P
BLOCKS = FULL_BLOCKS + EXPERTS - 1
USUAL_BLOCKS = FULL_BLOCKS + EXPERTS // 2
SPARE = EXPERTS - 1
LIST_ROWS = EXPERTS * TOKENS + SPARE * P
LIST_COLS = LIST_ROWS // P
WCOLS = KD * 2 * INTER + IC * D
GU_COLS = KD * 2 * INTER
SPLIT = 2 * WCOLS
GATHERS = 4
PARTS = KD + 1
EPS = 1e-5
NEG = -1e9
SCALE = 1.0 / HD ** 0.5


def chunk_heads(c):
    width = min(P, SCORES - c * P)
    first = c * P // KEYS
    return first, (c * P + width - 1) // KEYS - first + 1


def slot_rows():
    import numpy as np
    head = (np.arange(CHUNKS)[None, :] * P + np.arange(P)[:, None]) // KEYS
    first = np.array([chunk_heads(c)[0] for c in range(CHUNKS)])
    return (head[:, :, None] == first[None, :, None] + np.arange(CHUNK_SLOTS)).astype(np.float32)


PT_ROUNDS = -(-CHUNKS // 4)
SMALL, CONSTS = 4, 8
CHUNK_SLOTS = max(chunk_heads(c)[1] for c in range(CHUNKS))


class Step(tuple):
    def __new__(cls, n, r, unroll):
        step = super().__new__(cls, (n, r))
        step.unroll = unroll
        return step

    @property
    def par(self):
        return self[1] % 2


def back(it, lag):
    d = it[1] - lag
    return Step(it[0] + d // it.unroll, d % it.unroll, it.unroll)


def number(step):
    return step.unroll * step[0] + step[1]


LN1, XT, QK, PV, PROJ, LN2, MIX, LIST, SCATTER = range(9)


def within(tile, count):
    t = number(tile)
    return not isinstance(t, int) or 0 <= t < count


def wait_count(eng, sem, count):
    if not isinstance(count, int) or count > 0:
        eng.wait_ge(sem, count)


def wait_apart(eng, sem, count, met):
    eng.wait_ge(sem, count)
    eng.sem_inc(met, 1)


def pipeline(eng, body, count, lag, first, unroll=2, begin=0):
    rounds = (count - first) // unroll
    for i in range(begin, first):
        body(Step(i // unroll, i % unroll, unroll))
    with eng.Fori(first // unroll, first // unroll + rounds) as n:
        for r in range(unroll):
            body(Step(n, r, unroll))
    for i in range(first + unroll * rounds, count + lag):
        body(Step(i // unroll, i % unroll, unroll))


def xattn_moe(nc, x, ctx, mask, wqT, wkT, wvT, woT, awT, gwT, columns, bv, bo, slot_rows, experts, out):
    with ExitStack() as stack:
        def sb(name, shape, dt=F32):
            return stack.enter_context(nc.sbuf_tensor(name, shape, dt))

        def sem(name):
            return stack.enter_context(nc.semaphore(name))

        z2_rows = nc.dram_tensor("z2_rows", (TOKENS + P, D), F32).ap()
        acc_rows = nc.dram_tensor("acc_rows", (TOKENS + P, D), F32).ap()
        v_rows = nc.dram_tensor("v_rows", (SCORES, BATCH * VW), F32).ap()
        lists = nc.dram_tensor("lists", (LIST_ROWS, 2), I32).ap()

        psum = stack.enter_context(nc.psum_tensor("psum", [P, 8, 512], F32))
        bank = [psum[:, i, :] for i in range(8)]

        ident = sb("ident", [P, P])
        below = sb("below", [P, P], BF16)
        ones = sb("ones", [P, P], BF16)
        half_neg = sb("half_neg", [P, 1])
        head_of = sb("head_of", [P, HALF_HEADS])
        row_i = sb("row_i", [P, HALF_HEADS], I32)
        row_f = sb("row_f", [P, HALF_HEADS])
        gw_sb = sb("gw", [P, KD, EXPERTS])
        vecs = sb("vecs", [P, 6, KD])
        bq_c, bk_c, g1_c, b1_c, g2_c, b2_c = range(6)
        bv_sb = sb("bv", [P, D])
        bo_sb = sb("bo", [P, D])


        stats = sb("stats", [P, 2, 6])
        mv = [sb(f"mv{i}", [P, 2, 2]) for i in range(4)]
        var_eps = [sb(f"var_eps{i}", [P, 2]) for i in range(4)]
        rstd = [sb(f"rstd{i}", [P, 2]) for i in range(4)]
        shift = [sb(f"shift{i}", [P, 2]) for i in range(4)]
        rows = sb("rows", [P, GATHERS, D])
        xn = rows[:, 0:2, :]
        xnT = sb("xnT", [P, 2, KD, P])
        s_max = sb("s_max", [P, 2, HEADS])
        o_rec = sb("o_rec", [P, 2, HEADS])
        o_sb = sb("o_sb", [P, 2, D])
        z2 = rows[:, 2:4, :]
        tT = sb("tT", [P, 2, KD, P])

        expert_f = sb("expert_f", [P, EXPERTS])
        list_base = sb("list_base", [P, EXPERTS])
        top = sb("top", [P, 2, 8])
        top_i = sb("top_i", [P, 2, 8], U32)
        top_f = sb("top_f", [P, 2, TOPK])
        hot = sb("hot", [P, 2, TOPK, EXPERTS])
        chosen = sb("chosen", [P, 2, EXPERTS], BF16)
        before = sb("before", [P, 2, EXPERTS], BF16)
        place = sb("place", [P, 2, EXPERTS])
        picked = sb("picked", [P, 2, TOPK, EXPERTS])
        pos = sb("pos", [P, 2, TOPK], I32)
        tokens = sb("tokens", [P, TILES, TOPK], I32)
        expert_i = sb("expert_i", [P, EXPERTS], I32)
        gap = sb("gap", [P, 2, 1])
        e2 = sb("e2", [P, 2, 1])
        e_sum = sb("e_sum", [P, 2, 1])
        pair = sb("pair", [P, 2, TOPK, 2], I32)
        fill = sb("fill", [P, LIST_COLS, 2], I32)
        zeros = sb("zeros", [P, D])

        J = BLOCKS + 1
        steps_i = sb("steps_i", [1, J], I32)
        steps = sb("steps", [1, J])
        upto = sb("upto", [1, EXPERTS, EXPERTS])
        cnt = sb("cnt", [1, EXPERTS])
        over = sb("over", [1, EXPERTS, TILES])
        nblk = sb("nblk", [1, EXPERTS])
        cum_t = sb("cum_t", [1, EXPERTS, EXPERTS])
        cum = sb("cum", [1, EXPERTS])
        passed = sb("passed", [1, J, EXPERTS])
        passed_n = sb("passed_n", [1, J, EXPERTS])
        e_of = sb("e_of", [1, J])
        b_of = sb("b_of", [1, J])
        r_of = sb("r_of", [1, J])
        first = sb("first", [1, J])
        row_tab = sb("row_tab", [1, J], I32)
        wait_tab = sb("wait_tab", [1, J], I32)
        parity_tab = sb("parity_tab", [1, J], I32)
        next_tab = sb("next_tab", [1, J], I32)
        slot_tab = sb("slot_tab", [1, J], I32)
        first_tab = sb("first_tab", [1, J], I32)
        rush_tab = sb("rush_tab", [1, J], I32)
        present_tab = sb("present_tab", [1, J], I32)
        added_tab = sb("added_tab", [1, 1], I32)

        w_raw = sb("w_raw", [P, 2 * WCOLS])
        blk = sb("blk", [P, BLOCKS, 2], I32)
        zg = rows
        gather_at = sb("gather_at", [P, GATHERS, 1], I32)
        add_at = sb("add_at", [P, 2, 1], I32)
        tbT = xnT
        silu = sb("silu", [P, 2, 512])
        act = sb("act", [P, 2, INTER])
        y = o_sb

        tiles_only = ExitStack()

        def tile_sb(name, shape):
            return tiles_only.enter_context(nc.sbuf_tensor(name, shape, F32))

        x1_sb = tile_sb("x1_sb", [P, TILES, D])
        x_sb = tile_sb("x_sb", [P, TILES, D])
        k_diag = tile_sb("k_diag", [P, BATCH, KD, HALF_HEADS, KEYS])
        ceil_f = tile_sb("ceil_f", [P, TILES, KEYS])
        mask_i = ceil_f[:, :, :].bitcast(I32)
        s_sb = tile_sb("s_sb", [P, 2, SCORES])
        p_sb = tile_sb("p_sb", [P, 2, SCORES])
        pT = tile_sb("pT", [P, 2, CHUNKS, P])
        v_heads = tile_sb("v_heads", [P, HEADS, BATCH, VW])
        v_flat = tile_sb("v_flat", [P, CHUNKS, BATCH, VW])
        slots = tile_sb("slots", [P, CHUNKS, CHUNK_SLOTS])
        v_chunks = tile_sb("v_chunks", [P, CHUNKS, BATCH, CHUNK_SLOTS, VW])
        ctx_sb = tile_sb("ctx_sb", [P, BATCH, D])
        ctxT = tile_sb("ctxT", [P, KD, BATCH, KEYS])
        wq_sb, wk_sb, wv_sb, wo_sb, aw_sb = (tile_sb(n, [P, KD, D]) for n in ("wq", "wk", "wv", "wo", "aw"))
        xf, z, h = (tile_sb(n, [P, 2, D]) for n in ("xf", "z", "h"))
        qT, oT, uT = (tile_sb(n, [P, 2, KD, P]) for n in ("qT", "oT", "uT"))
        tiles_only.close()

        split_w = sb("split_w", [P, 2 * SPLIT], F32R)
        tb_hi = sb("tb_hi", [P, 2, KD, P], F32R)
        tb_lo = sb("tb_lo", [P, 2, KD, P], F32R)
        aT_hi = sb("aT_hi", [P, 2, IC, P], F32R)
        aT_lo = sb("aT_lo", [P, 2, IC, P], F32R)

        x_in = [sem(f"x_in{i}") for i in range(4)]
        ctx_in, mask_in, small_in, wkv_in, wqo_in, aw_in = (
            sem(n) for n in ("ctx_in", "mask_in", "small_in", "wkv_in", "wqo_in", "aw_in"))
        w_in = [sem(f"w_in{i}") for i in range(2)]
        raw_ready = sem("raw_ready")
        w_ready = sem("w_ready")
        dn_hi, gu_hi = sem("dn_hi"), [sem(f"gu_hi{k}") for k in range(KD)]
        consts = sem("consts")
        sel_step, head_step = sem("sel_step"), sem("head_step")
        ctxT_ps, ctxT_done, k_ps, v_ps, k_done, v_done, v_out, v_in, v_split = (
            sem(n) for n in ("ctxT_ps", "ctxT_done", "k_ps", "v_ps", "k_done", "v_done", "v_out", "v_in", "v_split"))
        ceil_step, ceil_done, xb_done = sem("ceil_step"), sem("ceil_done"), sem("xb_done")
        st = [sem(f"st{i}") for i in range(4)]
        var = [sem(f"var{i}") for i in range(4)]
        eps = [sem(f"eps{i}") for i in range(4)]
        rs = [sem(f"rs{i}") for i in range(4)]
        sh = [sem(f"sh{i}") for i in range(4)]
        xn_done, xnT_ps, xnT_done, q_ps, q_done = (
            sem(n) for n in ("xn_done", "xnT_ps", "xnT_done", "q_ps", "q_done"))
        s_ps, s_done, max_done, sub_done, p_done, pT_ps, pT_done = (
            sem(n) for n in ("s_ps", "s_done", "max_done", "sub_done", "p_done", "pT_ps", "pT_done"))
        o_ps, orec_done, o_done, oT_ps, oT_done, wo_ps, x1_done = (
            sem(n) for n in ("o_ps", "orec_done", "o_done", "oT_ps", "oT_done", "wo_ps", "x1_done"))
        xf_done, z_done, uT_ps, uT_done, aw_ps, h_done, z2_done, tT_ps, tT_done, lg_ps = (
            sem(n) for n in ("xf_done", "z_done", "uT_ps", "uT_done", "aw_ps", "h_done", "z2_done",
                             "tT_ps", "tT_done", "lg_ps"))
        acc_done, acc_out = sem("acc_done"), sem("acc_out")
        z2_out = [sem(f"z2_out{i}") for i in range(2)]
        pad_out, fill_done, fill_out = sem("pad_out"), sem("fill_done"), sem("fill_out")
        top_done, topi_done, topf_done, hot_done, chosen_done, before_done, gap_done, e2_done, rank_ps = (
            sem(n) for n in ("top_done", "topi_done", "topf_done", "hot_done", "chosen_done",
                             "before_done", "gap_done", "e2_done", "rank_ps"))
        place_done, picked_done, esum_done, w1_done, pair_done = (
            sem(n) for n in ("place_done", "picked_done", "esum_done", "w1_done", "pair_done"))
        iota_done, router_const = sem("iota_done"), sem("router_const")
        listed = [sem(f"listed{i}") for i in range(2)]
        cnt_ps, tab, tab_done = sem("cnt_ps"), sem("tab"), sem("tab_done")
        blk_in = [sem(f"blk_in{i}") for i in range(GATHERS)]
        zg_in = [sem(f"zg_in{i}") for i in range(GATHERS)]
        tb_ps, tb_done, tbh_done, tbl_done, g_ps, u_ps, silu_done, act_done, aT_ps, aTh_done, aTl_done, y_ps, y_done, added = (
            sem(n) for n in ("tb_ps", "tb_done", "tbh_done", "tbl_done", "g_ps", "u_ps", "silu_done", "act_done",
                             "aT_ps", "aTh_done", "aTl_done", "y_ps", "y_done", "added"))
        split_met = sem("split_met")
        dve_met, pool_met = sem("dve_met"), sem("pool_met")
        at_done, add_at_done, out_done = sem("at_done"), sem("add_at_done"), sem("out_done")

        x_tiles = x.rearrange("b (i p) d -> p i b d", p=P)
        out_tiles = out.rearrange("b (i p) d -> i b p d", p=P)
        z2_tiles = z2_rows[0:TOKENS, :].rearrange("(n b p) d -> n b p d", b=2, p=P)
        acc_tiles = acc_rows[0:TOKENS, :].rearrange("(n b p) d -> n b p d", b=2, p=P)
        x_sb_pairs = x_sb[:, :, :].rearrange("p (i b) d -> p i b d", b=2)
        x1_pairs = x1_sb[:, :, :].rearrange("p (i b) d -> p i b d", b=2)

        def of(tensor, tile):
            return tensor[:, number(tile)]

        def weights(buffer, slot, width, at, cols):
            return buffer[:, bass.ds(slot * width + at, cols)]

        def member(only):
            return lambda b: number(b) == only if only is not None else within(b, USUAL_BLOCKS)

        def blocks_behind(eng, body, lag):
            for j in range(USUAL_BLOCKS, BLOCKS):
                with eng.If(eng.value_load(present_tab[0:1, j:j + 1], min_val=0, max_val=1)):
                    for i in range(j, j + lag + 1):
                        body(Step(i // GATHERS, i % GATHERS, GATHERS), j)

        def entry(eng, table, b, low, high):
            return eng.value_load(table[0:1, bass.ds(number(b), 1)], min_val=low, max_val=high)

        def next_expert(eng, c, split, expert=None, slot=None):
            if expert is None:
                expert, slot = entry(eng, next_tab, c, 1, EXPERTS + 1), entry(eng, slot_tab, c, 0, 1)
            wait_count(eng, y_ps, number(c))
            eng.wait_ge(raw_ready, expert)
            eng.sem_inc(split_met, 1)
            split(slot, expert)

        block = stack.enter_context(nc.Block())

        @block.sync
        def _(sp):
            sp.dma_start(ctx_sb[0:KEYS, :, :], ctx.rearrange("b k d -> k b d")).then_inc(ctx_in, 16)

            def load_x(i):
                for b in range(BATCH):
                    sp.dma_start(x_sb_pairs[:, 2 * i:2 * i + 2, b, :], x_tiles[:, 2 * i:2 * i + 2, b, :]).then_inc(x_in[i], 16)

            load_x(0)
            for w, src, done in ((wv_sb, wvT, wkv_in), (wk_sb, wkT, wkv_in), (wq_sb, wqT, wqo_in)):
                sp.dma_start(w[:, :, :], src.rearrange("(k p) n -> p k n", p=P)).then_inc(done, 16)
            load_x(1)
            for w, src, done in ((wo_sb, woT, wqo_in), (aw_sb, awT, aw_in), (gw_sb, gwT, aw_in)):
                sp.dma_start(w[:, :, :], src.rearrange("(k p) n -> p k n", p=P)).then_inc(done, 16)

            sp.wait_ge(v_done, BATCH)
            sp.dma_start(v_rows.rearrange("(h k) v -> k h v", k=KEYS),
                         v_heads[0:KEYS, :, :, :].rearrange("k h b v -> k h (b v)")).then_inc(v_out, 16)
            load_x(2)
            load_x(3)
            sp.wait_ge(v_out, 16)
            last = CHUNKS - 1
            sp.dma_start(v_flat[:, 0:last, :, :].rearrange("p c b v -> p c (b v)"),
                         v_rows[0:last * P, :].rearrange("(c p) v -> p c v", p=P)).then_inc(v_in, 16)
            sp.dma_start(v_flat[0:SCORES - last * P, last, :, :].rearrange("p b v -> p (b v)"), v_rows[last * P:SCORES, :]).then_inc(v_in, 16)

            sp.wait_ge(fill_done, 1)
            sp.dma_start(lists.rearrange("(p c) k -> p c k", p=P), fill[:, :, :]).then_inc(fill_out, 16)
            sp.dma_start(z2_rows[TOKENS:TOKENS + P, :], zeros[:, :]).then_inc(pad_out, 16)
            sp.dma_start(acc_rows[TOKENS:TOKENS + P, :], zeros[:, :]).then_inc(pad_out, 16)

            sp.wait_ge(v_in, 32)
            for e in range(2):
                sp.dma_start(w_raw[:, e * WCOLS:(e + 1) * WCOLS], experts[e]).then_inc(w_in[e], 16)

            def store(t):
                sp.wait_ge(z2_done, number(t) + 1)
                sp.dma_start(z2_tiles[t[0], t[1]], z2[:, t[1], :]).then_inc(z2_out[t[1]], 16)
                sp.wait_ge(acc_done, number(t) + 1)
                sp.dma_start(acc_tiles[t[0], t[1]], of(x_sb, t)).then_inc(acc_out, 16)

            pipeline(sp, store, TILES, 0, 0)

            for e in range(2):
                sp.wait_ge(w_in[e], 16)
                sp.sem_inc(raw_ready, 1)
            for e in range(2, EXPERTS):
                sp.wait_ge(w_ready, PARTS * (e - 1))
                sp.dma_start(w_raw[:, e % 2 * WCOLS:(e % 2 + 1) * WCOLS], experts[e]).then_inc(w_in[e % 2], 16)
                sp.wait_ge(w_in[e % 2], 16 * (e // 2 + 1))
                sp.sem_inc(raw_ready, 1)

            every = sp.value_load(added_tab[0:1, 0:1], min_val=16 * USUAL_BLOCKS, max_val=16 * BLOCKS)
            sp.wait_ge(added, every)
            for b in range(BATCH):
                sp.dma_start(out_tiles[:, b], acc_tiles[:, b]).then_inc(out_done, 16)
            sp.wait_ge(out_done, 16 * BATCH)

        @block.gpsimd
        def _(pool):
            nc.gpsimd.memset(ident[:, :], 0.0).then_inc(sel_step, 1)
            nc.gpsimd.memset(below[:, :], 0.0).then_inc(sel_step, 1)
            nc.gpsimd.memset(upto[:, :, :], 1.0).then_inc(sel_step, 1)
            nc.gpsimd.memset(ones[:, :], 1.0).then_inc(consts, 1)
            nc.gpsimd.memset(half_neg[:, :], -0.5).then_inc(consts, 1)
            nc.gpsimd.memset(v_heads[:, :, :, HD:VW], 1.0).then_inc(consts, 1)
            nc.gpsimd.memset(before[:, 0, :], 0.0).then_inc(consts, 1)
            pool.wait_ge(sel_step, 3)
            nc.gpsimd.affine_select(out=ident[:, :], in_=ident[:, :], compare_op=ALU.not_equal, fill=1.0,
                                    base=0, pattern=[[-1, P]], channel_multiplier=1).then_inc(consts, 1)
            nc.gpsimd.affine_select(out=below[:, :], in_=below[:, :], compare_op=ALU.is_ge, fill=1.0,
                                    base=0, pattern=[[-1, P]], channel_multiplier=1).then_inc(consts, 1)
            nc.gpsimd.affine_select(out=upto[:, :, :], in_=upto[:, :, :], compare_op=ALU.is_ge, fill=0.0,
                                    base=0, pattern=[[1, EXPERTS], [-1, EXPERTS]], channel_multiplier=0).then_inc(consts, 1)
            nc.gpsimd.iota(row_i[:, :], pattern=[[-HD, HALF_HEADS]], base=0, channel_multiplier=1).then_inc(consts, 1)
            nc.gpsimd.iota(expert_i[:, :], pattern=[[1, EXPERTS]], base=0, channel_multiplier=0).then_inc(iota_done, 1)
            nc.gpsimd.iota(steps_i[:, :], pattern=[[1, J]], base=0, channel_multiplier=0).then_inc(iota_done, 1)
            nc.gpsimd.iota(fill[:, :, 0], pattern=[[1, LIST_COLS]], base=0, channel_multiplier=LIST_COLS).then_inc(iota_done, 1)
            nc.gpsimd.iota(tokens[:, :, :], pattern=[[P, TILES], [0, TOPK]], base=0, channel_multiplier=1).then_inc(iota_done, 1)
            nc.gpsimd.memset(fill[:, :, 1], 0).then_inc(iota_done, 1)
            nc.gpsimd.memset(zeros[:, :], 0.0).then_inc(iota_done, 1)

            def add_bias(i):
                pool.wait_ge(x_in[i], 32)
                nc.gpsimd.tensor_tensor(x1_sb[:, 4 * i:4 * i + 4, :], x_sb[:, 4 * i:4 * i + 4, :],
                                        bo_sb[:, :].unsqueeze(1).to_broadcast([P, 4, D]), ALU.add).then_inc(xb_done, 1)

            pool.wait_ge(small_in, 16 * SMALL)

            def inverse_root(norm, t, used=None):
                par = t[1]
                if used is not None:
                    wait_count(pool, used, number(t) - 1)
                wait_apart(pool, var[norm], number(t) + 1, pool_met)
                nc.gpsimd.tensor_scalar(var_eps[norm][:, par:par + 1], mv[norm][:, par, 1:2], EPS, None, ALU.add).then_inc(eps[norm], 1)
                pool.wait_ge(eps[norm], number(t) + 1)
                nc.gpsimd.tensor_tensor(rstd[norm][:, par:par + 1], var_eps[norm][:, par:par + 1], half_neg[:, :], ALU.pow).then_inc(rs[norm], 1)

            def tiles(it):
                t0, t2, t5, t6, t8 = (back(it, lag) for lag in (LN1, QK, LN2, MIX, SCATTER))
                if within(t0, TILES):
                    inverse_root(0, t0, xn_done)
                    if isinstance(number(t0), int) and number(t0) < 4:
                        add_bias(number(t0))
                    if isinstance(number(t0), int) and number(t0) == SCATTER - 1:
                        pool.wait_ge(fill_out, 16)
                if within(t5, TILES):
                    inverse_root(1, t5)
                if within(t6, TILES):
                    inverse_root(3, t6)
                if within(t5, TILES):
                    inverse_root(2, t5, z_done)
                if within(t8, TILES):
                    par = t8[1]
                    wait_apart(pool, pair_done, number(t8) + 1, pool_met)
                    for k in range(TOPK):
                        nc.gpsimd.indirect_dma_start(
                            lists, bass.IndirectOffsetOnAxis(ap=pos[:, par, k:k + 1], axis=0),
                            pair[:, par, k, :], None, bounds_check=LIST_ROWS - 1).then_inc(listed[par], 16)
                if within(t6, TILES):
                    pool.wait_ge(h_done, number(t6) + 1)
                    nc.gpsimd.tensor_tensor(of(x_sb, t6), of(x1_sb, t6), h[:, t6[1], :], ALU.add).then_inc(acc_done, 1)
                if within(t2, TILES):
                    par = t2[1]
                    s3 = s_sb[:, par, :].rearrange("p (h k) -> p h k", h=HEADS)
                    for part, (h0, h1) in enumerate(((0, FULL_HEADS), (FULL_HEADS, HEADS))):
                        pool.wait_ge(max_done, 2 * number(t2) + part + 1)
                        nc.gpsimd.tensor_tensor(s3[:, h0:h1, :], s3[:, h0:h1, :],
                                                s_max[:, par, h0:h1].unsqueeze(2).to_broadcast([P, h1 - h0, KEYS]),
                                                ALU.subtract).then_inc(sub_done, 1)

            pipeline(pool, tiles, TILES, SCATTER, SCATTER)

            def split(slot, expert):
                pool.wait_ge(dn_hi, expert)
                nc.gpsimd.tensor_tensor(weights(split_w, slot, SPLIT, WCOLS + GU_COLS, WCOLS - GU_COLS),
                                        weights(w_raw, slot, WCOLS, GU_COLS, WCOLS - GU_COLS),
                                        weights(split_w, slot, SPLIT, GU_COLS, WCOLS - GU_COLS).bitcast(F32), ALU.subtract).then_inc(w_ready, 1)

            split(0, 1)

            for par in range(2):
                pool.wait_ge(listed[par], 16 * TOPK * TILES // 2)
                pool.wait_ge(z2_out[par], 16 * TILES // 2)
            pool.wait_ge(pad_out, 32)
            pool.wait_ge(acc_out, 16 * TILES)
            pool.wait_ge(tab_done, 1)

            def serve(it, only=None):
                has = member(only)
                a, b, s, c = back(it, 0), back(it, 1), back(it, GATHERS + 1), back(it, GATHERS + 2)
                if has(s):
                    with pool.If(entry(pool, first_tab, s, 0, 1)):
                        next_expert(pool, s, split)
                if has(a):
                    row = pool.value_load(row_tab[0:1, bass.ds(number(a), 1)], min_val=0, max_val=LIST_ROWS - P)
                    nc.gpsimd.dma_start(blk[:, number(a)], lists[bass.ds(row, P), :]).then_inc(blk_in[a[1]], 16)
                if has(b):
                    pool.wait_ge(blk_in[b[1]], 16 * (b[0] + 1))
                    wait_count(pool, tb_ps, number(b) - GATHERS + 1)
                    pool.sem_inc(pool_met, 1)
                    nc.gpsimd.tensor_copy(gather_at[:, b[1], :], blk[:, number(b), 0:1]).then_inc(at_done, 1)
                    wait_apart(pool, at_done, number(b) + 1, pool_met)
                    nc.gpsimd.indirect_dma_start(
                        zg[:, b[1], :], None, z2_rows,
                        bass.IndirectOffsetOnAxis(ap=gather_at[:, b[1], :], axis=0),
                        bounds_check=TOKENS + P - 1).then_inc(zg_in[b[1]], 16)
                if has(c):
                    pool.wait_ge(y_done, number(c) + 1)
                    wait_count(pool, added, 16 * number(c))
                    pool.sem_inc(pool_met, 1)
                    nc.gpsimd.tensor_copy(add_at[:, c.par, :], blk[:, number(c), 0:1]).then_inc(add_at_done, 1)
                    wait_apart(pool, add_at_done, number(c) + 1, pool_met)
                    nc.gpsimd.indirect_dma_start(
                        acc_rows, bass.IndirectOffsetOnAxis(ap=add_at[:, c.par, :], axis=0),
                        y[:, c.par, :], None, bounds_check=TOKENS + P - 1, compute_op=ALU.add).then_inc(added, 16)

            for i in range(GATHERS):
                serve(Step(0, i, GATHERS))
            pipeline(pool, serve, USUAL_BLOCKS, GATHERS + 2, 2 * GATHERS, GATHERS, GATHERS)
            blocks_behind(pool, serve, GATHERS + 2)

        @block.scalar
        def _(act_e):
            act_e.dma_start(vecs[:, :, :], columns).then_inc(small_in, 16)
            act_e.dma_start(bv_sb[:, :], bv.partition_broadcast(P)).then_inc(small_in, 16)
            act_e.dma_start(bo_sb[:, :], bo.partition_broadcast(P)).then_inc(small_in, 16)
            act_e.dma_start(slots[:, :, :], slot_rows).then_inc(small_in, 16)
            for b in range(BATCH):
                act_e.dma_start(mask_i.rearrange("p (i b) k -> p i b k", b=2)[:, :, b, :],
                                mask.rearrange("b (i p) k -> p i b k", p=P)[:, :, b, :]).then_inc(mask_in, 16)

            act_e.wait_ge(small_in, 16 * SMALL)

            def tiles(it):
                t0, t1, t2, t3, t4, t5, t6, t7 = (back(it, lag) for lag in (LN1, XT, QK, PV, PROJ, LN2, MIX, LIST))

                def weights_out(r):
                    c0 = 4 * r
                    n = min(4, CHUNKS - c0)
                    act_e.wait_ge(pT_ps, PT_ROUNDS * number(t3) + r + 1)
                    nc.scalar.activation(pT[:, t3[1], c0:c0 + n, :], bank[4 + r % 2][:, 0:n * P], ACT.Copy).then_inc(pT_done, 1)

                def norm_apply(norm, dst, src, t, done):
                    act_e.wait_ge(sh[norm], number(t) + 1)
                    nc.scalar.activation(dst, src, ACT.Identity, bias=shift[norm][:, t[1]:t[1] + 1],
                                         scale=rstd[norm][:, t[1]:t[1] + 1]).then_inc(done, 1)

                if within(t2, TILES):
                    act_e.wait_ge(q_ps, number(t2) + 1)
                    for m in range(KD):
                        nc.scalar.activation(qT[:, t2[1], m, :], bank[6][:, m * P:(m + 1) * P], ACT.Identity,
                                             bias=vecs[:, bq_c, m:m + 1]).then_inc(q_done, 1)
                if within(t3, TILES):
                    weights_out(0)
                    weights_out(1)
                if within(t7, TILES):
                    act_e.wait_ge(gap_done, number(t7) + 1)
                    nc.scalar.activation(e2[:, t7[1], :], gap[:, t7[1], :], ACT.Exp).then_inc(e2_done, 1)
                if within(t4, TILES):
                    act_e.wait_ge(oT_ps, number(t4) + 1)
                    nc.scalar.activation(oT[:, t4[1], :, :], bank[7][:, 0:D], ACT.Copy).then_inc(oT_done, 1)
                if within(t1, TILES):
                    act_e.wait_ge(xnT_ps, number(t1) + 1)
                    nc.scalar.activation(xnT[:, t1[1], :, :], bank[6][:, 0:D], ACT.Copy).then_inc(xnT_done, 1)
                if within(t3, TILES):
                    weights_out(2)
                if within(t6, TILES):
                    act_e.wait_ge(tT_ps, number(t6) + 1)
                    for k in range(KD):
                        nc.scalar.activation(tT[:, t6[1], k, :], bank[3][:, k * P:(k + 1) * P], ACT.Identity,
                                             bias=vecs[:, b2_c, k:k + 1], scale=vecs[:, g2_c, k:k + 1]).then_inc(tT_done, 1)
                if within(t5, TILES):
                    norm_apply(2, z[:, t5[1], :], xf[:, t5[1], :], t5, z_done)
                    act_e.wait_ge(uT_ps, number(t5) + 1)
                    for k in range(KD):
                        nc.scalar.activation(uT[:, t5[1], k, :], bank[5][:, k * P:(k + 1) * P], ACT.Identity,
                                             bias=vecs[:, b1_c, k:k + 1], scale=vecs[:, g1_c, k:k + 1]).then_inc(uT_done, 1)
                if within(t0, TILES):
                    norm_apply(0, xn[:, t0[1], :], of(x_sb, t0), t0, xn_done)
                if within(t2, TILES):
                    for part, (c0, c1) in enumerate(((0, FULL_HEADS * KEYS), (FULL_HEADS * KEYS, SCORES))):
                        act_e.wait_ge(sub_done, 2 * number(t2) + part + 1)
                        nc.scalar.activation(p_sb[:, t2[1], c0:c1], s_sb[:, t2[1], c0:c1], ACT.Exp, scale=SCALE).then_inc(p_done, 1)

            pipeline(act_e, tiles, TILES, LIST, SCATTER)

            def split(slot, expert):
                for k in range(KD):
                    at, cols = k * 2 * INTER, 2 * INTER
                    nc.scalar.activation(weights(split_w, slot, SPLIT, at, cols),
                                         weights(w_raw, slot, WCOLS, at, cols), ACT.Copy).then_inc(gu_hi[k], 1)

            act_e.wait_ge(acc_out, 16 * TILES)
            act_e.wait_ge(raw_ready, 1)
            nc.scalar.activation(weights(split_w, 0, SPLIT, GU_COLS, WCOLS - GU_COLS),
                                 weights(w_raw, 0, WCOLS, GU_COLS, WCOLS - GU_COLS), ACT.Copy).then_inc(dn_hi, 1)
            split(0, 1)

            def experts_(it, only=None):
                a, b, c = back(it, 0), back(it, 1), back(it, 2)
                has = member(only)
                if has(c):
                    with act_e.If(entry(act_e, first_tab, c, 0, 1)):
                        next_expert(act_e, c, split)
                if has(b):
                    act_e.wait_ge(g_ps, 2 * number(b) + 1)
                    wait_count(act_e, act_done, 2 * number(b) - 1)
                    nc.scalar.activation(silu[:, 0, :], bank[0], ACT.Silu).then_inc(silu_done, 1)
                if has(c):
                    for half in range(2):
                        act_e.wait_ge(aT_ps, 2 * number(c) + half + 1)
                        nc.scalar.activation(aT_hi[:, c.par, 4 * half:4 * half + 4, :], bank[4 + half], ACT.Copy).then_inc(aTh_done, 1)
                if has(b):
                    act_e.wait_ge(g_ps, 2 * number(b) + 2)
                    wait_count(act_e, act_done, 2 * number(b))
                    nc.scalar.activation(silu[:, 1, :], bank[2], ACT.Silu).then_inc(silu_done, 1)
                if has(a):
                    act_e.wait_ge(tb_ps, number(a) + 1)
                    wait_count(act_e, tbl_done, number(a) - 1)
                    for k in range(KD):
                        nc.scalar.activation(tbT[:, a.par, k, :], bank[6][:, k * P:(k + 1) * P], ACT.Identity,
                                             bias=vecs[:, b2_c, k:k + 1], scale=vecs[:, g2_c, k:k + 1]).then_inc(tb_done, 1)

            pipeline(act_e, experts_, USUAL_BLOCKS, 2, 4, GATHERS)
            blocks_behind(act_e, experts_, 2)

        @block.vector
        def _(dve):
            dve.wait_ge(iota_done, 6)
            nc.vector.tensor_scalar(fill[:, :, 0], fill[:, :, 0], P - 1, TOKENS, ALU.bitwise_and, ALU.bitwise_or).then_inc(fill_done, 1)
            dve.wait_ge(ctxT_ps, 1)
            nc.vector.tensor_copy(ctxT[:, :, :, :], bank[0][:, 0:KD * BATCH * KEYS]).then_inc(ctxT_done, 1)

            def norm_stats(norm, src, t):
                nc.vector.bn_stats(stats[:, t[1], :], src).then_inc(st[norm], 1)

            def norm_moments(norm, t):
                wait_apart(dve, st[norm], number(t) + 1, dve_met)
                nc.vector.bn_aggr(mv[norm][:, t[1], :], stats[:, t[1], :]).then_inc(var[norm], 1)

            def norm_shift(norm, t):
                par = t[1]
                dve.wait_ge(rs[norm], number(t) + 1)
                nc.vector.tensor_scalar(shift[norm][:, par:par + 1], mv[norm][:, par, 0:1], rstd[norm][:, par:par + 1], -1.0,
                                        ALU.mult, ALU.mult).then_inc(sh[norm], 1)

            def norm_apply(norm, dst, src, t, done):
                dve.wait_ge(rs[norm], number(t) + 1)
                nc.vector.tensor_scalar(dst, src, mv[norm][:, t[1], 0:1], rstd[norm][:, t[1]:t[1] + 1],
                                        ALU.subtract, ALU.mult).then_inc(done, 1)

            def tiles(it):
                t0, t2, t4, t5, t6, t7 = (back(it, lag) for lag in (LN1, QK, PROJ, LN2, MIX, LIST))
                if within(t0, TILES):
                    if isinstance(number(t0), int):
                        dve.wait_ge(x_in[number(t0) // 4], 32)
                        if number(t0) == SCATTER:
                            dve.wait_ge(x_in[3], 32)
                    norm_stats(0, of(x_sb, t0), t0)
                if within(t5, TILES):
                    if isinstance(number(t5), int) and number(t5) == 0:
                        dve.wait_ge(xb_done, 4)
                    dve.wait_ge(wo_ps, number(t5) + 1)
                    nc.vector.tensor_tensor(of(x1_sb, t5), bank[7][:, 0:D], of(x1_sb, t5), ALU.add).then_inc(x1_done, 1)
                if within(t0, TILES):
                    norm_moments(0, t0)
                if within(t5, TILES):
                    wait_apart(dve, x1_done, number(t5) + 1, dve_met)
                    norm_stats(1, of(x1_sb, t5), t5)
                    norm_moments(1, t5)
                if within(t0, TILES):
                    norm_shift(0, t0)
                if within(t6, TILES):
                    dve.wait_ge(aw_ps, number(t6) + 1)
                    wait_count(dve, acc_done, number(t6) - 1)
                    nc.vector.tensor_tensor(h[:, t6[1], :], bank[5][:, 0:D], xf[:, t6[1], :], ALU.add).then_inc(h_done, 1)
                    dve.wait_ge(h_done, number(t6) + 1)
                    norm_stats(3, h[:, t6[1], :], t6)
                    norm_moments(3, t6)
                if within(t4, TILES):
                    par = t4[1]
                    dve.wait_ge(o_ps, number(t4) + 1)
                    o3 = bank[3][:, 0:HEADS * VW].rearrange("p (h v) -> p h v", h=HEADS)
                    nc.vector.reciprocal(o_rec[:, par, :], o3[:, :, HD]).then_inc(orec_done, 1)
                if within(t5, TILES):
                    norm_apply(1, xf[:, t5[1], :], of(x1_sb, t5), t5, xf_done)
                if within(t4, TILES):
                    dve.wait_ge(orec_done, number(t4) + 1)
                    nc.vector.tensor_tensor(o_sb[:, t4[1], :].rearrange("p (h d) -> p h d", h=HEADS), o3[:, :, 0:HD],
                                            o_rec[:, t4[1], :].unsqueeze(2).to_broadcast([P, HEADS, HD]), ALU.mult).then_inc(o_done, 1)
                if within(t5, TILES):
                    dve.wait_ge(xf_done, number(t5) + 1)
                    norm_stats(2, xf[:, t5[1], :], t5)
                if within(t7, TILES):
                    par, n = t7[1], number(t7) + 1
                    logits = bank[3][:, LOGITS_AT:LOGITS_AT + EXPERTS]
                    wait_apart(dve, lg_ps, n, dve_met)
                    nc.vector.max(top[:, par, :], logits).then_inc(top_done, 1)
                if within(t5, TILES):
                    norm_moments(2, t5)
                if within(t7, TILES):
                    wait_apart(dve, top_done, n, dve_met)
                    nc.vector.max_index(top_i[:, par, :], top[:, par, :], logits).then_inc(topi_done, 1)
                    nc.vector.tensor_tensor(gap[:, par, :], top[:, par, 1:2], top[:, par, 0:1], ALU.subtract).then_inc(gap_done, 1)
                if within(t6, TILES):
                    wait_count(dve, z2_out[t6[1]], 16 * t6[0])
                    norm_apply(3, z2[:, t6[1], :], h[:, t6[1], :], t6, z2_done)
                if within(t7, TILES):
                    dve.wait_ge(topi_done, n)
                    nc.vector.tensor_copy(top_f[:, par, :], top_i[:, par, 0:TOPK]).then_inc(topf_done, 1)
                    dve.wait_ge(topf_done, n)
                    nc.vector.tensor_tensor(hot[:, par, :, :], expert_f[:, :].unsqueeze(1).to_broadcast([P, TOPK, EXPERTS]),
                                            top_f[:, par, :].unsqueeze(2).to_broadcast([P, TOPK, EXPERTS]), ALU.is_equal).then_inc(hot_done, 1)
                    dve.wait_ge(hot_done, n)
                    nc.vector.tensor_tensor(chosen[:, par, :], hot[:, par, 0, :], hot[:, par, 1, :], ALU.add).then_inc(chosen_done, 1)
                if within(t5, TILES):
                    norm_shift(2, t5)
                if within(t7, TILES):
                    dve.wait_ge(chosen_done, n)
                    nc.vector.tensor_tensor(before[:, 1 - par, :], before[:, par, :], chosen[:, par, :], ALU.add).then_inc(before_done, 1)

                def scores_out(part):
                    s3 = s_sb[:, t2[1], :].rearrange("p (h k) -> p h k", h=HEADS)
                    if part == 0:
                        nc.vector.tensor_tensor(
                            s3[:, 0:FULL_HEADS, :].rearrange("p (g s) k -> p g s k", g=FULL_BANKS),
                            psum[:, 0:FULL_BANKS, 0:BANK_HEADS * KEYS].rearrange("p g (s k) -> p g s k", s=BANK_HEADS),
                            of(ceil_f, t2).unsqueeze(1).unsqueeze(1).to_broadcast([P, FULL_BANKS, BANK_HEADS, KEYS]), ALU.min).then_inc(s_done, 1)
                    else:
                        rest = HEADS - FULL_HEADS
                        nc.vector.tensor_tensor(
                            s3[:, FULL_HEADS:HEADS, :], psum[:, FULL_BANKS, 0:rest * KEYS].rearrange("p (s k) -> p s k", s=rest),
                            of(ceil_f, t2).unsqueeze(1).to_broadcast([P, rest, KEYS]), ALU.min).then_inc(s_done, 1)

                def maxima(part):
                    h0, h1 = ((0, FULL_HEADS), (FULL_HEADS, HEADS))[part]
                    s3 = s_sb[:, t2[1], :].rearrange("p (h k) -> p h k", h=HEADS)
                    dve.wait_ge(s_done, 2 * number(t2) + part + 1)
                    nc.vector.reduce_max(s_max[:, t2[1], h0:h1], s3[:, h0:h1, :], AX_X).then_inc(max_done, 1)

                if within(t2, TILES):
                    dve.wait_ge(s_ps, 2 * number(t2) + 1)
                    wait_count(dve, p_done, 2 * number(t2) - 2)
                    scores_out(0)
                if within(t2, TILES):
                    maxima(0)
                if within(t2, TILES):
                    dve.wait_ge(s_ps, 2 * number(t2) + 2)
                    if within(t7, TILES):
                        dve.wait_ge(rank_ps, n)
                    scores_out(1)
                if within(t7, TILES):
                    par = t7[1]
                    dve.wait_ge(rank_ps, n)
                    nc.vector.tensor_tensor(place[:, par, :], bank[FULL_BANKS][:, RANKS_AT:RANKS_AT + EXPERTS], list_base[:, :], ALU.add).then_inc(place_done, 1)
                    dve.wait_ge(e2_done, n)
                    nc.vector.tensor_scalar(e_sum[:, par, :], e2[:, par, :], 1.0, None, ALU.add).then_inc(esum_done, 1)
                if within(t2, TILES):
                    maxima(1)
                if within(t7, TILES):
                    dve.wait_ge(place_done, n)
                    nc.vector.tensor_tensor(picked[:, par, :, :], hot[:, par, :, :],
                                            place[:, par, :].unsqueeze(1).to_broadcast([P, TOPK, EXPERTS]), ALU.mult).then_inc(picked_done, 1)
                    wait_count(dve, listed[par], 16 * TOPK * t7[0])
                    weight = pair[:, par, :, :].bitcast(F32)
                    dve.wait_ge(esum_done, n)
                    nc.vector.reciprocal(weight[:, 0, 1:2], e_sum[:, par, :]).then_inc(w1_done, 1)
                    dve.wait_ge(picked_done, n)
                    with nc.allow_low_precision(reason="one of eight is not 0: a whole number under 2^24"):
                        nc.vector.tensor_reduce(pos[:, par, :], picked[:, par, :, :], AX_X, ALU.add)
                    nc.vector.tensor_copy(pair[:, par, :, 0], of(tokens, t7))
                    dve.wait_ge(w1_done, n)
                    nc.vector.tensor_tensor(weight[:, 1, 1:2], weight[:, 0, 1:2], e2[:, par, :], ALU.mult).then_inc(pair_done, 1)

            for i in range(QK):
                tiles(Step(0, i, 2))

            dve.wait_ge(small_in, 16 * SMALL)
            dve.wait_ge(consts, CONSTS)
            dve.wait_ge(v_ps, 1)
            for b in range(BATCH):
                nc.vector.tensor_tensor(v_heads[0:KEYS, :, b, 0:HD],
                                        bank[2 + b][0:KEYS, 0:D].rearrange("p (h d) -> p h d", h=HEADS),
                                        bv_sb[0:KEYS, :].rearrange("p (h d) -> p h d", h=HEADS), ALU.add).then_inc(v_done, 1)
            nc.vector.tensor_copy(row_f[:, :], row_i[:, :]).then_inc(head_step, 1)
            dve.wait_ge(head_step, 1)
            nc.vector.tensor_scalar(head_of[:, :], row_f[:, :], float(HD), None, ALU.is_lt).then_inc(head_step, 1)
            nc.vector.tensor_scalar(row_f[:, :], row_f[:, :], 0.0, None, ALU.is_ge).then_inc(head_step, 1)
            dve.wait_ge(head_step, 3)
            nc.vector.tensor_tensor(head_of[:, :], head_of[:, :], row_f[:, :], ALU.mult).then_inc(head_step, 1)
            dve.wait_ge(head_step, 4)
            dve.wait_ge(k_ps, 1)
            for m in range(KD):
                for q in range(HALF_HEADS):
                    nc.vector.tensor_scalar(k_diag[:, :, m, q, :],
                                            bank[1][:, m * BATCH * KEYS:(m + 1) * BATCH * KEYS].rearrange("p (b k) -> p b k", b=BATCH),
                                            vecs[:, bk_c, m:m + 1], head_of[:, q:q + 1], ALU.add, ALU.mult).then_inc(k_done, 1)
            dve.wait_ge(mask_in, 32)
            nc.vector.tensor_scalar(ceil_f[:, :, :], mask_i, 0.0, 3e38, ALU.not_equal, ALU.mult).then_inc(ceil_step, 1)
            dve.wait_ge(ceil_step, 1)
            nc.vector.tensor_scalar(ceil_f[:, :, :], ceil_f[:, :, :], NEG / SCALE, None, ALU.add).then_inc(ceil_step, 1)
            dve.wait_ge(ceil_step, 2)
            nc.vector.tensor_copy(expert_f[:, :], expert_i[:, :]).then_inc(router_const, 1)
            nc.vector.tensor_copy(steps[:, :], steps_i[:, :]).then_inc(router_const, 1)
            dve.wait_ge(router_const, 2)
            nc.vector.tensor_scalar(list_base[:, :], expert_f[:, :], float(TOKENS), None, ALU.mult).then_inc(router_const, 1)

            dve.wait_ge(v_in, 32)
            for c0, c1, rows_ in ((0, CHUNKS - 1, P), (CHUNKS - 1, CHUNKS, SCORES - (CHUNKS - 1) * P)):
                shape = [rows_, c1 - c0, CHUNK_SLOTS, VW]
                for b in range(BATCH):
                    nc.vector.tensor_tensor(v_chunks[0:rows_, c0:c1, b, :, :],
                                            v_flat[0:rows_, c0:c1, b, :].unsqueeze(2).to_broadcast(shape),
                                            slots[0:rows_, c0:c1, :].unsqueeze(3).to_broadcast(shape), ALU.mult).then_inc(v_split, 1)

            pipeline(dve, tiles, TILES, LIST, SCATTER + 2, begin=QK)

            steps_done = [0]

            def step(instruction):
                steps_done[0] += 1
                instruction.then_inc(tab, 1)
                dve.wait_ge(tab, steps_done[0])

            dve.wait_ge(cnt_ps, 1)
            step(nc.vector.tensor_copy(cnt[:, :], bank[0][0:1, 0:EXPERTS]))
            step(nc.vector.tensor_scalar(over[0:1, 0, :], steps[0:1, 0:TILES], float(P), None, ALU.mult))
            step(nc.vector.tensor_tensor(passed_n[0:1, 0:TILES, :], cnt[:, :].unsqueeze(1).to_broadcast([1, TILES, EXPERTS]),
                                         over[0:1, 0, :].unsqueeze(2).to_broadcast([1, TILES, EXPERTS]), ALU.is_gt))
            step(nc.vector.tensor_reduce(nblk[:, :], passed_n[0:1, 0:TILES, :].rearrange("o t e -> o e t"), AX_X, ALU.add))
            step(nc.vector.tensor_scalar(nblk[:, :], nblk[:, :], 1.0, None, ALU.max))
            step(nc.vector.tensor_tensor(cum_t[:, :, :], upto[:, :, :], nblk[:, :].unsqueeze(1).to_broadcast([1, EXPERTS, EXPERTS]), ALU.mult))
            step(nc.vector.tensor_reduce(cum[:, :], cum_t[:, :, :], AX_X, ALU.add))
            step(nc.vector.tensor_tensor(passed[:, :, :], steps[:, :].unsqueeze(2).to_broadcast([1, J, EXPERTS]),
                                         cum[:, :].unsqueeze(1).to_broadcast([1, J, EXPERTS]), ALU.is_ge))
            step(nc.vector.tensor_tensor(passed_n[:, :, :], passed[:, :, :], nblk[:, :].unsqueeze(1).to_broadcast([1, J, EXPERTS]), ALU.mult))
            step(nc.vector.tensor_reduce(e_of[:, :], passed[:, :, :], AX_X, ALU.add))
            step(nc.vector.tensor_reduce(b_of[:, :], passed_n[:, :, :], AX_X, ALU.add))
            step(nc.vector.scalar_tensor_tensor(r_of[:, :], e_of[:, :], float(TOKENS // P), steps[:, :], ALU.mult, ALU.add))
            step(nc.vector.tensor_tensor(r_of[:, :], r_of[:, :], b_of[:, :], ALU.subtract))
            step(nc.vector.tensor_scalar(row_tab[:, :], r_of[:, :], float(P), None, ALU.mult))
            step(nc.vector.tensor_scalar(e_of[:, :], e_of[:, :], float(EXPERTS - 1), None, ALU.min))
            step(nc.vector.tensor_scalar(wait_tab[:, :], e_of[:, :], 1.0, float(PARTS), ALU.add, ALU.mult))
            step(nc.vector.tensor_scalar(next_tab[:, :], e_of[:, :], 2.0, None, ALU.add))
            step(nc.vector.tensor_tensor(first[:, :], b_of[:, :], steps[:, :], ALU.is_equal))
            step(nc.vector.scalar_tensor_tensor(first_tab[:, :], e_of[:, :], float(EXPERTS - 1), first[:, :], ALU.is_lt, ALU.mult))
            step(nc.vector.memset(rush_tab[:, :], 0))
            step(nc.vector.tensor_tensor(rush_tab[:, 0:BLOCKS], first_tab[:, 0:BLOCKS], first[:, 1:J], ALU.mult))
            step(nc.vector.tensor_scalar(present_tab[:, :], steps[:, :], cum[:, EXPERTS - 1:EXPERTS], None, ALU.is_lt))
            step(nc.vector.tensor_scalar(added_tab[:, :], cum[:, EXPERTS - 1:EXPERTS], float(USUAL_BLOCKS), 16.0, ALU.max, ALU.mult))
            step(nc.vector.tensor_copy(parity_tab[:, :], e_of[:, :]))
            step(nc.vector.tensor_scalar(slot_tab[:, :], next_tab[:, :], 1, 1, ALU.bitwise_and, ALU.bitwise_xor))
            nc.vector.tensor_scalar(parity_tab[:, :], parity_tab[:, :], 1, None, ALU.bitwise_and).then_inc(tab_done, 1)

            def leftovers(slot, expert, halves):
                for k in halves:
                    at, cols = k * 2 * INTER, 2 * INTER
                    dve.wait_ge(gu_hi[k], expert)
                    nc.vector.tensor_tensor(weights(split_w, slot, SPLIT, WCOLS + at, cols),
                                            weights(w_raw, slot, WCOLS, at, cols),
                                            weights(split_w, slot, SPLIT, at, cols).bitcast(F32), ALU.subtract).then_inc(w_ready, 1)

            def split(slot, expert):
                nc.vector.tensor_copy(weights(split_w, slot, SPLIT, GU_COLS, WCOLS - GU_COLS),
                                      weights(w_raw, slot, WCOLS, GU_COLS, WCOLS - GU_COLS)).then_inc(dn_hi, 1)
                leftovers(slot, expert, (0,))

            leftovers(0, 1, range(KD))

            def experts_(it, only=None):
                a, b, c, d = (back(it, lag) for lag in range(4))
                has = member(only)

                def weighted():
                    if has(d):
                        dve.wait_ge(y_ps, number(d) + 1)
                        wait_count(dve, added, 16 * (number(d) - 1))
                        nc.vector.tensor_scalar(y[:, d.par, :], bank[7][:, 0:D], blk[:, number(d), 1:2].bitcast(F32), None, ALU.mult).then_inc(y_done, 1)

                if has(c):
                    first_c, rush, expert, slot = (entry(dve, *column) for column in (
                        (first_tab, c, 0, 1), (rush_tab, c, 0, 1), (next_tab, c, 1, EXPERTS + 1), (slot_tab, c, 0, 1)))
                weighted()
                if has(c):
                    with dve.If(first_c):
                        next_expert(dve, c, split, expert, slot)
                    with dve.If(rush):
                        leftovers(slot, expert, (1,))
                    for half in range(2):
                        dve.wait_ge(aTh_done, 2 * number(c) + half + 1)
                        nc.vector.tensor_tensor(aT_lo[:, c.par, 4 * half:4 * half + 4, :], bank[4 + half].rearrange("p (i t) -> p i t", i=4),
                                                aT_hi[:, c.par, 4 * half:4 * half + 4, :].bitcast(F32), ALU.subtract).then_inc(aTl_done, 1)
                if has(b):
                    for half in range(2):
                        dve.wait_ge(silu_done, 2 * number(b) + half + 1)
                        dve.wait_ge(u_ps, 2 * number(b) + half + 1)
                        nc.vector.tensor_tensor(act[:, b.par, half * 512:half * 512 + 512], bank[1 + 2 * half], silu[:, half, :], ALU.mult).then_inc(act_done, 1)
                if has(a):
                    n = number(a)
                    dve.wait_ge(tb_done, KD * n + KD)
                    nc.vector.tensor_copy(tb_hi[:, a.par, :, :], tbT[:, a.par, :, :]).then_inc(tbh_done, 1)
                    dve.wait_ge(tbh_done, n + 1)
                    nc.vector.tensor_tensor(tb_lo[:, a.par, :, :], tbT[:, a.par, :, :], tb_hi[:, a.par, :, :].bitcast(F32), ALU.subtract).then_inc(tbl_done, 1)

                if has(c):
                    with dve.If(first_c - rush):
                        leftovers(slot, expert, (1,))

            pipeline(dve, experts_, USUAL_BLOCKS, 3, 4, GATHERS)
            blocks_behind(dve, experts_, 3)

        @block.tensor
        def _(pe):
            pe.wait_ge(consts, CONSTS)
            pe.wait_ge(ctx_in, 16)
            for k in range(KD):
                for b in range(BATCH):
                    at = (k * BATCH + b) * KEYS
                    last = nc.tensor.transpose(bank[0][:, at:at + KEYS], ctx_sb[0:KEYS, b, k * P:(k + 1) * P], ident[0:KEYS, 0:KEYS])
            last.then_inc(ctxT_ps, 1)
            pe.wait_ge(wkv_in, 32)
            pe.wait_ge(ctxT_done, 1)
            for b in range(BATCH):
                for k in range(KD):
                    last = nc.tensor.matmul(bank[2 + b][0:KEYS, 0:D], ctxT[:, k, b, :], wv_sb[:, k, :], start=k == 0, stop=k == KD - 1)
            last.then_inc(v_ps, 1)
            for m in range(2):
                for k in range(KD):
                    last = nc.tensor.matmul(bank[1][:, m * BATCH * KEYS:(m + 1) * BATCH * KEYS], wk_sb[:, k, m * P:(m + 1) * P],
                                            ctxT[:, k, :, :].rearrange("p b k -> p (b k)"), start=k == 0, stop=k == KD - 1)
            last.then_inc(k_ps, 1)
            pe.wait_ge(wqo_in, 32)
            pe.wait_ge(aw_in, 32)

            def tiles(it):
                t1, t2, t3, t4, t5, t6, t7 = (back(it, lag) for lag in (XT, QK, PV, PROJ, LN2, MIX, LIST))

                def transposed(dst, src):
                    for k in range(KD):
                        done = nc.tensor.transpose(dst[:, k * P:(k + 1) * P], src[:, k * P:(k + 1) * P], ident[:, :])
                    return done

                def row_product(dst, rows_T, w):
                    for k in range(KD):
                        done = nc.tensor.matmul(dst, rows_T[:, k, :], w[:, k, :], start=k == 0, stop=k == KD - 1)
                    return done

                def weights_T(r):
                    for c in range(4 * r, min(4 * r + 4, CHUNKS)):
                        w = min(P, SCORES - c * P)
                        done = nc.tensor.transpose(bank[4 + r % 2][0:w, (c - 4 * r) * P:(c - 4 * r + 1) * P],
                                                   p_sb[:, t3[1], c * P:c * P + w], ident[:, :])
                    return done

                def weighted_values(c0, c1):
                    for c in range(c0, c1):
                        w = min(P, SCORES - c * P)
                        first, heads = chunk_heads(c)
                        done = nc.tensor.matmul(bank[3][:, first * VW:(first + heads) * VW], pT[0:w, t3[1], c, :],
                                                v_chunks[0:w, c, t3[1], 0:heads, :].rearrange("p s v -> p (s v)"),
                                                start=c == 0, stop=c == CHUNKS - 1, skip_group_check=True)
                    return done

                if within(t2, TILES):
                    pe.wait_ge(xnT_done, number(t2) + 1)
                    for m in range(KD):
                        for k in range(KD):
                            last = nc.tensor.matmul(bank[6][:, m * P:(m + 1) * P], wq_sb[:, k, m * P:(m + 1) * P],
                                                    xnT[:, t2[1], k, :], start=k == 0, stop=k == KD - 1)
                    last.then_inc(q_ps, 1)
                if within(t3, TILES):
                    pe.wait_ge(p_done, 2 * number(t3) + 2)
                    wait_count(pe, pT_done, PT_ROUNDS * number(t3))
                    weights_T(0).then_inc(pT_ps, 1)
                    if within(t6, TILES):
                        pe.wait_ge(h_done, number(t6) + 1)
                    weights_T(1).then_inc(pT_ps, 1)
                if within(t2, TILES):
                    n, par = number(t2), t2[1]
                    if isinstance(n, int) and n == 0:
                        pe.wait_ge(k_done, HEADS)
                        pe.wait_ge(ceil_step, 2)
                    pe.wait_ge(q_done, KD * (n + 1))
                    wait_count(pe, s_done, 2 * n)
                    if within(t7, TILES):
                        wait_count(pe, place_done, number(t7))
                    for g in range(-(-HEADS // BANK_HEADS)):
                        for m in range(KD):
                            h0 = max(g * BANK_HEADS, m * HALF_HEADS)
                            h1 = min((g + 1) * BANK_HEADS, (m + 1) * HALF_HEADS, HEADS)
                            if h0 < h1:
                                last = nc.tensor.matmul(
                                    bank[g][:, (h0 - g * BANK_HEADS) * KEYS:(h1 - g * BANK_HEADS) * KEYS], qT[:, par, m, :],
                                    k_diag[:, par, m, h0 - m * HALF_HEADS:h1 - m * HALF_HEADS, :].rearrange("p q k -> p (q k)"),
                                    start=True, stop=True)
                        if g >= FULL_BANKS - 1:
                            last.then_inc(s_ps, 1)
                if within(t4, TILES):
                    pe.wait_ge(o_done, number(t4) + 1)
                    wait_count(pe, x1_done, number(t4))
                    transposed(bank[7], o_sb[:, t4[1], :]).then_inc(oT_ps, 1)
                if within(t7, TILES):
                    par = t7[1]
                    pe.wait_ge(chosen_done, number(t7) + 1)
                    ranks = bank[FULL_BANKS][:, RANKS_AT:RANKS_AT + EXPERTS]
                    if not within(t2, TILES):
                        wait_count(pe, place_done, number(t7))
                        pe.wait_ge(s_done, 2 * TILES)
                    nc.tensor.matmul(ranks, below[:, :], chosen[:, par, :], start=True, stop=False)
                    nc.tensor.matmul(ranks, ones[:, :], before[:, par, :], start=False, stop=True).then_inc(rank_ps, 1)
                if within(t1, TILES):
                    pe.wait_ge(xn_done, number(t1) + 1)
                    transposed(bank[6], xn[:, t1[1], :]).then_inc(xnT_ps, 1)
                if within(t3, TILES):
                    pe.wait_ge(pT_done, PT_ROUNDS * number(t3) + 1)
                    weights_T(2).then_inc(pT_ps, 1)
                if within(t6, TILES):
                    pe.wait_ge(z2_done, number(t6) + 1)
                    if within(t7, TILES):
                        pe.wait_ge(topi_done, number(t7) + 1)
                    transposed(bank[3], z2[:, t6[1], :]).then_inc(tT_ps, 1)
                if within(t4, TILES):
                    pe.wait_ge(oT_done, number(t4) + 1)
                    row_product(bank[7][:, 0:D], oT[:, t4[1], :, :], wo_sb).then_inc(wo_ps, 1)
                if within(t5, TILES):
                    pe.wait_ge(z_done, number(t5) + 1)
                    wait_count(pe, h_done, number(t5))
                    if within(t3, TILES):
                        pe.wait_ge(pT_done, PT_ROUNDS * number(t3) + 2)
                    transposed(bank[5], z[:, t5[1], :]).then_inc(uT_ps, 1)
                if within(t6, TILES):
                    pe.wait_ge(tT_done, KD * (number(t6) + 1))
                    row_product(bank[3][:, LOGITS_AT:LOGITS_AT + EXPERTS], tT[:, t6[1], :, :], gw_sb).then_inc(lg_ps, 1)
                if within(t3, TILES):
                    n, par = number(t3), t3[1]
                    if isinstance(n, int) and n == 0:
                        pe.wait_ge(v_split, 2 * BATCH)
                    pe.wait_ge(pT_done, PT_ROUNDS * (n + 1))
                    weighted_values(0, CHUNKS // 2)
                if within(t5, TILES):
                    pe.wait_ge(uT_done, KD * (number(t5) + 1))
                    row_product(bank[5][:, 0:D], uT[:, t5[1], :, :], aw_sb).then_inc(aw_ps, 1)
                if within(t3, TILES):
                    weighted_values(CHUNKS // 2, CHUNKS).then_inc(o_ps, 1)

            pipeline(pe, tiles, TILES, LIST, SCATTER)

            pe.wait_ge(s_done, 2 * TILES)
            pe.wait_ge(before_done, TILES)
            nc.tensor.matmul(bank[0][:, 0:EXPERTS], ones[:, :], before[:, 0, :], start=True, stop=True).then_inc(cnt_ps, 1)
            pe.wait_ge(place_done, TILES)
            pe.wait_ge(tab_done, 1)

            def three_products(dst, hi, lo, parity, at, cols, first, last):
                w_hi = weights(split_w, parity, SPLIT, at, cols)
                w_lo = weights(split_w, parity, SPLIT, WCOLS + at, cols)
                nc.tensor.matmul(dst, hi, w_hi, start=first, stop=False)
                nc.tensor.matmul(dst, hi, w_lo, start=False, stop=False)
                return nc.tensor.matmul(dst, lo, w_hi, start=False, stop=last)

            def gate_up(half, b, parity):
                par, n = b.par, number(b)
                for which, sem_ in ((0, g_ps), (1, u_ps)):
                    wait_count(pe, silu_done if which == 0 else act_done, 2 * n - 1 + half)
                    for k in range(KD):
                        last = three_products(bank[2 * half + which], tb_hi[:, par, k, :], tb_lo[:, par, k, :], parity,
                                              (2 * k + which) * INTER + half * 512, 512, k == 0, k == KD - 1)
                    last.then_inc(sem_, 1)

            def experts_(it, only=None):
                a, b, c = back(it, 0), back(it, 1), back(it, 2)
                has = member(only)
                if has(b):
                    ready = pe.value_load(wait_tab[0:1, bass.ds(number(b), 1)], min_val=1, max_val=PARTS * EXPERTS)
                    parity = pe.value_load(parity_tab[0:1, bass.ds(number(b), 1)], min_val=0, max_val=1)
                    pe.wait_ge(w_ready, ready)
                    pe.wait_ge(tbl_done, number(b) + 1)
                    gate_up(0, b, parity)
                if has(c):
                    par, n = c.par, number(c)
                    for half in range(2):
                        pe.wait_ge(act_done, 2 * n + half + 1)
                        wait_count(pe, aTl_done, 2 * n - 1 + half)
                        for i in range(4):
                            at = half * 512 + i * P
                            last = nc.tensor.transpose(bank[4 + half][:, i * P:(i + 1) * P], act[:, par, at:at + P], ident[:, :])
                        last.then_inc(aT_ps, 1)
                if has(b):
                    parity = pe.value_load(parity_tab[0:1, bass.ds(number(b), 1)], min_val=0, max_val=1)
                    gate_up(1, b, parity)
                if has(a):
                    pe.wait_ge(zg_in[a[1]], 16 * (a[0] + 1))
                    wait_count(pe, tb_done, 2 * number(a))
                    for k in range(KD):
                        last = nc.tensor.transpose(bank[6][:, k * P:(k + 1) * P], zg[:, a[1], k * P:(k + 1) * P], ident[:, :])
                    last.then_inc(tb_ps, 1)
                if has(c):
                    parity_c = pe.value_load(parity_tab[0:1, bass.ds(number(c), 1)], min_val=0, max_val=1)
                    wait_count(pe, y_done, n)
                    for i in range(IC):
                        if i % 4 == 0:
                            pe.wait_ge(aTl_done, 2 * n + i // 4 + 1)
                        last = three_products(bank[7][:, 0:D], aT_hi[:, par, i, :], aT_lo[:, par, i, :], parity_c,
                                              GU_COLS + i * D, D, i == 0, i == IC - 1)
                    last.then_inc(y_ps, 1)

            pipeline(pe, experts_, USUAL_BLOCKS, 2, 4, GATHERS)
            blocks_behind(pe, experts_, 2)


_INS = ["x", "ctx", "mask", "wqT", "wkT", "wvT", "woT", "awT", "gwT", "columns", "bv", "bo", "slot_rows", "experts"]


def kernel(**inputs):
    import numpy as np
    import concourse.bacc as bacc
    from concourse.bass_utils import run_bass_kernel_spmd

    a = {k: np.asarray(v) for k, v in inputs.items()}
    per_column = ["L0_xattn_bq", "L0_xattn_bk", "L0_ffn_ln1_g", "L0_ffn_ln1_b", "L0_ffn_ln2_g", "L0_ffn_ln2_b"]
    gate_up = np.stack([a["L0_ffn_gate_proj"], a["L0_ffn_up_proj"]], axis=1)
    gate_up = gate_up.reshape(EXPERTS, 2, INTER, KD, P).transpose(0, 4, 3, 1, 2).reshape(EXPERTS, P, KD * 2 * INTER)
    down = a["L0_ffn_down_proj"].reshape(EXPERTS, D, IC, P).transpose(0, 3, 2, 1).reshape(EXPERTS, P, IC * D)
    laid = {
        "x": a["x"], "ctx": a["ctx_1024"], "mask": a["mask_BxSxS2_ik0"],
        "wqT": a["L0_xattn_Wq"].T, "wkT": a["L0_xattn_Wk"].T, "wvT": a["L0_xattn_Wv"].T,
        "woT": a["L0_xattn_Wo"].T, "awT": a["L0_ffn_attn_w"].T, "gwT": a["L0_ffn_gate_w"].T,
        "columns": np.stack([a[n].reshape(KD, P).T for n in per_column], axis=1),
        "bv": a["L0_xattn_bv"], "bo": a["L0_xattn_bo"], "slot_rows": slot_rows(),
        "experts": np.concatenate([gate_up, down], axis=2),
    }
    nc = bacc.Bacc("TRN2", target_bir_lowering=False, num_devices=1)
    arrays, args = {}, []
    for name in _INS:
        v = np.ascontiguousarray(laid[name])
        arrays[f"in_{name}"] = v
        args.append(nc.dram_tensor(f"in_{name}", v.shape, mybir.dt.from_np(v.dtype), kind="ExternalInput").ap())
    result = nc.dram_tensor("out_x", (BATCH, SEQ, D), F32, kind="ExternalOutput").ap()
    xattn_moe(nc, *args, result)
    r = run_bass_kernel_spmd(nc, [arrays], core_ids=[0])
    return r.results[0]["out_x"]
```
